# Optimizing a Trainium2 kernel written in Bass

```python
import numpy as np
import jax
import jax.numpy as jnp

def _softmax(x, axis=-1):
    return jax.nn.softmax(x, axis=axis)

def _gelu(x):
    return jax.nn.gelu(x, approximate=True)

def _silu(x):
    return jax.nn.silu(x)

def _sigmoid(x):
    return jax.nn.sigmoid(x)

def _layernorm(x, axis=-1, eps=1e-05):
    m = jnp.mean(x, axis=axis, keepdims=True)
    v = jnp.var(x, axis=axis, keepdims=True)
    return (x - m) / jnp.sqrt(v + eps)

def _scatter_add(tgt, idx, src, axis=0):
    return tgt.at[idx].add(src)

def _segment_sum(src, seg, n):
    return jax.ops.segment_sum(src, seg, n)
kernel_name = 'mk_xattn_ffn_d2_seqx_r4_434f76'

def setup_inputs(seed: int=0):
    np.random.seed(seed)
    _w = jnp.asarray

    def _rec_inputs():
        import jax
        import jax.numpy as jnp
        _rk = jax.random.key(seed)
        x = -0.0005963 + 1.001 * jax.random.normal(jax.random.fold_in(_rk, 1), (1, 2048, 256), jnp.float32)
        _lenS = 2048 - jax.random.randint(jax.random.fold_in(_rk, 7), (1,), 0, max(1, 2048 // 4) + 1, jnp.int32)
        _lenS2 = 1601 - jax.random.randint(jax.random.fold_in(_rk, 8), (1,), 0, max(1, 1601 // 4) + 1, jnp.int32)
        _ctx_1024P = jax.random.normal(jax.random.fold_in(_rk, 11), (1, 16, 256), jnp.float32)
        _ctx_1024c = jax.random.dirichlet(jax.random.fold_in(_rk, 511), 0.3 * jnp.ones((16,), jnp.float32), (1, 1601))
        _ctx_1024t = jnp.einsum('bsk,bkd->bsd', _ctx_1024c, _ctx_1024P)
        _ctx_1024t = _ctx_1024t * jax.lax.rsqrt(jnp.mean(jnp.square(_ctx_1024t)) + 1e-12) * 0.953939
        ctx_1024 = 4.13588e-05 + 0.999923 * (_ctx_1024t + 0.3 * jax.random.normal(jax.random.fold_in(_rk, 611), (1, 1601, 256), jnp.float32))
        itok_BxS_3_4095 = jax.random.randint(jax.random.fold_in(_rk, 12), (1, 2048), 3, 1024, jnp.int32)
        itok_BxS2_0_4095 = jax.random.randint(jax.random.fold_in(_rk, 13), (1, 1601), 0, 1024, jnp.int32)
        return (x, ctx_1024, itok_BxS_3_4095, itok_BxS2_0_4095)
    x, ctx_1024, itok_BxS_3_4095, itok_BxS2_0_4095 = _rec_inputs()

    def _L0_xattn_setup():
        import jax, jax.numpy as jnp
        import numpy as np
        DIM = 256
        HEADS = 16
        ROPE_BASE = 100.0

        def _rope(x, pos):
            d = x.shape[-1]
            inv_freq = ROPE_BASE ** (-jnp.arange(0, d, 2, dtype=jnp.float32) / d)
            ang = pos.astype(jnp.float32)[:, None, :, None] * inv_freq
            cos, sin = (jnp.cos(ang), jnp.sin(ang))
            x1, x2 = (x[..., 0::2], x[..., 1::2])
            r1 = x1 * cos - x2 * sin
            r2 = x1 * sin + x2 * cos
            return jnp.stack([r1, r2], axis=-1).reshape(x.shape)
        key0 = jax.random.key(seed)
        ks = jax.random.split(key0, 10)
        B, Nq, Nk, C = (4, 192, 512, DIM)
        query = jax.random.normal(ks[0], (B, Nq, C), dtype=jnp.float32)
        key_t = jax.random.normal(ks[1], (B, Nk, C), dtype=jnp.float32)
        value = jax.random.normal(ks[2], (B, Nk, C), dtype=jnp.float32)
        qpos = jax.random.randint(ks[3], (B, Nq), 0, 1024, dtype=jnp.int32)
        kpos = jax.random.randint(ks[4], (B, Nk), 0, 1024, dtype=jnp.int32)
        s = 1.0 / np.sqrt(C)
        Wq = jax.random.normal(ks[5], (C, C), dtype=jnp.float32) * s
        Wk = jax.random.normal(ks[6], (C, C), dtype=jnp.float32) * s
        Wv = jax.random.normal(ks[7], (C, C), dtype=jnp.float32) * s
        Wo = jax.random.normal(ks[8], (C, C), dtype=jnp.float32) * s
        bo = jnp.zeros((C,), dtype=jnp.float32)
        return {'query': query, 'key': key_t, 'value': value, 'qpos': qpos, 'kpos': kpos, 'Wq': Wq, 'Wk': Wk, 'Wv': Wv, 'Wo': Wo, 'bo': bo}
    _L0_xattn_all = _L0_xattn_setup()
    _L0_xattn_in = {k: v for k, v in _L0_xattn_all.items() if k in ('Wq', 'Wk', 'Wv', 'Wo', 'bo')}
    del _L0_xattn_all

    def _L0_ffn_setup():
        import jax, jax.numpy as jnp
        import numpy as np
        D, H, E, K = (256, 256, 8, 2)

        def _moe(x, router_w, w_in, b_in, w_out, b_out):
            B, S, Dm = x.shape
            T = B * S
            x2 = x.reshape(T, Dm)
            logits = x2 @ router_w
            probs = jax.nn.softmax(logits, axis=-1)
            top_p, top_e = jax.lax.top_k(probs, K)
            flat_e = top_e.reshape(-1)
            flat_p = top_p.reshape(-1)
            tok = jnp.repeat(jnp.arange(T), K)
            order = jnp.argsort(flat_e)
            se, sp, st = (flat_e[order], flat_p[order], tok[order])
            xd = x2[st]
            N = xd.shape[0]
            h = jnp.zeros((N, H), x.dtype)
            for e in range(E):
                m = (se == e)[:, None]
                h = h + jnp.where(m, jax.nn.gelu(xd @ w_in[e] + b_in[e]), 0.0)
            y = jnp.zeros((N, Dm), x.dtype)
            for e in range(E):
                m = (se == e)[:, None]
                y = y + jnp.where(m, h @ w_out[e] + b_out[e], 0.0)
            y = y * sp[:, None]
            out = jnp.zeros((T, Dm), x.dtype).at[st].add(y)
            return out.reshape(B, S, Dm)
        key = jax.random.key(seed)
        ks = jax.random.split(key, 5)
        s = lambda k, shape, scale: jax.random.normal(k, shape, dtype=jnp.float32) * scale
        return {'input_batch': s(ks[0], (2, 128, D), 1.0), 'router_w': s(ks[1], (D, E), D ** (-0.5)), 'w_in': s(ks[2], (E, D, H), D ** (-0.5)), 'b_in': jnp.zeros((E, H), jnp.float32), 'w_out': s(ks[3], (E, H, D), H ** (-0.5)), 'b_out': jnp.zeros((E, D), jnp.float32)}
    _L0_ffn_all = _L0_ffn_setup()
    _L0_ffn_in = {k: v for k, v in _L0_ffn_all.items() if k in ('router_w', 'w_in', 'b_in', 'w_out', 'b_out')}
    del _L0_ffn_all

    def _L1_xattn_setup():
        import jax, jax.numpy as jnp
        import numpy as np
        D_MODEL = 256
        N_HEADS = 16
        HEAD_DIM = D_MODEL // N_HEADS
        key = jax.random.key(seed)
        k1, k2, k3, k4, k5, k6 = jax.random.split(key, 6)
        B, T_q, T_kv = (4, 256, 1024)
        s = 1.0 / np.sqrt(D_MODEL)
        return {'query': jax.random.normal(k1, (B, T_q, D_MODEL), dtype=jnp.float32), 'kv_source': jax.random.normal(k2, (B, T_kv, D_MODEL), dtype=jnp.float32), 'w_q': jax.random.normal(k3, (D_MODEL, D_MODEL), dtype=jnp.float32) * s, 'w_k': jax.random.normal(k4, (D_MODEL, D_MODEL), dtype=jnp.float32) * s, 'w_v': jax.random.normal(k5, (D_MODEL, D_MODEL), dtype=jnp.float32) * s, 'w_o': jax.random.normal(k6, (D_MODEL, D_MODEL), dtype=jnp.float32) * s}
    _L1_xattn_all = _L1_xattn_setup()
    _L1_xattn_in = {k: v for k, v in _L1_xattn_all.items() if k in ('w_q', 'w_k', 'w_v', 'w_o')}
    del _L1_xattn_all

    def _L1_ffn_setup():
        import jax, jax.numpy as jnp
        import numpy as np
        B, S, DIM = (2, 512, 256)
        HID = 512
        E, NSH, TOPK = (8, 2, 2)

        def _ffn(x, w1, w2, w3):
            return jax.nn.silu(x @ w1.T) * (x @ w3.T) @ w2.T
        key = jax.random.key(seed)
        ks = jax.random.split(key, 8)
        sc = 0.02
        return {'x': jax.random.normal(ks[0], (B, S, DIM), jnp.float32), 'router_w': jax.random.normal(ks[1], (E, DIM), jnp.float32) * sc, 'expert_bias': jnp.zeros((E,), jnp.float32), 'w1': jax.random.normal(ks[2], (E, HID, DIM), jnp.float32) * sc, 'w3': jax.random.normal(ks[3], (E, HID, DIM), jnp.float32) * sc, 'w2': jax.random.normal(ks[4], (E, DIM, HID), jnp.float32) * sc, 'sw1': jax.random.normal(ks[5], (NSH, HID, DIM), jnp.float32) * sc, 'sw3': jax.random.normal(ks[6], (NSH, HID, DIM), jnp.float32) * sc, 'sw2': jax.random.normal(ks[7], (NSH, DIM, HID), jnp.float32) * sc}
    _L1_ffn_all = _L1_ffn_setup()
    _L1_ffn_in = {k: v for k, v in _L1_ffn_all.items() if k in ('router_w', 'expert_bias', 'w1', 'w3', 'w2', 'sw1', 'sw3', 'sw2')}
    del _L1_ffn_all
    return {'x': x, 'ctx_1024': ctx_1024, 'itok_BxS_3_4095': itok_BxS_3_4095, 'itok_BxS2_0_4095': itok_BxS2_0_4095, 'L0_xattn_Wq': _L0_xattn_in['Wq'], 'L0_xattn_Wk': _L0_xattn_in['Wk'], 'L0_xattn_Wv': _L0_xattn_in['Wv'], 'L0_xattn_Wo': _L0_xattn_in['Wo'], 'L0_xattn_bo': _L0_xattn_in['bo'], 'L0_ffn_router_w': _L0_ffn_in['router_w'], 'L0_ffn_w_in': _L0_ffn_in['w_in'], 'L0_ffn_b_in': _L0_ffn_in['b_in'], 'L0_ffn_w_out': _L0_ffn_in['w_out'], 'L0_ffn_b_out': _L0_ffn_in['b_out'], 'L1_xattn_w_q': _L1_xattn_in['w_q'], 'L1_xattn_w_k': _L1_xattn_in['w_k'], 'L1_xattn_w_v': _L1_xattn_in['w_v'], 'L1_xattn_w_o': _L1_xattn_in['w_o'], 'L1_ffn_router_w': _L1_ffn_in['router_w'], 'L1_ffn_expert_bias': _L1_ffn_in['expert_bias'], 'L1_ffn_w1': _L1_ffn_in['w1'], 'L1_ffn_w3': _L1_ffn_in['w3'], 'L1_ffn_w2': _L1_ffn_in['w2'], 'L1_ffn_sw1': _L1_ffn_in['sw1'], 'L1_ffn_sw3': _L1_ffn_in['sw3'], 'L1_ffn_sw2': _L1_ffn_in['sw2']}

def reference(x, ctx_1024, itok_BxS_3_4095, itok_BxS2_0_4095, L0_xattn_Wq, L0_xattn_Wk, L0_xattn_Wv, L0_xattn_Wo, L0_xattn_bo, L0_ffn_router_w, L0_ffn_w_in, L0_ffn_b_in, L0_ffn_w_out, L0_ffn_b_out, L1_xattn_w_q, L1_xattn_w_k, L1_xattn_w_v, L1_xattn_w_o, L1_ffn_router_w, L1_ffn_expert_bias, L1_ffn_w1, L1_ffn_w3, L1_ffn_w2, L1_ffn_sw1, L1_ffn_sw3, L1_ffn_sw2):
    import jax
    import jax.numpy as jnp

    def _L0_xattn_ref(query, key, value, qpos, kpos, Wq, Wk, Wv, Wo, bo):
        import jax, jax.numpy as jnp
        import numpy as np
        DIM = 256
        HEADS = 16
        ROPE_BASE = 100.0

        def _rope(x, pos):
            d = x.shape[-1]
            inv_freq = ROPE_BASE ** (-jnp.arange(0, d, 2, dtype=jnp.float32) / d)
            ang = pos.astype(jnp.float32)[:, None, :, None] * inv_freq
            cos, sin = (jnp.cos(ang), jnp.sin(ang))
            x1, x2 = (x[..., 0::2], x[..., 1::2])
            r1 = x1 * cos - x2 * sin
            r2 = x1 * sin + x2 * cos
            return jnp.stack([r1, r2], axis=-1).reshape(x.shape)
        B, Nq, C = query.shape
        Nk = key.shape[1]
        h, dh = (HEADS, C // HEADS)
        q = (query @ Wq.T).reshape(B, Nq, h, dh).transpose(0, 2, 1, 3)
        k = (key @ Wk.T).reshape(B, Nk, h, dh).transpose(0, 2, 1, 3)
        v = (value @ Wv.T).reshape(B, Nk, h, dh).transpose(0, 2, 1, 3)
        q = _rope(q, qpos)
        k = _rope(k, kpos)
        scores = jnp.einsum('bhqd,bhkd->bhqk', q, k) / jnp.sqrt(jnp.float32(dh))
        attn = jax.nn.softmax(scores, axis=-1)
        x = jnp.einsum('bhqk,bhkd->bhqd', attn, v)
        x = x.transpose(0, 2, 1, 3).reshape(B, Nq, C)
        return x @ Wo.T + bo

    def _L0_ffn_ref(input_batch, router_w, w_in, b_in, w_out, b_out):
        import jax, jax.numpy as jnp
        import numpy as np
        D, H, E, K = (256, 256, 8, 2)

        def _moe(x, router_w, w_in, b_in, w_out, b_out):
            B, S, Dm = x.shape
            T = B * S
            x2 = x.reshape(T, Dm)
            logits = x2 @ router_w
            probs = jax.nn.softmax(logits, axis=-1)
            top_p, top_e = jax.lax.top_k(probs, K)
            flat_e = top_e.reshape(-1)
            flat_p = top_p.reshape(-1)
            tok = jnp.repeat(jnp.arange(T), K)
            order = jnp.argsort(flat_e)
            se, sp, st = (flat_e[order], flat_p[order], tok[order])
            xd = x2[st]
            N = xd.shape[0]
            h = jnp.zeros((N, H), x.dtype)
            for e in range(E):
                m = (se == e)[:, None]
                h = h + jnp.where(m, jax.nn.gelu(xd @ w_in[e] + b_in[e]), 0.0)
            y = jnp.zeros((N, Dm), x.dtype)
            for e in range(E):
                m = (se == e)[:, None]
                y = y + jnp.where(m, h @ w_out[e] + b_out[e], 0.0)
            y = y * sp[:, None]
            out = jnp.zeros((T, Dm), x.dtype).at[st].add(y)
            return out.reshape(B, S, Dm)
        return _moe(input_batch, router_w, w_in, b_in, w_out, b_out)

    def _L1_xattn_ref(query, kv_source, w_q, w_k, w_v, w_o):
        import jax, jax.numpy as jnp
        import numpy as np
        D_MODEL = 256
        N_HEADS = 16
        HEAD_DIM = D_MODEL // N_HEADS
        B, T_q, _ = query.shape
        T_kv = kv_source.shape[1]
        q = (query @ w_q.T).reshape(B, T_q, N_HEADS, HEAD_DIM)
        k = (kv_source @ w_k.T).reshape(B, T_kv, N_HEADS, HEAD_DIM)
        v = (kv_source @ w_v.T).reshape(B, T_kv, N_HEADS, HEAD_DIM)
        scale = HEAD_DIM ** (-0.5)
        attn = jax.nn.softmax(jnp.einsum('bqhd,bkhd->bhqk', q, k) * scale, axis=-1)
        out = jnp.einsum('bhqk,bkhd->bqhd', attn, v).reshape(B, T_q, D_MODEL)
        return out @ w_o.T

    def _L1_ffn_ref(x, router_w, expert_bias, w1, w3, w2, sw1, sw3, sw2):
        import jax, jax.numpy as jnp
        import numpy as np
        B, S, DIM = (2, 512, 256)
        HID = 512
        E, NSH, TOPK = (8, 2, 2)

        def _ffn(x, w1, w2, w3):
            return jax.nn.silu(x @ w1.T) * (x @ w3.T) @ w2.T
        bs, sl, d = x.shape
        xf = x.reshape(-1, d)
        shared = jnp.zeros_like(xf)
        for i in range(sw1.shape[0]):
            shared = shared + _ffn(xf, sw1[i], sw2[i], sw3[i])
        logits = xf @ router_w.T + expert_bias
        rw, sel = jax.lax.top_k(logits, TOPK)
        rw = jax.nn.softmax(rw.astype(jnp.float32), axis=-1).astype(x.dtype)
        onehot = jax.nn.one_hot(sel, E, dtype=x.dtype)
        combine = jnp.einsum('tk,tke->te', rw, onehot)

        def body(acc, ew):
            e1, e3, e2, cw = ew
            acc = acc + cw[:, None] * _ffn(xf, e1, e2, e3)
            return (acc, None)
        out, _ = jax.lax.scan(body, jnp.zeros_like(xf), (w1, w3, w2, combine.T))
        out = out + shared
        return out.reshape(bs, sl, -1)
    x = x + _L0_xattn_ref(_layernorm(x, axis=-1), ctx_1024, ctx_1024, itok_BxS_3_4095, itok_BxS2_0_4095, L0_xattn_Wq, L0_xattn_Wk, L0_xattn_Wv, L0_xattn_Wo, L0_xattn_bo)
    x = x + _L0_ffn_ref(_layernorm(x, axis=-1), L0_ffn_router_w, L0_ffn_w_in, L0_ffn_b_in, L0_ffn_w_out, L0_ffn_b_out)
    x = x + _L1_xattn_ref(_layernorm(x, axis=-1), ctx_1024, L1_xattn_w_q, L1_xattn_w_k, L1_xattn_w_v, L1_xattn_w_o)
    x = x + _L1_ffn_ref(_layernorm(x, axis=-1), L1_ffn_router_w, L1_ffn_expert_bias, L1_ffn_w1, L1_ffn_w3, L1_ffn_w2, L1_ffn_sw1, L1_ffn_sw3, L1_ffn_sw2)
    return x

_drawn_inputs = setup_inputs


def setup_inputs(seed=0):
    import zlib

    import numpy as np

    out = dict(_drawn_inputs(seed))
    spreads = {'L0_xattn_bo': (0.0, 0.1),
     'L0_ffn_b_in': (0.0, 0.337),
     'L0_ffn_b_out': (0.0, 0.1),
     'L1_ffn_expert_bias': (0.0, 0.8)}
    factors = {'L1_ffn_router_w': 5.12,
     'L1_ffn_w1': 4.351,
     'L1_ffn_w3': 4.311,
     'L1_ffn_w2': 4.297,
     'L1_ffn_sw1': 3.863,
     'L1_ffn_sw3': 3.825,
     'L1_ffn_sw2': 3.841}
    for name, (base, spread) in spreads.items():
        noise = np.random.default_rng([zlib.crc32(name.encode()), seed]).standard_normal(out[name].shape)
        drawn = base * np.exp(spread * noise) if base else spread * noise
        out[name] = jnp.asarray(drawn.astype(out[name].dtype))
    for name, factor in factors.items():
        out[name] = (out[name] * factor).astype(out[name].dtype)
    return out
```

```python
from contextlib import ExitStack

import concourse.bass as bass
import numpy as np
from concourse import mybir

T, D, S, H, DH = 2048, 256, 1601, 16, 16
NT = T // 128
KC = D // 128
NB, QB = 4, 512
NG, HG = 4, 4
NIT = NB * NG
KT = -(-S // 128)
KROWS = [min(128, S - 128 * j) for j in range(KT)]
SC = 401
SP = 4 * SC
MAXCOLS = [(0, 401), (401, 400), (801, 400), (1201, 400)]
PRODUCTS = [(0, 0), (0, 1), (0, 2), (1, 0), (1, 1), (2, 0)]
NSTACK = 16 * len(PRODUCTS)
NPAIR = HG * (QB // 128)
NCH = NPAIR * len(MAXCOLS)
NPOS = T + SP
E0, HC0 = 8, 2
E1, HC1 = 10, 4
NR = 8
EPS = 1e-5
ROUND = 12582912.0
PI_BELOW = 3.1415925
TWO_PI_PARTS = (6.28125, 0.0019350051879882812, 3.0199159819e-07)

C_FREQ, C_SIGN, C_HALFPI, C_EPS = range(4)


def build(nc, dram, out):
    f32, bf16, f32r, i32 = (mybir.dt.float32, mybir.dt.bfloat16, mybir.dt.float32r, mybir.dt.int32)
    ALU, ACT, AX = mybir.AluOpType, mybir.ActivationFunctionType, mybir.AxisListType

    start, limit = -(-nc.sbuf_base // 32) * 32, nc.sbuf_usable_end

    def place(offset, name, shape, dt):
        return nc.alloc_sbuf_tensor_at(name, shape, dt, offset=offset)

    class Region:
        def __init__(self, start):
            self.at = start

        def take(self, name, shape, dt):
            size = int(np.prod(shape[1:])) * (2 if dt == bf16 else 4)
            t = place(self.at, name, shape, dt)
            self.at += -(-size // 32) * 32
            assert self.at <= limit, (name, self.at)
            return t

    keep = Region(start)
    X = keep.take("X", [128, NT, D], f32)
    XN = keep.take("XN", [128, KC, T], f32)
    ident = keep.take("ident", [128, 128], f32)
    spread = keep.take("spread", [128, 128], f32)
    const = keep.take("const", [128, 8], f32)
    stats = keep.take("stats", [128, NT, 6], f32)
    norm = keep.take("norm", [128, 6, NT], f32)
    WO = keep.take("WO", [128, 2, NG, D], f32)
    WQ1 = keep.take("WQ1", [128, KC, D], f32)
    router = keep.take("router", [128, 2, KC, NR], f32)
    rbias = keep.take("rbias", [128, NR], f32)
    PW = keep.take("PW", [128, NT, E1], f32)
    prio = keep.take("prio", [128, NT, NR], f32)
    BRAW = [keep.take(f"BRAW{u}", [128, HC0], f32) for u in range(2)]
    BIN = [keep.take(f"BIN{u}", [128, HC0], f32) for u in range(2)]
    bout0 = keep.take("bout0", [NR, D], f32)
    bo0 = keep.take("bo0", [128, D], f32)
    scrap = keep.take("scrap", [1, 32], f32)
    kregion = keep.at
    KSTK = keep.take("KSTK", [NSTACK + 3, H, S], bf16)
    vregion = keep.at
    V = [keep.take(f"V{l}", [128, NG, KT, HG * DH], f32) for l in range(2)]
    gregion = keep.at
    VG = [keep.take(f"VG{u}", [128, KT, HG, 32], f32) for u in range(2)]
    rregion = keep.at

    r = Region(rregion)
    COS = r.take("COS", [128, NPOS], f32)
    SIN = r.take("SIN", [128, NPOS], f32)
    r = Region(kregion)
    ANG = r.take("ANG", [128, NPOS], f32)
    TURN = r.take("TURN", [128, NPOS], f32)
    POS = place(kregion + -(-4 * NPOS // 32) * 32, "POS", [128, NPOS], i32)
    CTX = r.take("CTX", [128, KC, SP], f32)
    r = Region(rregion + 2 * (-(-4 * NPOS // 32) * 32))
    F = [r.take(f"F{c}", [128, QB], f32) for c in range(2)]
    G = [r.take(f"G{c}", [128, QB], f32) for c in range(2)]
    PARTS = [r.take(f"PARTS{c}", [128, 3, QB], bf16) for c in range(2)]
    W5 = {n: r.take(f"W_{n}", [128, KC, D], f32) for n in ("k0", "k0s", "k1", "q0", "q0s")}
    WV = r.take("WV", [128, KC, 2 * D], f32)
    XC = [place(gregion + 1024 * i, f"XC{i}", [128, D], f32) for i in range(4)]

    r = Region(rregion)
    QST = r.take("QST", [NSTACK + 3, H, QB], bf16)
    PR = [r.take(f"PR{n}", [128, 2, QB], f32) for n in range(4)]
    ON = r.take("ON", [128, NIT, QB], f32)
    U = r.take("U", [128, QB], f32)
    RD = r.take("RD", [128, QB], f32)
    NM = r.take("NM", [NPAIR, 3, 128], bf16)
    NMF = r.take("NMF", [NPAIR, 2, 128], f32)
    ZERO = r.take("ZERO", [NPAIR, 128], f32)
    MXC = r.take("MXC", [128, NPAIR, len(MAXCOLS)], f32)
    M16 = r.take("M16", [128, NPAIR], f32)

    r = Region(rregion)
    XH = r.take("XH", [128, KC, T], f32r)
    XL = r.take("XL", [128, KC, T], f32r)
    moe_at = r.at
    topk = Region(gregion)
    LG = topk.take("LG", [128, NT, NR], f32)
    PB = topk.take("PB", [128, NT, NR], f32)
    TK = [topk.take(f"TK{i}", [128, NT, NR], f32) for i in range(2)]
    ONE1 = topk.take("ONE1", [128, NT, NR], f32)
    ONE2 = topk.take("ONE2", [128, NT, NR], f32)
    M1 = topk.take("M1", [128, NT], f32)
    M2 = topk.take("M2", [128, NT], f32)
    MK = topk.take("MK", [128, NT], f32)
    WT1 = topk.take("WT1", [128, NT], f32)
    WT2 = topk.take("WT2", [128, NT], f32)
    PT = place(moe_at, "PT", [NR, T], f32)

    class Experts:
        pass

    moe = []
    for l, (ne, hc, gated) in enumerate(((E0, HC0, False), (E1, HC1, True))):
        m = Experts()
        m.l, m.ne, m.hc, m.gated = l, ne, hc, gated
        m.hid = 128 * hc
        m.wcols = KC * m.hid * (2 if gated else 1) + hc * D
        r = Region(moe_at)
        m.HH = [r.take(f"HH{l}{u}", [128, hc, QB], f32r) for u in range(2)]
        m.HL = [r.take(f"HL{l}{u}", [128, hc, QB], f32r) for u in range(2)]
        if gated:
            m.SG = [r.take(f"SG{u}", [128, QB], f32) for u in range(2)]
            w = Region(kregion)
            raw = Region(vregion)
            hf = Region(gregion + 8192)
        else:
            w, raw, hf = r, Region(gregion + 5120), r
        m.WH = [w.take(f"WH{l}{u}", [128, m.wcols], f32r) for u in range(2)]
        m.WL = [w.take(f"WL{l}{u}", [128, m.wcols], f32r) for u in range(2)]
        m.RAW = [raw.take(f"RAW{l}{u}", [128, m.wcols], f32) for u in range(2)]
        m.HF = [hf.take(f"HF{l}{u}", [128, QB], f32) for u in range(2)]
        moe.append(m)

    ctx = ExitStack()
    with ctx:
        ps = ctx.enter_context(nc.psum_tensor("ps", [128, 8, 512], f32))

        def sem(name):
            return ctx.enter_context(nc.semaphore(name))

        kd = [nc.dram_tensor(f"k_parts{l}", [3, D, SP], bf16).ap() for l in range(2)]
        qd = [nc.dram_tensor(f"q_parts{l}", [3, D, T], bf16).ap() for l in range(2)]

        pos_loaded, const_loaded, ctx_loaded, wctx_loaded, x_loaded, rest_loaded = (
            sem("pos_loaded"), sem("const_loaded"), sem("ctx_loaded"), sem("wctx_loaded"),
            sem("x_loaded"), sem("rest_loaded"))
        dve_done, pool_done, act_done = sem("dve_done"), sem("pool_done"), sem("act_done")
        angle_ready, table_ready = sem("angle_ready"), sem("table_ready")
        v_ready, v_taken = sem("v_ready"), sem("v_taken")
        unit_ready, unit_free, f_ready = sem("unit_ready"), sem("unit_free"), sem("f_ready")
        part1_ready, rest1_ready, part2_ready, part3_ready = (
            sem("part1_ready"), sem("rest1_ready"), sem("part2_ready"), sem("part3_ready"))
        parts_stored = [sem(f"parts_stored{c}") for c in range(2)]
        stats_done = sem("stats_done")
        var_ready, sd_ready, xc_ready, xt_ready, xn_ready = (
            sem("var_ready"), sem("sd_ready"), sem("xc_ready"), sem("xt_ready"), sem("xn_ready"))
        k_loaded, q_loaded, nm_loaded = sem("k_loaded"), sem("q_loaded"), sem("nm_loaded")
        row_ready, row_taken, m16_ready, cut_done, nm_ready, ones_set = (
            sem("row_ready"), sem("row_taken"), sem("m16_ready"), sem("cut_done"), sem("nm_ready"),
            sem("ones_set"))
        s_ready, exp_done, vg_ready, pv_done, acc_set, u_ready, on_ready = (
            sem("s_ready"), sem("exp_done"), sem("vg_ready"), sem("pv_done"), sem("acc_set"),
            sem("u_ready"), sem("on_ready"))
        o_ready, o_taken = sem("o_ready"), sem("o_taken")
        lg_ready, lg_moved, ex_ready, pw_ready, pt_ready, pt_copied, yb_ready, yb_taken, xh_ready, xl_ready = (
            sem("lg_ready"), sem("lg_moved"), sem("ex_ready"), sem("pw_ready"), sem("pt_ready"),
            sem("pt_copied"), sem("yb_ready"), sem("yb_taken"), sem("xh_ready"), sem("xl_ready"))
        w_loaded = [sem(f"w_loaded{u}") for u in range(2)]
        wh_ready, wl_ready = sem("wh_ready"), sem("wl_ready")
        h_ready, h_free, sg_ready, hh_ready, hl_ready, y_ready, y_free = (
            sem("h_ready"), sem("h_free"), sem("sg_ready"), sem("hh_ready"), sem("hl_ready"),
             sem("y_ready"), sem("y_free"))
        out_stored = sem("out_stored")

        class Order:

            def __init__(self, eng, done):
                self.eng, self.done, self.count = eng, done, 0

            def then(self, ins):
                ins.then_inc(self.done, 1)
                self.count = self.count + 1

            def wait(self):
                self.eng.wait_ge(self.done, self.count)

        one, two, y_start, y_slots, store_start = 1, 2, 32, 4, 16

        UNITS = {"k1": (0, False, SC, kd[1]), "k0": (8, True, SC, kd[0]),
                 "q0": (16, True, QB, qd[0]), "q1": (24, False, QB, qd[1])}

        def row_pieces(with_t, with_prep):
            n = NCH if with_prep else 0
            return ([("T", 0)] if with_t else []) + [("M", c) for c in range(min(16, n))] + [("D", 0)] + \
                   [("M", c) for c in range(16, n)]

        ROWS_HEAD = NCH + 1 + NCH
        ROWS_LOOP = NCH + 2
        ROWS_LAYER = ROWS_HEAD + (NIT - 2) * ROWS_LOOP + 2 + 1 + 1
        PAIRS = 2 * KT
        EXP_LAYER, PV_LAYER = PAIRS * NIT, KT * NIT

        def p_slot(u, j, half):
            return (2 * (u * KT + j) + half) % 4

        block = ctx.enter_context(nc.Block())

        @block.sync
        def _(sp):
            sp.dma_start(POS[:, :], dram["pos"].to_broadcast([128, NPOS])).then_inc(pos_loaded, 16)
            sp.dma_start(const[:, :], dram["const"]).then_inc(const_loaded, 16)
            sp.dma_start(ident[:, :], dram["ident"]).then_inc(const_loaded, 16)
            sp.dma_start(spread[:, :], dram["spread"]).then_inc(const_loaded, 16)
            sp.dma_start(CTX[:, :, :], dram["ctxT"].rearrange("(c p) n -> p c n", p=128)).then_inc(ctx_loaded, 16)
            sp.dma_start(WV[:, :, :], dram["wv"].rearrange("(c p) n -> p c n", p=128)).then_inc(ctx_loaded, 16)
            for n in ("k0", "k0s", "k1", "q0", "q0s"):
                sp.dma_start(W5[n][:, :, :], dram[n].rearrange("(c p) n -> p c n", p=128)).then_inc(wctx_loaded, 16)
            sp.dma_start(X[:, :, :], dram["x"].rearrange("(t p) d -> p t d", p=128)).then_inc(x_loaded, 16)
            sp.dma_start(WQ1[:, :, :], dram["q1"].rearrange("(c p) n -> p c n", p=128)).then_inc(rest_loaded, 16)
            for l in range(2):
                sp.dma_start(WO[:, l, :, :], dram[f"wo{l}"]).then_inc(rest_loaded, 16)
                sp.dma_start(router[:, l, :, :],
                             dram[f"router{l}"].rearrange("(c p) n -> p c n", p=128)).then_inc(rest_loaded, 16)
            sp.dma_start(rbias[:, :], dram["rbias"].to_broadcast([128, NR])).then_inc(rest_loaded, 16)
            sp.dma_start(prio[:, :, :], dram["prio"]).then_inc(rest_loaded, 16)
            sp.dma_start(bo0[:, :], dram["bo0"].to_broadcast([128, D])).then_inc(rest_loaded, 16)
            sp.dma_start(bout0[:, :], dram["bout0"]).then_inc(rest_loaded, 16)

            def store_parts(kind):
                first, _, n, dst = UNITS[kind]
                view = dst.rearrange("s f n -> f s n")
                with sp.Fori(0, 4) as b:
                    for c in range(2):
                        sp.wait_ge(part3_ready, two + first + 2 * b + c + 1)
                        sp.dma_start(view[128 * c:128 * c + 128, :, bass.ds(b * n, n)],
                                     PARTS[c][:, :, 0:n]).then_inc(parts_stored[c], 16)

            def load_k(l):
                for p, (_, part) in enumerate(PRODUCTS):
                    sp.dma_start(KSTK[16 * p:16 * p + 16, :, :],
                                 kd[l][part].rearrange("(h d) n -> d h n", d=DH)[:, :, 0:S]).then_inc(k_loaded, 16)

            def load_q(l, slot, b, g):
                for p, (part, _) in enumerate(PRODUCTS):
                    src = qd[l][part].rearrange("(g h d) n -> d g h n", d=DH, h=HG)
                    sp.dma_start(QST[16 * p:16 * p + 16, bass.ds(slot * HG, HG), :],
                                 src[:, bass.ds(g, 1), :, bass.ds(b * QB, QB)].rearrange("d g h n -> d (g h) n")
                                 ).then_inc(q_loaded, 16)

            def load_nm(l, n, slot):
                sp.wait_ge(nm_ready, l * NIT + n + 1)
                for s in range(3):
                    sp.dma_start(QST[NSTACK + s:NSTACK + s + 1, bass.ds(slot * HG, HG), :],
                                 NM[:, s, :]).then_inc(nm_loaded, 16)

            def attention(l):
                for c in range(2):
                    sp.wait_ge(parts_stored[c], store_start + 16 * (UNITS[f"q{l}"][0] // 2 + 4))
                for n in range(3):
                    load_q(l, n, 0, n)
                load_nm(l, 0, 0)
                with sp.Fori(3, NIT) as n:
                    sp.wait_ge(row_ready, l * ROWS_LAYER + ROWS_HEAD + ROWS_LOOP * (n - 3) + 2)
                    load_q(l, n % 4, n // 4, n % 4)
                    load_nm(l, n - 2, (n - 2) % 4)
                load_nm(l, NIT - 2, (NIT - 2) % 4)
                load_nm(l, NIT - 1, (NIT - 1) % 4)

            def expert_weights(m):
                with sp.Fori(0, m.ne // 2) as pair:
                    for u in range(2):
                        e = 2 * pair + u
                        sp.wait_ge(wl_ready, m.l * E0 + e + 1)
                        if not m.gated:
                            sp.dma_start(BRAW[u][:, :], dram["bin0"][bass.ds(e, 1), :, :].rearrange("e p c -> p (e c)")
                                         ).then_inc(w_loaded[u], 16)
                        at = 0
                        for name in (("w1", "w3", "w2") if m.gated else ("w_in", "w_out")):
                            src = dram[name]
                            rows, cols = src.shape[1] // 128, src.shape[2]
                            sp.dma_start(m.RAW[u][:, at:at + rows * cols].rearrange("p (c n) -> p c n", c=rows),
                                         src[bass.ds(e, 1), :, :].rearrange("e (c p) n -> p (e c) n", p=128)
                                         ).then_inc(w_loaded[u], 16)
                            at += rows * cols

            store_parts("k1")
            store_parts("k0")
            for c in range(2):
                sp.wait_ge(parts_stored[c], store_start + 16 * 8)
            sp.wait_ge(v_taken, 2 * KT)
            sp.dma_start(KSTK[NSTACK:NSTACK + 3, :, :], dram["ones"]).then_inc(k_loaded, 16)
            load_k(0)
            store_parts("q0")
            attention(0)
            sp.wait_ge(s_ready, EXP_LAYER)
            load_k(1)
            sp.wait_ge(pv_done, two + PV_LAYER)
            expert_weights(moe[0])
            store_parts("q1")
            attention(1)
            sp.wait_ge(o_ready, 2 * NT)
            expert_weights(moe[1])
            for b in range(NB):
                sp.wait_ge(y_free, y_slots + (E0 + E1) * NT - NT + 4 * b + 4)
                sp.dma_start(out.rearrange("(t p) d -> p t d", p=128)[:, 4 * b:4 * b + 4, :],
                             X[:, 4 * b:4 * b + 4, :]).then_inc(out_stored, 16)
            sp.wait_ge(out_stored, 16 * NB)

        @block.tensor
        def _(pe):
            def v_of_context():
                pe.wait_ge(ctx_loaded, 32)
                for j, rows in enumerate(KROWS):
                    if j >= 2:
                        pe.wait_ge(v_taken, 2 * (j - 1))
                    for c in range(KC):
                        last = nc.tensor.matmul(ps[0:rows, 4 + j % 2, :], CTX[:, c, 128 * j:128 * j + rows],
                                                WV[:, c, :], start=(c == 0), stop=(c == KC - 1))
                    last.then_inc(v_ready, 1)

            def units(kind):
                first, rope, n, _ = UNITS[kind]
                w = WQ1 if kind == "q1" else W5[kind]
                src = CTX if kind[0] == "k" else XN
                with pe.Fori(0, 4) as b:
                    for c in range(2):
                        pe.wait_ge(unit_free, first + 2 * b + c + 1)
                        for k, wk in enumerate((w, W5[kind + "s"]) if rope else (w,)):
                            for kc in range(KC):
                                last = nc.tensor.matmul(ps[:, 2 * c + k, 0:n], wk[:, kc, 128 * c:128 * c + 128],
                                                        src[:, kc, bass.ds(b * n, n)],
                                                        start=(kc == 0), stop=(kc == KC - 1))
                        last.then_inc(unit_ready, 1)

            def norm_transposes(k):
                with pe.Fori(0, 4) as q:
                    for half in range(2):
                        pair = 2 * q + half
                        pe.wait_ge(xc_ready, NT * k + 2 * pair + 2)
                        pe.wait_ge(xn_ready, 8 * k + pair + 1)
                        for i in range(2):
                            for c in range(KC):
                                last = nc.tensor.transpose(
                                    ps[:, half, 256 * c + 128 * i:256 * c + 128 * i + 128],
                                    XC[2 * half + i][:, 128 * c:128 * c + 128], ident[:, :])
                        last.then_inc(xt_ready, 1)

            def row_piece(e, bank, what, c, kq):
                pe.wait_ge(row_taken, e + 1)
                if what == "T":
                    last = nc.tensor.transpose(ps[0:NPAIR, bank, 0:128], M16[:, :], ident[:, :])
                elif what == "D":
                    last = nc.tensor.matmul(ps[:, bank, :], spread[:, :], U[:, :], start=True, stop=True)
                else:
                    pair, ch = divmod(c, len(MAXCOLS))
                    h, qt = divmod(pair, QB // 128)
                    off, w = MAXCOLS[ch]
                    head = kq * HG + h
                    last = nc.tensor.matmul(
                        ps[:, bank, 0:w],
                        QST[0:NSTACK, bass.ds(head, 1), 128 * qt:128 * qt + 128].rearrange("p a b -> p (a b)"),
                        KSTK[0:NSTACK, bass.ds(head, 1), off:off + w].rearrange("p a b -> p (a b)"),
                        start=True, stop=True)
                last.then_inc(row_ready, 1)

            def weigh(l, step, j, u):
                pe.wait_ge(exp_done, two + l * EXP_LAYER + 2 * step + 2)
                rows = KROWS[j]
                for h in range(HG):
                    last = nc.tensor.matmul(ps[32 * h:32 * h + 32, 4 + u, :], VG[u][0:rows, j, h, :],
                                            PR[p_slot(u, j, h // 2)][0:rows, h % 2, :],
                                            start=(j == 0), stop=(j == KT - 1), tile_position=(0, 32 * h))
                last.then_inc(pv_done, 1)

            def iteration(l, it, u, g, g2, with_t, with_prep, first):
                pieces = row_pieces(with_t, with_prep)
                at = [0]

                def rows(n, j):
                    for k in range(at[0], min(at[0] + n, len(pieces))):
                        what, c = pieces[k]
                        if what == "D" and j < 2:
                            return
                        if what == "D":
                            pe.wait_ge(u_ready, one + l * (NIT + 1) + it + 1)
                        if what == "T":
                            pe.wait_ge(m16_ready, l * NIT + it + 2)
                        if what == "M" and c == 0:
                            pe.wait_ge(q_loaded, 96 * (l * NIT + it + 3))
                        row_piece(first + k, 6 + (ROWS_HEAD + k) % 2, what, c, g2)
                        at[0] = k + 1

                pe.wait_ge(nm_loaded, 48 * (l * NIT + it + 1))
                for j in range(KT):
                    step = KT * it + j
                    for half in range(2):
                        pe.wait_ge(exp_done, l * EXP_LAYER + 2 * step + half + 1)
                        for h in (2 * half, 2 * half + 1):
                            head = g * HG + h
                            last = nc.tensor.matmul(
                                ps[0:KROWS[j], h, :],
                                KSTK[:, bass.ds(head, 1), 128 * j:128 * j + KROWS[j]].rearrange("p a b -> p (a b)"),
                                QST[:, bass.ds(head, 1), :].rearrange("p a b -> p (a b)"),
                                start=True, stop=True)
                        last.then_inc(s_ready, 1)
                        rows(1, j)
                    if j > 0:
                        if j == 1:
                            pe.wait_ge(vg_ready, l * NIT + it + 1)
                            pe.wait_ge(u_ready, one + l * (NIT + 1) + it)
                        weigh(l, step - 1, j - 1, u)
                    rows(3, j)
                rows(NCH, KT)
                weigh(l, KT * it + KT - 1, KT - 1, u)

            def attention(l):
                pe.wait_ge(k_loaded, 16 + 96 * (l + 1))
                e = 0
                pe.wait_ge(q_loaded, 96 * (l * NIT + 3))
                for n in range(2):
                    for c in range(NCH):
                        row_piece(l * ROWS_LAYER + e, 6 + e % 2, "M", c, n)
                        e += 1
                    if n == 0:
                        pe.wait_ge(m16_ready, l * NIT + 1)
                        row_piece(l * ROWS_LAYER + e, 6 + e % 2, "T", 0, 0)
                        e += 1
                first = l * ROWS_LAYER + ROWS_HEAD
                with pe.Fori(0, NIT // 2 - 1) as i:
                    for u in range(2):
                        it = 2 * i + u
                        iteration(l, it, u, it % 4, (it + 2) % 4, True, True, first + ROWS_LOOP * it)
                first = first + ROWS_LOOP * (NIT - 2)
                iteration(l, NIT - 2, 0, 2, 0, True, False, first)
                iteration(l, NIT - 1, 1, 3, 0, False, False, first + 2)
                pe.wait_ge(u_ready, one + (l + 1) * (NIT + 1))
                row_piece(first + 3, 6 + (ROWS_HEAD + 3) % 2, "D", 0, 0)

            def output_projection(l):
                pe.wait_ge(rest_loaded, 16 * 9)
                pe.wait_ge(on_ready, one + (l + 1) * (NIT + 1))
                for t in range(NT):
                    if t >= 4:
                        pe.wait_ge(o_taken, NT * l + t - 3)
                    b, qt = divmod(t, 4)
                    for g in range(NG):
                        last = nc.tensor.matmul(ps[:, t % 4, 0:D], ON[:, NG * b + g, 128 * qt:128 * qt + 128],
                                                WO[:, l, g, :], start=(g == 0), stop=(g == NG - 1))
                    last.then_inc(o_ready, 1)

            def router_logits(l):
                pe.wait_ge(rest_loaded, 16 * 9)
                for t in range(NT):
                    if t % 2 == 0:
                        pe.wait_ge(xn_ready, two + 8 * (2 * l + 1) + t // 2 + 1)
                    for c in range(KC):
                        last = nc.tensor.matmul(ps[:, 2, NR * t:NR * t + NR], XN[:, c, 128 * t:128 * t + 128],
                                                router[:, l, c, :], start=(c == 0), stop=(c == KC - 1))
                last.then_inc(lg_ready, 1)

            def expert_output_bias():
                pe.wait_ge(pw_ready, 1)
                for b in range(NB):
                    for i in range(4):
                        last = nc.tensor.transpose(ps[0:NR, 4 + b, 128 * i:128 * i + 128],
                                                   PW[:, 4 * b + i, 0:NR], ident[:, :])
                    last.then_inc(pt_ready, 1)
                for t in range(NT):
                    if t % 4 == 0:
                        pe.wait_ge(pt_copied, NB)
                    if t >= 4:
                        pe.wait_ge(yb_taken, t - 3)
                    nc.tensor.matmul(ps[:, 4 + t % 4, 0:D], PT[:, 128 * t:128 * t + 128], bout0[:, :],
                                     start=True, stop=True).then_inc(yb_ready, 1)

            def experts(m):
                hc, ne, l = m.hc, m.ne, m.l
                base_e = l * E0
                base_k = l * E0 * NB
                base_q = l * E0 * NB * HC0
                pe.wait_ge(pw_ready, l + 1)
                pe.wait_ge(xl_ready, NB * (l + 1))

                def three_passes(dst, lh, ll, rh, rl, first, final):
                    nc.tensor.matmul(dst, lh, rh, start=first, stop=False)
                    nc.tensor.matmul(dst, lh, rl, start=False, stop=False)
                    return nc.tensor.matmul(dst, ll, rh, start=False, stop=final)

                with pe.Fori(0, ne // 2) as pair:
                    for u in range(2):
                        e = 2 * pair + u
                        with pe.Fori(0, 2) as tp:
                            pe.wait_ge(wl_ready, two + base_e + e + 1)
                            for v in range(2):
                                tb = 2 * tp + v
                                for c in range(hc):
                                    q = base_q + (NB * e + tb) * hc + c
                                    pe.wait_ge(h_free, q + 1)
                                    for w in range(2 if m.gated else 1):
                                        for kc in range(KC):
                                            at = (w * KC + kc) * m.hid + 128 * c
                                            last = three_passes(
                                                ps[:, 2 * (c % 2) + w, :],
                                                m.WH[u][:, at:at + 128], m.WL[u][:, at:at + 128],
                                                XH[:, kc, bass.ds(QB * tb, QB)], XL[:, kc, bass.ds(QB * tb, QB)],
                                                kc == 0, kc == KC - 1)
                                    last.then_inc(h_ready, 1)
                            for v in range(2):
                                tb = 2 * tp + v
                                k = base_k + NB * e + tb
                                w2 = m.wcols - hc * D
                                pe.wait_ge(hl_ready, two + base_q + (NB * e + tb) * hc + hc)
                                for qt in range(4):
                                    pe.wait_ge(y_free, 4 * k + qt + 1)
                                    for c in range(hc):
                                        last = three_passes(
                                            ps[:, 4 + qt, 0:D],
                                            m.HH[v][:, c, 128 * qt:128 * qt + 128],
                                            m.HL[v][:, c, 128 * qt:128 * qt + 128],
                                            m.WH[u][:, w2 + D * c:w2 + D * c + D],
                                            m.WL[u][:, w2 + D * c:w2 + D * c + D],
                                            c == 0, c == hc - 1)
                                    last.then_inc(y_ready, 1)

            pe.wait_ge(const_loaded, 48)
            v_of_context()
            pe.wait_ge(wctx_loaded, 16 * 5)
            units("k1")
            pe.wait_ge(table_ready, 2)
            units("k0")
            norm_transposes(0)
            pe.wait_ge(xn_ready, two + 8)
            units("q0")
            attention(0)
            output_projection(0)
            norm_transposes(1)
            router_logits(0)
            expert_output_bias()
            experts(moe[0])
            norm_transposes(2)
            pe.wait_ge(xn_ready, two + 24)
            units("q1")
            attention(1)
            output_projection(1)
            norm_transposes(3)
            router_logits(1)
            experts(moe[1])

        @block.scalar
        def _(act):
            def evacuate_v(j, rows):
                act.wait_ge(v_ready, j + 1)
                for l in range(2):
                    nc.scalar.activation(V[l][0:rows, :, j, :],
                                         ps[0:rows, 4 + j % 2, D * l:D * l + D].rearrange("p (g n) -> p g n", g=NG),
                                         ACT.Copy).then_inc(v_taken, 1)

            def unit_parts(kind):
                first, _, n, _ = UNITS[kind]
                with act.Fori(0, 4) as b:
                    u0 = first + 2 * b
                    for c in range(2):
                        act.wait_ge(f_ready, u0 + c + 1)
                        act.wait_ge(parts_stored[c], 16 * (first // 2 + b + 1))
                        nc.scalar.activation(PARTS[c][:, 0, 0:n], F[c][:, 0:n], ACT.Copy).then_inc(part1_ready, 1)
                    for c in range(2):
                        act.wait_ge(rest1_ready, u0 + c + 1)
                        nc.scalar.activation(PARTS[c][:, 1, 0:n], G[c][:, 0:n], ACT.Copy).then_inc(part2_ready, 1)

            def norm_sd(k):
                act.wait_ge(var_ready, k + 1)
                nc.scalar.activation(norm[:, 3, :], norm[:, 2, :], ACT.Sqrt,
                                     bias=const[:, C_EPS:C_EPS + 1]).then_inc(sd_ready, 1)

            def norm_copies(k):
                with act.Fori(0, 4) as q:
                    for half in range(2):
                        pair = 2 * q + half
                        act.wait_ge(xt_ready, 8 * k + pair + 1)
                        act.wait_ge(sd_ready, k + 1)
                        nc.scalar.activation(XN[:, :, bass.ds(256 * pair, 256)],
                                             ps[:, half, :].rearrange("p (c n) -> p c n", c=KC),
                                             ACT.Copy).then_inc(xn_ready, 1)

            def exp_pair(l, it, j, half, u):
                step = KT * it + j
                rows = KROWS[j]
                act.wait_ge(s_ready, l * EXP_LAYER + 2 * step + half + 1)
                act.wait_ge(pv_done, l * PV_LAYER + step + 1)
                nc.scalar.activation(PR[p_slot(u, j, half)][0:rows, :, :],
                                     ps[0:rows, 2 * half:2 * half + 2, :], ACT.Exp,
                                     scale=DH ** -0.5).then_inc(exp_done, 1)

            def copy_sums(l, it, u):
                act.wait_ge(pv_done, two + l * PV_LAYER + KT * it)
                act.wait_ge(on_ready, one + l * (NIT + 1) + it)
                nc.scalar.activation(U[:, :], ps[:, 4 + u, :], ACT.Copy).then_inc(u_ready, 1)

            def attention(l):
                act.wait_ge(acc_set, l + 1)

                def iteration(it, u):
                    for j in range(KT):
                        for half in range(2):
                            exp_pair(l, it, j, half, u)
                        if j == 0:
                            copy_sums(l, it, 1 - u)

                with act.Fori(0, NIT // 2) as i:
                    for u in range(2):
                        iteration(2 * i + u, u)
                copy_sums(l, NIT, 1)

            def split_tokens(l):
                act.wait_ge(o_ready, NT * (l + 1))
                for b in range(NB):
                    act.wait_ge(xn_ready, two + 8 * (2 * l + 1) + 2 * b + 2)
                    nc.scalar.activation(XH[:, :, QB * b:QB * b + QB], XN[:, :, QB * b:QB * b + QB],
                                         ACT.Copy).then_inc(xh_ready, 1)

            def experts(m):
                hc, ne, l = m.hc, m.ne, m.l
                base_e, base_q, base_k = l * E0, l * E0 * NB * HC0, l * E0 * NB
                nload = 3
                base_w = l * nload * E0 // 2
                with act.Fori(0, ne // 2) as pair:
                    for u in range(2):
                        e = 2 * pair + u
                        act.wait_ge(w_loaded[u], 16 * (base_w + nload * (pair + 1)))
                        act.wait_ge(y_ready, y_start + NT * (base_e + e - 1))
                        if not m.gated:
                            nc.scalar.activation(BIN[u][:, :], BRAW[u][:, :], ACT.Copy)
                        nc.scalar.activation(m.WH[u][:, :], m.RAW[u][:, :], ACT.Copy).then_inc(wh_ready, 1)
                        act.wait_ge(wh_ready, base_e + e + 1)
                        with act.Fori(0, 2) as tp:
                            for v in range(2):
                                for c in range(hc):
                                    q = base_q + (NB * e + 2 * tp + v) * hc + c
                                    act.wait_ge(h_ready, q + 1)
                                    if m.gated:
                                        act.wait_ge(h_free, q + 1)
                                        nc.scalar.activation(m.SG[c % 2][:, :], ps[:, 2 * (c % 2), :],
                                                             ACT.Silu).then_inc(sg_ready, 1)
                                    else:
                                        act.wait_ge(hl_ready, q + 1)
                                        nc.scalar.activation(m.HF[c % 2][:, :], ps[:, 2 * (c % 2), :],
                                                             ACT.Gelu_apprx_tanh,
                                                             bias=BIN[u][:, c:c + 1]
                                                             ).then_inc(h_free, 1)

            for j, rows in enumerate(KROWS):
                evacuate_v(j, rows)
            unit_parts("k1")
            act.wait_ge(const_loaded, 48)
            act.wait_ge(angle_ready, 1)
            nc.scalar.activation(SIN[:, :], ANG[:, :], ACT.Sin, scale=const[:, C_SIGN:C_SIGN + 1]).then_inc(table_ready, 1)
            nc.scalar.activation(TURN[:, :], ANG[:, :], ACT.Abs).then_inc(act_done, 1)
            act.wait_ge(act_done, 1)
            nc.scalar.activation(COS[:, :], TURN[:, :], ACT.Sin, scale=-1.0,
                                 bias=const[:, C_HALFPI:C_HALFPI + 1]).then_inc(table_ready, 1)
            unit_parts("k0")
            norm_sd(0)
            norm_copies(0)
            unit_parts("q0")
            attention(0)
            norm_sd(1)
            norm_copies(1)
            act.wait_ge(lg_moved, 1)
            nc.scalar.activation(PB[:, :, :], LG[:, :, :], ACT.Exp).then_inc(ex_ready, 1)
            split_tokens(0)
            for b in range(NB):
                act.wait_ge(pt_ready, b + 1)
                nc.scalar.activation(PT[:, QB * b:QB * b + QB], ps[0:NR, 4 + b, :], ACT.Copy).then_inc(pt_copied, 1)
            experts(moe[0])
            norm_sd(2)
            norm_copies(2)
            unit_parts("q1")
            attention(1)
            norm_sd(3)
            norm_copies(3)
            act.wait_ge(lg_moved, 2)
            nc.scalar.activation(WT2[:, :], MK[:, :], ACT.Exp).then_inc(ex_ready, 1)
            split_tokens(1)
            experts(moe[1])

        @block.gpsimd
        def _(pool):
            def unit_parts(kind):
                first, _, n, _ = UNITS[kind]
                with pool.Fori(0, 4) as b:
                    u0 = first + 2 * b
                    for c in range(2):
                        pool.wait_ge(part1_ready, u0 + c + 1)
                        nc.gpsimd.tensor_tensor(G[c][:, 0:n], F[c][:, 0:n], PARTS[c][:, 0, 0:n],
                                                ALU.subtract).then_inc(rest1_ready, 1)
                    for c in range(2):
                        pool.wait_ge(part2_ready, u0 + c + 1)
                        nc.gpsimd.tensor_tensor(PARTS[c][:, 2, 0:n], G[c][:, 0:n], PARTS[c][:, 1, 0:n],
                                                ALU.subtract).then_inc(part3_ready, 1)

            def stage_v(l, n, u, g):
                pool.wait_ge(ones_set, 3 * (l + 1))
                for rows, j0, j1 in ((128, 0, KT - 1), (KROWS[-1], KT - 1, KT)):
                    last = nc.gpsimd.tensor_copy(
                        VG[u][0:rows, j0:j1, :, 0:DH].rearrange("p j h d -> p (j h) d"),
                        V[l][0:rows, bass.ds(g, 1), j0:j1, :].rearrange("p g j (h d) -> p (g j h) d", d=DH))
                last.then_inc(vg_ready, 1)

            def cut_maxima(l, n, t_piece):
                pool.wait_ge(row_taken, two + t_piece + 1)
                pool.wait_ge(nm_loaded, 48 * (l * NIT + n))
                base = l * NIT * 3 + 3 * n
                nc.gpsimd.tensor_tensor(NM[:, 0, :], NMF[:, 0, :], ZERO[:, :], ALU.add).then_inc(cut_done, 1)
                pool.wait_ge(cut_done, base + 1)
                nc.gpsimd.tensor_tensor(NMF[:, 1, :], NMF[:, 0, :], NM[:, 0, :], ALU.subtract).then_inc(cut_done, 1)
                pool.wait_ge(cut_done, base + 2)
                nc.gpsimd.tensor_tensor(NM[:, 1, :], NMF[:, 1, :], ZERO[:, :], ALU.add).then_inc(cut_done, 1)
                pool.wait_ge(cut_done, base + 3)
                nc.gpsimd.tensor_tensor(NM[:, 2, :], NMF[:, 1, :], NM[:, 1, :], ALU.subtract).then_inc(nm_ready, 1)

            def divide(slot, d_piece):
                pool.wait_ge(row_taken, two + d_piece + 1)
                nc.gpsimd.tensor_tensor(ON[:, bass.ds(slot, 1), :].rearrange("p a b -> p (a b)"),
                                        U[:, :], RD[:, :], ALU.mult).then_inc(on_ready, 1)

            def attention(l):
                nc.gpsimd.memset(ZERO[:, :], 0.0).then_inc(ones_set, 1)
                for u in range(2):
                    nc.gpsimd.memset(VG[u][:, :, :, DH:32], 1.0).then_inc(ones_set, 1)
                stage_v(l, 0, 0, 0)
                first = l * ROWS_LAYER
                cut_maxima(l, 0, first + NCH)
                first = first + ROWS_HEAD
                d_at = row_pieces(True, True).index(("D", 0))
                with pool.Fori(0, NIT // 2 - 1) as i:
                    for u in range(2):
                        it = 2 * i + u
                        cut_maxima(l, it + 1, first + ROWS_LOOP * it)
                        pool.wait_ge(pv_done, two + l * PV_LAYER + KT * it)
                        stage_v(l, it + 1, 1 - u, (it + 1) % 4)
                        divide((it + NIT - 1) % NIT, first + ROWS_LOOP * it + d_at)
                first = first + ROWS_LOOP * (NIT - 2)
                cut_maxima(l, NIT - 1, first)
                pool.wait_ge(pv_done, two + l * PV_LAYER + KT * (NIT - 2))
                stage_v(l, NIT - 1, 1, 3)
                for n in range(3):
                    divide(NIT - 3 + n, first + 1 + n)

            def experts(m):
                hc, ne, l = m.hc, m.ne, m.l
                base_e, base_q, base_k = l * E0, l * E0 * NB * HC0, l * E0 * NB
                with pool.Fori(0, ne // 2) as pair:
                    for u in range(2):
                        e = 2 * pair + u
                        pool.wait_ge(wh_ready, base_e + e + 1)
                        nc.gpsimd.tensor_tensor(m.WL[u][:, :], m.RAW[u][:, :], m.WH[u][:, :].bitcast(f32),
                                                ALU.subtract).then_inc(wl_ready, 1)
                        with pool.Fori(0, 2) as tp:
                            for v in range(2):
                                for c in range(hc):
                                    q = base_q + (NB * e + 2 * tp + v) * hc + c
                                    pool.wait_ge(hh_ready, q + 1)
                                    nc.gpsimd.tensor_tensor(m.HL[v][:, c, :], m.HF[c % 2][:, :],
                                                            m.HH[v][:, c, :].bitcast(f32),
                                                            ALU.subtract).then_inc(hl_ready, 1)

            unit_parts("k1")
            unit_parts("k0")
            unit_parts("q0")
            attention(0)
            experts(moe[0])
            unit_parts("q1")
            attention(1)
            experts(moe[1])

        @block.vector
        def _(dve):
            order = Order(dve, dve_done)

            def ordered(ins):
                order.then(ins)
                order.wait()

            def angles():
                dve.wait_ge(pos_loaded, 16)
                dve.wait_ge(const_loaded, 48)
                ordered(nc.vector.tensor_copy(ANG[:, :], POS[:, :]))
                ordered(nc.vector.tensor_scalar(ANG[:, :], ANG[:, :], const[:, C_FREQ:C_FREQ + 1], None, ALU.mult))
                ordered(nc.vector.tensor_scalar(TURN[:, :], ANG[:, :], float(0.5 / np.pi), ROUND, ALU.mult, ALU.add))
                ordered(nc.vector.tensor_scalar(TURN[:, :], TURN[:, :], ROUND, None, ALU.subtract))
                for part in TWO_PI_PARTS:
                    ordered(nc.vector.scalar_tensor_tensor(ANG[:, :], TURN[:, :], -part, ANG[:, :], ALU.mult, ALU.add))
                nc.vector.tensor_scalar(ANG[:, :], ANG[:, :], PI_BELOW, -PI_BELOW, ALU.min,
                                        ALU.max).then_inc(angle_ready, 1)

            def units(kind):
                first, rope, n, _ = UNITS[kind]
                col = T if kind[0] == "k" else 0
                with dve.Fori(0, 4) as b:
                    for c in range(2):
                        u = first + 2 * b + c
                        dve.wait_ge(unit_ready, u + 1)
                        dve.wait_ge(part3_ready, u + 1)
                        if rope:
                            nc.vector.tensor_tensor(F[c][:, 0:n], ps[:, 2 * c, 0:n],
                                                    COS[:, bass.ds(b * n + col, n)], ALU.mult)
                            nc.vector.tensor_tensor(G[c][:, 0:n], ps[:, 2 * c + 1, 0:n],
                                                    SIN[:, bass.ds(b * n + col, n)], ALU.mult).then_inc(unit_free, 1)
                            dve.wait_ge(unit_free, two + u + 1)
                            nc.vector.tensor_tensor(F[c][:, 0:n], F[c][:, 0:n], G[c][:, 0:n],
                                                    ALU.add).then_inc(f_ready, 1)
                        else:
                            nc.vector.tensor_copy(F[c][:, 0:n], ps[:, 2 * c, 0:n]).then_inc(f_ready, 1)
                            dve.wait_ge(f_ready, u + 1)
                            nc.vector.memset(scrap[:, 30 + c:31 + c], 0.0).then_inc(unit_free, 1)

            def norm_variance():
                half = D // 2
                ordered(nc.vector.tensor_tensor(norm[:, 0, :], stats[:, :, 1], stats[:, :, 4], ALU.add))
                ordered(nc.vector.tensor_scalar(norm[:, 0, :], norm[:, 0, :], 0.5, None, ALU.mult))
                ordered(nc.vector.tensor_tensor(norm[:, 1, :], stats[:, :, 1], stats[:, :, 4], ALU.subtract))
                ordered(nc.vector.tensor_tensor(norm[:, 1, :], norm[:, 1, :], norm[:, 1, :], ALU.mult))
                ordered(nc.vector.tensor_scalar(norm[:, 1, :], norm[:, 1, :], 0.25, None, ALU.mult))
                ordered(nc.vector.tensor_tensor(norm[:, 2, :], stats[:, :, 2], stats[:, :, 5], ALU.add))
                nc.vector.scalar_tensor_tensor(norm[:, 2, :], norm[:, 2, :], 1.0 / D, norm[:, 1, :], ALU.mult,
                                               ALU.add).then_inc(var_ready, 1)

            def norm_apply(k):
                dve.wait_ge(sd_ready, k + 1)
                ordered(nc.vector.reciprocal(norm[:, 4, :], norm[:, 3, :]))
                with dve.Fori(0, 4) as q:
                    for i in range(4):
                        t = 4 * q + i
                        if i % 2 == 0:
                            dve.wait_ge(xn_ready, 8 * k + 2 * q + i // 2 + 1)
                        nc.vector.tensor_scalar(XC[i][:, :], X[:, bass.ds(t, 1), :].rearrange("p a d -> p (a d)"),
                                                norm[:, 0, bass.ds(t, 1)],
                                                norm[:, 4, bass.ds(t, 1)], ALU.subtract, ALU.mult
                                                ).then_inc(xc_ready, 1)

            def norm_stats():
                with dve.Fori(0, NT) as t:
                    nc.vector.bn_stats(stats[:, bass.ds(t, 1), :].rearrange("p a s -> p (a s)"),
                                       X[:, bass.ds(t, 1), :].rearrange("p a d -> p (a d)")).then_inc(stats_done, 1)

            def row_piece(l, it, e, bank, what, c):
                dve.wait_ge(row_ready, e + 1)
                if what == "M":
                    pair, ch = divmod(c, len(MAXCOLS))
                    nc.vector.reduce_max(MXC[:, pair, ch:ch + 1], ps[:, bank, 0:MAXCOLS[ch][1]],
                                         AX.X).then_inc(row_taken, 1)
                elif what == "T":
                    dve.wait_ge(nm_ready, l * NIT + it + 1)
                    nc.vector.tensor_scalar(NMF[:, 0, :], ps[0:NPAIR, bank, 0:128], -1.0, None,
                                            ALU.mult).then_inc(row_taken, 1)
                else:
                    dve.wait_ge(on_ready, one + l * (NIT + 1) + it)
                    nc.vector.reciprocal(RD[:, :], ps[:, bank, :]).then_inc(row_taken, 1)

            def row_maxima(e_last):
                dve.wait_ge(row_taken, two + e_last + 1)
                nc.vector.tensor_reduce(M16[:, :], MXC[:, :, :], AX.X, ALU.max).then_inc(m16_ready, 1)

            def attention(l):
                nc.vector.memset(ps[:, 5, :], 1.0).then_inc(acc_set, 1)
                first = l * ROWS_LAYER
                for c in range(NCH):
                    row_piece(l, 0, first + c, 6 + c % 2, "M", c)
                row_maxima(first + NCH - 1)
                e = NCH
                row_piece(l, -1, first + e, 6 + e % 2, "T", 0)
                for c in range(NCH):
                    row_piece(l, 0, first + e + 1 + c, 6 + (e + 1 + c) % 2, "M", c)
                row_maxima(first + ROWS_HEAD - 1)

                def iteration(it, first, with_t, with_prep):
                    pieces = row_pieces(with_t, with_prep)
                    for k, (what, c) in enumerate(pieces):
                        row_piece(l, it, first + k, 6 + (ROWS_HEAD + k) % 2, what, c)
                    if with_prep:
                        row_maxima(first + len(pieces) - 1)

                first = first + ROWS_HEAD
                with dve.Fori(0, NIT // 2 - 1) as i:
                    for u in range(2):
                        it = 2 * i + u
                        iteration(it, first + ROWS_LOOP * it, True, True)
                first = first + ROWS_LOOP * (NIT - 2)
                iteration(NIT - 2, first, True, False)
                iteration(NIT - 1, first + 2, False, False)
                row_piece(l, NIT, first + 3, 6 + (ROWS_HEAD + 3) % 2, "D", 0)

            def output_residual(l):
                for t in range(NT):
                    dve.wait_ge(o_ready, NT * l + t + 1)
                    nc.vector.tensor_tensor(X[:, t, :], ps[:, t % 4, 0:D], X[:, t, :], ALU.add).then_inc(o_taken, 1)
                dve.wait_ge(o_taken, NT * (l + 1))

            def wide(a):
                return a[:, :].unsqueeze(2).to_broadcast([128, NT, NR])

            def first_greatest(values, greatest, chosen):
                ordered(nc.vector.tensor_reduce(greatest[:, :], values[:, :, :], AX.X, ALU.max))
                ordered(nc.vector.tensor_tensor(TK[0][:, :, :], values[:, :, :], wide(greatest), ALU.is_equal))
                ordered(nc.vector.tensor_tensor(TK[0][:, :, :], TK[0][:, :, :], prio[:, :, :], ALU.mult))
                ordered(nc.vector.tensor_reduce(MK[:, :], TK[0][:, :, :], AX.X, ALU.max))
                ordered(nc.vector.tensor_tensor(chosen[:, :, :], TK[0][:, :, :], wide(MK), ALU.is_equal))

            def two_greatest(values):
                first_greatest(values, M1, ONE1)
                ordered(nc.vector.scalar_tensor_tensor(TK[1][:, :, :], ONE1[:, :, :], -3e38, values[:, :, :],
                                                       ALU.mult, ALU.add))
                first_greatest(TK[1], M2, ONE2)

            def route(l):
                dve.wait_ge(rest_loaded, 16 * 9)
                dve.wait_ge(lg_ready, l + 1)
                logits = ps[:, 2, 0:NT * NR].rearrange("p (t e) -> p t e", e=NR)
                if l == 0:
                    ordered(nc.vector.tensor_copy(LG[:, :, :], logits))
                    ordered(nc.vector.tensor_reduce(M1[:, :], LG[:, :, :], AX.X, ALU.max))
                    nc.vector.tensor_tensor(LG[:, :, :], LG[:, :, :], wide(M1), ALU.subtract).then_inc(lg_moved, 1)
                    dve.wait_ge(ex_ready, 1)
                    ordered(nc.vector.tensor_reduce(M2[:, :], PB[:, :, :], AX.X, ALU.add))
                    ordered(nc.vector.reciprocal(M2[:, :], M2[:, :]))
                    ordered(nc.vector.tensor_tensor(PB[:, :, :], PB[:, :, :], wide(M2), ALU.mult))
                    two_greatest(PB)
                    ordered(nc.vector.tensor_tensor(ONE1[:, :, :], ONE1[:, :, :], ONE2[:, :, :], ALU.add))
                    nc.vector.tensor_tensor(PW[:, :, 0:NR], ONE1[:, :, :], PB[:, :, :], ALU.mult).then_inc(pw_ready, 1)
                else:
                    ordered(nc.vector.tensor_tensor(LG[:, :, :], logits,
                                                    rbias[:, :].unsqueeze(1).to_broadcast([128, NT, NR]), ALU.add))
                    two_greatest(LG)
                    nc.vector.tensor_tensor(MK[:, :], M2[:, :], M1[:, :], ALU.subtract).then_inc(lg_moved, 1)
                    dve.wait_ge(ex_ready, 2)
                    ordered(nc.vector.tensor_scalar(WT1[:, :], WT2[:, :], 1.0, None, ALU.add))
                    ordered(nc.vector.reciprocal(WT1[:, :], WT1[:, :]))
                    ordered(nc.vector.tensor_tensor(WT2[:, :], WT2[:, :], WT1[:, :], ALU.mult))
                    ordered(nc.vector.tensor_tensor(ONE1[:, :, :], ONE1[:, :, :], wide(WT1), ALU.mult))
                    ordered(nc.vector.tensor_tensor(ONE2[:, :, :], ONE2[:, :, :], wide(WT2), ALU.mult))
                    ordered(nc.vector.memset(PW[:, :, NR:E1], 1.0))
                    nc.vector.tensor_tensor(PW[:, :, 0:NR], ONE1[:, :, :], ONE2[:, :, :], ALU.add).then_inc(pw_ready, 1)

            def split_tokens(l):
                for b in range(NB):
                    dve.wait_ge(xh_ready, NB * l + b + 1)
                    cols = slice(QB * b, QB * b + QB)
                    nc.vector.tensor_tensor(XL[:, :, cols], XN[:, :, cols], XH[:, :, cols].bitcast(f32),
                                            ALU.subtract).then_inc(xl_ready, 1)

            def expert_output_bias():
                for t in range(NT):
                    dve.wait_ge(yb_ready, t + 1)
                    nc.vector.tensor_tensor(X[:, t, :], ps[:, 4 + t % 4, 0:D], X[:, t, :],
                                            ALU.add).then_inc(yb_taken, 1)
                dve.wait_ge(yb_taken, NT)

            def experts(m):
                hc, ne, l = m.hc, m.ne, m.l
                base_q, base_k = l * E0 * NB * HC0, l * E0 * NB
                with dve.Fori(0, ne // 2) as pair:
                    for u in range(2):
                        e = 2 * pair + u
                        with dve.Fori(0, 2) as tp:
                            for v in range(2):
                                k = base_k + NB * e + 2 * tp + v
                                dve.wait_ge(y_ready, 4 * k + y_start - 4)
                                for c in range(hc):
                                    q = base_q + (NB * e + 2 * tp + v) * hc + c
                                    if m.gated:
                                        dve.wait_ge(sg_ready, q - base_q + 1)
                                        dve.wait_ge(hl_ready, q + 1)
                                        nc.vector.tensor_tensor(m.HF[c % 2][:, :], m.SG[c % 2][:, :],
                                                                ps[:, 2 * (c % 2) + 1, :], ALU.mult).then_inc(h_free, 1)
                                    dve.wait_ge(h_free, two + q + 1)
                                    nc.vector.tensor_copy(m.HH[v][:, c, :], m.HF[c % 2][:, :]).then_inc(hh_ready, 1)
                            for v in range(2):
                                k = base_k + NB * e + 2 * tp + v
                                for qt in range(4):
                                    t = 4 * (2 * tp + v) + qt
                                    dve.wait_ge(y_ready, y_start + 4 * k + qt + 1)
                                    dve.wait_ge(y_free, y_slots + 4 * k + qt)
                                    nc.vector.scalar_tensor_tensor(
                                        X[:, bass.ds(t, 1), :].rearrange("p a d -> p (a d)"), ps[:, 4 + qt, 0:D],
                                        PW[:, bass.ds(t, 1), bass.ds(e, 1)].rearrange("p a b -> p (a b)"),
                                        X[:, bass.ds(t, 1), :].rearrange("p a d -> p (a d)"),
                                        ALU.mult, ALU.add).then_inc(y_free, 1)

            for col, (s, n) in enumerate(((unit_free, two), (part3_ready, two), (parts_stored[0], store_start), (parts_stored[1], store_start), (xn_ready, two),
                         (row_taken, two), (exp_done, two), (pv_done, two), (wl_ready, two), (h_free, two),
                         (hl_ready, two), (y_ready, y_start), (y_free, y_slots), (u_ready, one),
                                           (on_ready, one))):
                nc.vector.memset(scrap[:, col:col + 1], 0.0).then_inc(s, n)
            angles()
            units("k1")
            dve.wait_ge(x_loaded, 16)
            norm_stats()
            dve.wait_ge(stats_done, NT)
            norm_variance()
            dve.wait_ge(table_ready, 2)
            units("k0")
            norm_apply(0)
            dve.wait_ge(xc_ready, NT)
            dve.wait_ge(rest_loaded, 16 * 9)
            ordered(nc.vector.tensor_tensor(X[:, :, :], X[:, :, :],
                                            bo0[:, :].unsqueeze(1).to_broadcast([128, NT, D]), ALU.add))
            units("q0")
            attention(0)
            output_residual(0)
            norm_stats()
            dve.wait_ge(stats_done, 2 * NT)
            norm_variance()
            norm_apply(1)
            route(0)
            split_tokens(0)
            expert_output_bias()
            experts(moe[0])
            dve.wait_ge(y_free, y_slots + E0 * NT)
            norm_stats()
            dve.wait_ge(stats_done, 3 * NT)
            norm_variance()
            norm_apply(2)
            units("q1")
            attention(1)
            output_residual(1)
            norm_stats()
            dve.wait_ge(stats_done, 4 * NT)
            norm_variance()
            norm_apply(3)
            route(1)
            split_tokens(1)
            experts(moe[1])


def _rows_swapped(w):
    return w.reshape(D // 2, 2, D)[:, ::-1].reshape(D, D)


def _heads_apart(wo):
    w = np.zeros((NG, HG, 32, D), wo.dtype)
    w[:, :, :DH] = wo.T.reshape(NG, HG, DH, D)
    return np.ascontiguousarray(w.reshape(NG, HG * 32, D).transpose(1, 0, 2))


def _laid_out(i):
    t = np.ascontiguousarray
    freq = np.float32(100.0) ** (-np.arange(0, DH, 2, dtype=np.float32) / np.float32(DH))
    const = np.zeros((128, 8), np.float32)
    const[:, C_FREQ] = np.tile(np.repeat(freq, 2), 128 // DH)
    const[:, C_SIGN] = np.tile([-1.0, 1.0], 64)
    const[:, C_HALFPI] = np.pi / 2
    const[:, C_EPS] = EPS
    spread = np.zeros((128, 128), np.float32)
    for h in range(HG):
        spread[32 * h + DH, 32 * h:32 * h + 32] = 1.0
    pos = np.zeros((1, NPOS), np.int32)
    pos[0, :T] = i["itok_BxS_3_4095"][0]
    pos[0, T:T + S] = i["itok_BxS2_0_4095"][0]
    ctx = np.zeros((D, SP), np.float32)
    ctx[:, :S] = i["ctx_1024"][0].T
    joined = lambda a, b: np.concatenate([i[a], i[b]], 0)
    a = {
        "x": i["x"][0], "pos": pos, "ctxT": ctx, "const": const, "ident": np.eye(128, dtype=np.float32),
        "spread": spread, "ones": np.ones((3, H, S), np.dtype("bfloat16")),
        "q0": i["L0_xattn_Wq"].T, "q0s": _rows_swapped(i["L0_xattn_Wq"]).T,
        "k0": i["L0_xattn_Wk"].T, "k0s": _rows_swapped(i["L0_xattn_Wk"]).T,
        "k1": i["L1_xattn_w_k"].T, "q1": i["L1_xattn_w_q"].T,
        "wv": np.concatenate([i["L0_xattn_Wv"].T, i["L1_xattn_w_v"].T], 1),
        "wo0": _heads_apart(i["L0_xattn_Wo"]), "wo1": _heads_apart(i["L1_xattn_w_o"]),
        "bo0": i["L0_xattn_bo"].reshape(1, D),
        "router0": i["L0_ffn_router_w"], "router1": i["L1_ffn_router_w"].T,
        "rbias": i["L1_ffn_expert_bias"].reshape(1, NR),
        "prio": np.tile(np.arange(NR, 0, -1, dtype=np.float32), (128, NT, 1)),
        "w_in": i["L0_ffn_w_in"], "w_out": i["L0_ffn_w_out"], "bout0": i["L0_ffn_b_out"],
        "bin0": i["L0_ffn_b_in"].reshape(E0, HC0, 128).transpose(0, 2, 1),
        "w1": joined("L1_ffn_w1", "L1_ffn_sw1").transpose(0, 2, 1),
        "w3": joined("L1_ffn_w3", "L1_ffn_sw3").transpose(0, 2, 1),
        "w2": joined("L1_ffn_w2", "L1_ffn_sw2").transpose(0, 2, 1),
    }
    return {n: t(v) for n, v in a.items()}


def kernel(**inputs):
    import concourse.bacc as _bacc
    from concourse.bass_utils import run_bass_kernel_spmd as _run

    nc = _bacc.Bacc("TRN2", target_bir_lowering=False, num_devices=1)
    arrays = _laid_out({n: np.asarray(v) for n, v in inputs.items()})
    dram = {n: nc.dram_tensor(f"in_{n}", a.shape, mybir.dt.from_np(a.dtype), kind="ExternalInput").ap()
            for n, a in arrays.items()}
    out = nc.dram_tensor("out", (T, D), mybir.dt.float32, kind="ExternalOutput").ap()
    build(nc, dram, out)
    r = _run(nc, [{f"in_{n}": a for n, a in arrays.items()}], core_ids=[0])
    return r.results[0]["out"].reshape(1, T, D)
```

```python
from contextlib import ExitStack

import concourse.bass as bass
import numpy as np
from concourse import mybir

T, D, S, H, DH = 2048, 256, 1601, 16, 16
NT = T // 128
KC = D // 128
NB, QB = 4, 512
NG, HG = 4, 4
NIT = NB * NG
KT = -(-S // 128)
KROWS = [min(128, S - 128 * j) for j in range(KT)]
SC = 401
SP = 4 * SC
MAXCOLS = [(0, 401), (401, 400), (801, 400), (1201, 400)]
PRODUCTS = [(0, 0), (0, 1), (0, 2), (1, 0), (1, 1), (2, 0)]
NSTACK = 16 * len(PRODUCTS)
NPAIR = HG * (QB // 128)
NCH = NPAIR * len(MAXCOLS)
NPOS = T + SP
E0, HC0 = 8, 2
E1, HC1 = 10, 4
NR = 8
EPS = 1e-5
ROUND = 12582912.0
PI_BELOW = 3.1415925
TWO_PI_PARTS = (6.28125, 0.0019350051879882812, 3.0199159819e-07)

C_FREQ, C_SIGN, C_HALFPI, C_EPS = range(4)


def build(nc, dram, out):
    f32, bf16, f32r, i32 = (mybir.dt.float32, mybir.dt.bfloat16, mybir.dt.float32r, mybir.dt.int32)
    ALU, ACT, AX = mybir.AluOpType, mybir.ActivationFunctionType, mybir.AxisListType

    start, limit = -(-nc.sbuf_base // 32) * 32, nc.sbuf_usable_end

    def place(offset, name, shape, dt):
        return nc.alloc_sbuf_tensor_at(name, shape, dt, offset=offset)

    class Region:
        def __init__(self, start):
            self.at = start

        def take(self, name, shape, dt):
            size = int(np.prod(shape[1:])) * (2 if dt == bf16 else 4)
            t = place(self.at, name, shape, dt)
            self.at += -(-size // 32) * 32
            assert self.at <= limit, (name, self.at)
            return t

    keep = Region(start)
    X = keep.take("X", [128, NT, D], f32)
    XN = keep.take("XN", [128, KC, T], f32)
    ident = keep.take("ident", [128, 128], f32)
    pick = keep.take("pick", [128, HG], f32)
    const = keep.take("const", [128, 8], f32)
    stats = keep.take("stats", [128, NT, 6], f32)
    norm = keep.take("norm", [128, 6, NT], f32)
    WO = keep.take("WO", [128, 2, NG, D], f32)
    WQ1 = keep.take("WQ1", [128, KC, D], f32)
    router = keep.take("router", [128, 2, KC, NR], f32)
    rbias = keep.take("rbias", [128, NR], f32)
    PW = keep.take("PW", [128, NT, E1], f32)
    prio = keep.take("prio", [128, NT, NR], f32)
    BRAW = [keep.take(f"BRAW{u}", [128, HC0], f32) for u in range(2)]
    BIN = [keep.take(f"BIN{u}", [128, HC0], f32) for u in range(2)]
    bout0 = keep.take("bout0", [NR, D], f32)
    bo0 = keep.take("bo0", [128, D], f32)
    scrap = keep.take("scrap", [1, 32], f32)
    kregion = keep.at
    KSTK = keep.take("KSTK", [NSTACK + 3, H, S], bf16)
    vregion = keep.at
    V = [keep.take(f"V{l}", [128, NG, KT, HG * DH], f32) for l in range(2)]
    gregion = keep.at
    VG = [keep.take(f"VG{u}", [128, KT, HG, 32], f32) for u in range(2)]
    rregion = keep.at

    r = Region(kregion)
    ANG = r.take("ANG", [128, NPOS], f32)
    TURN = r.take("TURN", [128, NPOS], f32)
    POS = place(kregion + -(-4 * NPOS // 32) * 32, "POS", [128, NPOS], i32)
    CTX = r.take("CTX", [128, KC, SP], f32)
    r = Region(rregion)
    W5 = {n: r.take(f"W_{n}", [128, KC, D], f32) for n in ("k0", "k0s", "k1")}
    WV = r.take("WV", [128, KC, 2 * D], f32)
    r = Region(rregion + 2 * HG * NG * QB)
    COS = r.take("COS", [128, NPOS], f32)
    SIN = r.take("SIN", [128, NPOS], f32)
    F = [r.take(f"F{c}", [128, QB], f32) for c in range(2)]
    G = [r.take(f"G{c}", [128, QB], f32) for c in range(2)]
    PARTS = [r.take(f"PARTS{c}", [128, 3, QB], bf16) for c in range(2)]
    W5.update({n: r.take(f"W_{n}", [128, KC, D], f32) for n in ("q0", "q0s")})
    XC = [place(gregion + 1024 * i, f"XC{i}", [128, D], f32) for i in range(4)]

    r = Region(rregion)
    QST = r.take("QST", [NSTACK + 3, H, QB], bf16)
    PR = [r.take(f"PR{n}", [128, 2, QB], f32) for n in range(4)]
    ON = r.take("ON", [128, NIT, QB], f32)
    U = r.take("U", [128, QB], f32)
    R16 = r.take("R16", [128, QB // 128, HG], f32)
    NM = r.take("NM", [NPAIR, 3, 128], bf16)
    NMF = r.take("NMF", [NPAIR, 2, 128], f32)
    ZERO = r.take("ZERO", [NPAIR, 128], f32)
    MXC = r.take("MXC", [128, NPAIR, len(MAXCOLS)], f32)
    M16 = r.take("M16", [128, NPAIR], f32)

    r = Region(rregion)
    XH = r.take("XH", [128, KC, T], f32r)
    XL = r.take("XL", [128, KC, T], f32r)
    moe_at = r.at
    topk = Region(gregion)
    LG = topk.take("LG", [128, NT, NR], f32)
    PB = topk.take("PB", [128, NT, NR], f32)
    TK = [topk.take(f"TK{i}", [128, NT, NR], f32) for i in range(2)]
    ONE1 = topk.take("ONE1", [128, NT, NR], f32)
    ONE2 = topk.take("ONE2", [128, NT, NR], f32)
    M1 = topk.take("M1", [128, NT], f32)
    M2 = topk.take("M2", [128, NT], f32)
    MK = topk.take("MK", [128, NT], f32)
    PT = place(moe_at, "PT", [NR, T], f32)

    class Experts:
        pass

    moe = []
    for l, (ne, hc, gated) in enumerate(((E0, HC0, False), (E1, HC1, True))):
        m = Experts()
        m.l, m.ne, m.hc, m.gated = l, ne, hc, gated
        m.hid = 128 * hc
        m.wcols = KC * m.hid * (2 if gated else 1) + hc * D
        r = Region(moe_at)
        m.HH = [r.take(f"HH{l}{u}", [128, hc, QB], f32r) for u in range(2)]
        m.HL = [r.take(f"HL{l}{u}", [128, hc, QB], f32r) for u in range(2)]
        if gated:
            m.SG = [r.take(f"SG{u}", [128, QB], f32) for u in range(2)]
            w = Region(kregion)
            raw = Region(vregion)
            hf = Region(gregion + 8192)
        else:
            w, raw, hf = r, Region(gregion + 5120), r
        m.WH = [w.take(f"WH{l}{u}", [128, m.wcols], f32r) for u in range(2)]
        m.WL = [w.take(f"WL{l}{u}", [128, m.wcols], f32r) for u in range(2)]
        m.RAW = [raw.take(f"RAW{l}{u}", [128, m.wcols], f32) for u in range(2)]
        m.HF = [hf.take(f"HF{l}{u}", [128, QB], f32) for u in range(2)]
        moe.append(m)

    ctx = ExitStack()
    with ctx:
        ps = ctx.enter_context(nc.psum_tensor("ps", [128, 8, 512], f32))

        def sem(name):
            return ctx.enter_context(nc.semaphore(name))

        kd = [nc.dram_tensor(f"k_parts{l}", [3, D, SP], bf16).ap() for l in range(2)]
        qd = [nc.dram_tensor(f"q_parts{l}", [3, D, T], bf16).ap() for l in range(2)]

        pos_loaded, const_loaded, ctx_loaded, wctx_loaded, x_loaded, rest_loaded = (
            sem("pos_loaded"), sem("const_loaded"), sem("ctx_loaded"), sem("wctx_loaded"),
            sem("x_loaded"), sem("rest_loaded"))
        dve_done, pool_done, act_done = sem("dve_done"), sem("pool_done"), sem("act_done")
        angle_ready, table_ready = sem("angle_ready"), sem("table_ready")
        v_ready, v_taken = sem("v_ready"), sem("v_taken")
        unit_ready, unit_free, f_ready = sem("unit_ready"), sem("unit_free"), sem("f_ready")
        part1_ready, rest1_ready, part2_ready, part3_ready = (
            sem("part1_ready"), sem("rest1_ready"), sem("part2_ready"), sem("part3_ready"))
        parts_stored = [sem(f"parts_stored{c}") for c in range(2)]
        stats_done = sem("stats_done")
        var_ready, sd_ready, xc_ready, xt_ready, xn_ready = (
            sem("var_ready"), sem("sd_ready"), sem("xc_ready"), sem("xt_ready"), sem("xn_ready"))
        k_loaded, q_loaded, nm_loaded = sem("k_loaded"), sem("q_loaded"), sem("nm_loaded")
        row_ready, row_taken, m16_ready, cut_done, nm_ready, ones_set = (
            sem("row_ready"), sem("row_taken"), sem("m16_ready"), sem("cut_done"), sem("nm_ready"),
            sem("ones_set"))
        s_ready, exp_done, vg_ready, pv_done, acc_set, u_ready, on_ready = (
            sem("s_ready"), sem("exp_done"), sem("vg_ready"), sem("pv_done"), sem("acc_set"),
            sem("u_ready"), sem("on_ready"))
        o_ready, o_taken = sem("o_ready"), sem("o_taken")
        lg_ready, lg_read, lg_moved, ex_ready, pw_ready, pt_ready, pt_copied, yb_ready, yb_taken, xl_ready = (
            sem("lg_ready"), sem("lg_read"), sem("lg_moved"), sem("ex_ready"), sem("pw_ready"), sem("pt_ready"),
            sem("pt_copied"), sem("yb_ready"), sem("yb_taken"), sem("xl_ready"))
        w_loaded = [sem(f"w_loaded{u}") for u in range(2)]
        wh_ready, wl_ready = sem("wh_ready"), sem("wl_ready")
        h_ready, h_free, sg_ready, hh_ready, hl_ready, y_ready, y_free = (
            sem("h_ready"), sem("h_free"), sem("sg_ready"), sem("hh_ready"), sem("hl_ready"),
             sem("y_ready"), sem("y_free"))
        out_stored = sem("out_stored")

        class Order:

            def __init__(self, eng, done):
                self.eng, self.done, self.count = eng, done, 0

            def then(self, ins):
                ins.then_inc(self.done, 1)
                self.count = self.count + 1

            def wait(self):
                self.eng.wait_ge(self.done, self.count)

        one, two, three, y_start, y_slots, store_start = 1, 2, 3, 32, 4, 16

        UNITS = {"k1": (0, False, SC, kd[1]), "k0": (8, True, SC, kd[0]),
                 "q0": (16, True, QB, qd[0]), "q1": (24, False, QB, qd[1])}

        def row_pieces(kind):
            if kind == "loop":
                return [("M", c) for c in range(8)] + [("TR", 0)] + [("M", c) for c in range(8, 14)] + \
                       [("D", 0)] + [("M", c) for c in range(14, NCH)]
            return [("TR", 0), ("D", 0)] if kind == "last but one" else [("R", 0), ("D", 0)]

        ROWS_HEAD = NCH + 1 + NCH
        ROWS_LOOP = len(row_pieces("loop"))
        TR_AT = row_pieces("loop").index(("TR", 0))
        ROWS_LAYER = ROWS_HEAD + (NIT - 2) * ROWS_LOOP + 6
        PAIRS = 2 * KT
        EXP_LAYER, PV_LAYER = PAIRS * NIT, KT * NIT

        ACC = 4

        assert ROWS_HEAD % 3 == 0 and ROWS_LOOP % 3 == 0 and ROWS_LAYER % 3 == 0

        def row_bank(k):
            return 5 + k % 3

        def p_slot(u, j, half):
            return (2 * (u * KT + j) + half) % 4

        block = ctx.enter_context(nc.Block())

        @block.sync
        def _(sp):
            sp.dma_start(POS[:, :], dram["pos"].to_broadcast([128, NPOS])).then_inc(pos_loaded, 16)
            sp.dma_start(const[:, :], dram["const"]).then_inc(const_loaded, 16)
            sp.dma_start(ident[:, :], dram["ident"]).then_inc(const_loaded, 16)
            sp.dma_start(pick[:, :], dram["pick"]).then_inc(const_loaded, 16)
            sp.dma_start(CTX[:, :, :], dram["ctxT"].rearrange("(c p) n -> p c n", p=128)).then_inc(ctx_loaded, 16)
            sp.dma_start(WV[:, :, :], dram["wv"].rearrange("(c p) n -> p c n", p=128)).then_inc(ctx_loaded, 16)
            for n in ("k0", "k0s", "k1", "q0", "q0s"):
                sp.dma_start(W5[n][:, :, :], dram[n].rearrange("(c p) n -> p c n", p=128)).then_inc(wctx_loaded, 16)
            sp.dma_start(X[:, :, :], dram["x"].rearrange("(t p) d -> p t d", p=128)).then_inc(x_loaded, 16)
            sp.dma_start(WQ1[:, :, :], dram["q1"].rearrange("(c p) n -> p c n", p=128)).then_inc(rest_loaded, 16)
            for l in range(2):
                sp.dma_start(WO[:, l, :, :], dram[f"wo{l}"]).then_inc(rest_loaded, 16)
                sp.dma_start(router[:, l, :, :],
                             dram[f"router{l}"].rearrange("(c p) n -> p c n", p=128)).then_inc(rest_loaded, 16)
            sp.dma_start(rbias[:, :], dram["rbias"].to_broadcast([128, NR])).then_inc(rest_loaded, 16)
            sp.dma_start(prio[:, :, :], dram["prio"]).then_inc(rest_loaded, 16)
            sp.dma_start(bo0[:, :], dram["bo0"].to_broadcast([128, D])).then_inc(rest_loaded, 16)
            sp.dma_start(bout0[:, :], dram["bout0"]).then_inc(rest_loaded, 16)

            def store_parts(kind, b0=0, b1=4):
                first, _, n, dst = UNITS[kind]
                view = dst.rearrange("s f n -> f s n")
                with sp.Fori(b0, b1) as b:
                    for c in range(2):
                        sp.wait_ge(part3_ready, two + first + 2 * b + c + 1)
                        sp.dma_start(view[128 * c:128 * c + 128, :, bass.ds(b * n, n)],
                                     PARTS[c][:, :, 0:n]).then_inc(parts_stored[c], 16)

            def load_k(l):
                for p, (_, part) in enumerate(PRODUCTS):
                    sp.dma_start(KSTK[16 * p:16 * p + 16, :, :],
                                 kd[l][part].rearrange("(h d) n -> d h n", d=DH)[:, :, 0:S]).then_inc(k_loaded, 16)

            def load_q(l, slot, b, g):
                for p, (part, _) in enumerate(PRODUCTS):
                    src = qd[l][part].rearrange("(g h d) n -> d g h n", d=DH, h=HG)
                    sp.dma_start(QST[16 * p:16 * p + 16, bass.ds(slot * HG, HG), :],
                                 src[:, bass.ds(g, 1), :, bass.ds(b * QB, QB)].rearrange("d g h n -> d (g h) n")
                                 ).then_inc(q_loaded, 16)

            def load_nm(l, n, slot):
                sp.wait_ge(nm_ready, l * NIT + n + 1)
                for s in range(3):
                    sp.dma_start(QST[NSTACK + s:NSTACK + s + 1, bass.ds(slot * HG, HG), :],
                                 NM[:, s, :]).then_inc(nm_loaded, 16)

            def attention(l):
                kind = f"q{l}"
                store_parts(kind, 0, 1)
                for c in range(2):
                    sp.wait_ge(parts_stored[c], store_start + 16 * (UNITS[kind][0] // 2 + 1))
                for n in range(3):
                    load_q(l, n, 0, n)
                store_parts(kind, 1, 4)
                for c in range(2):
                    sp.wait_ge(parts_stored[c], store_start + 16 * (UNITS[kind][0] // 2 + 4))
                load_nm(l, 0, 0)
                with sp.Fori(3, NIT) as n:
                    sp.wait_ge(row_ready, l * ROWS_LAYER + ROWS_HEAD + ROWS_LOOP * (n - 3) + 1)
                    load_q(l, n % 4, n // 4, n % 4)
                    load_nm(l, n - 2, (n - 2) % 4)
                load_nm(l, NIT - 2, (NIT - 2) % 4)
                load_nm(l, NIT - 1, (NIT - 1) % 4)

            def expert_weights(m):
                with sp.Fori(0, m.ne // 2) as pair:
                    for u in range(2):
                        e = 2 * pair + u
                        sp.wait_ge(wl_ready, m.l * E0 + e + 1)
                        if not m.gated:
                            sp.dma_start(BRAW[u][:, :], dram["bin0"][bass.ds(e, 1), :, :].rearrange("e p c -> p (e c)")
                                         ).then_inc(w_loaded[u], 16)
                        at = 0
                        for name in (("w1", "w3", "w2") if m.gated else ("w_in", "w_out")):
                            src = dram[name]
                            rows, cols = src.shape[1] // 128, src.shape[2]
                            sp.dma_start(m.RAW[u][:, at:at + rows * cols].rearrange("p (c n) -> p c n", c=rows),
                                         src[bass.ds(e, 1), :, :].rearrange("e (c p) n -> p (e c) n", p=128)
                                         ).then_inc(w_loaded[u], 16)
                            at += rows * cols

            store_parts("k1")
            store_parts("k0")
            for c in range(2):
                sp.wait_ge(parts_stored[c], store_start + 16 * 8)
            sp.wait_ge(v_taken, 2 * KT)
            sp.dma_start(KSTK[NSTACK:NSTACK + 3, :, :], dram["ones"]).then_inc(k_loaded, 16)
            load_k(0)
            attention(0)
            sp.wait_ge(s_ready, EXP_LAYER)
            load_k(1)
            sp.wait_ge(pv_done, two + PV_LAYER)
            expert_weights(moe[0])
            attention(1)
            sp.wait_ge(o_ready, 2 * NT)
            expert_weights(moe[1])
            for b in range(NB):
                sp.wait_ge(y_free, y_slots + (E0 + E1) * NT - NT + 4 * b + 4)
                sp.dma_start(out.rearrange("(t p) d -> p t d", p=128)[:, 4 * b:4 * b + 4, :],
                             X[:, 4 * b:4 * b + 4, :]).then_inc(out_stored, 16)
            sp.wait_ge(out_stored, 16 * NB)

        @block.tensor
        def _(pe):
            def v_of_context():
                pe.wait_ge(ctx_loaded, 32)
                for j, rows in enumerate(KROWS):
                    if j >= 2:
                        pe.wait_ge(v_taken, 2 * (j - 1))
                    for c in range(KC):
                        last = nc.tensor.matmul(ps[0:rows, 4 + j % 2, :], CTX[:, c, 128 * j:128 * j + rows],
                                                WV[:, c, :], start=(c == 0), stop=(c == KC - 1))
                    last.then_inc(v_ready, 1)

            def units(kind):
                first, rope, n, _ = UNITS[kind]
                w = WQ1 if kind == "q1" else W5[kind]
                src = CTX if kind[0] == "k" else XN
                with pe.Fori(0, 4) as b:
                    for c in range(2):
                        pe.wait_ge(unit_free, first + 2 * b + c + 1)
                        for k, wk in enumerate((w, W5[kind + "s"]) if rope else (w,)):
                            for kc in range(KC):
                                last = nc.tensor.matmul(ps[:, 2 * c + k, 0:n], wk[:, kc, 128 * c:128 * c + 128],
                                                        src[:, kc, bass.ds(b * n, n)],
                                                        start=(kc == 0), stop=(kc == KC - 1))
                        last.then_inc(unit_ready, 1)

            def norm_transposes(k):
                with pe.Fori(0, 4) as q:
                    for half in range(2):
                        pair = 2 * q + half
                        pe.wait_ge(xc_ready, NT * k + 2 * pair + 2)
                        pe.wait_ge(xn_ready, 8 * k + pair + 1)
                        for i in range(2):
                            for c in range(KC):
                                last = nc.tensor.transpose(
                                    ps[:, half, 256 * c + 128 * i:256 * c + 128 * i + 128],
                                    XC[2 * half + i][:, 128 * c:128 * c + 128], ident[:, :])
                        last.then_inc(xt_ready, 1)

            def row_piece(e, bank, what, c, kq):
                pe.wait_ge(row_taken, e + 1)
                if what in ("T", "TR"):
                    last = nc.tensor.transpose(ps[0:NPAIR, bank, 0:128], M16[:, :], ident[:, :])
                if what in ("R", "TR"):
                    for qt in range(QB // 128):
                        last = nc.tensor.matmul(ps[:, bank, 128 + HG * qt:128 + HG * qt + HG],
                                                U[:, 128 * qt:128 * qt + 128], pick[:, :], start=True, stop=True)
                elif what == "D":
                    for qt in range(QB // 128):
                        for h in range(HG):
                            last = nc.tensor.matmul(ps[32 * h:32 * h + 32, bank, 128 * qt:128 * qt + 128],
                                                    R16[:, qt, h:h + 1].to_broadcast([128, 32]), ident[:, :],
                                                    start=True, stop=True, tile_position=(0, 32 * h))
                elif what == "M":
                    pair, ch = divmod(c, len(MAXCOLS))
                    h, qt = divmod(pair, QB // 128)
                    off, w = MAXCOLS[ch]
                    head = kq * HG + h
                    last = nc.tensor.matmul(
                        ps[:, bank, 0:w],
                        QST[0:NSTACK, bass.ds(head, 1), 128 * qt:128 * qt + 128].rearrange("p a b -> p (a b)"),
                        KSTK[0:NSTACK, bass.ds(head, 1), off:off + w].rearrange("p a b -> p (a b)"),
                        start=True, stop=True)
                last.then_inc(row_ready, 1)

            def weigh(l, step, j, u):
                pe.wait_ge(exp_done, two + l * EXP_LAYER + 2 * step + 2)
                rows = KROWS[j]
                for h in range(HG):
                    last = nc.tensor.matmul(ps[32 * h:32 * h + 32, ACC, :], VG[u][0:rows, j, h, :],
                                            PR[p_slot(u, j, h // 2)][0:rows, h % 2, :],
                                            start=(j == 0), stop=(j == KT - 1), tile_position=(0, 32 * h))
                last.then_inc(pv_done, 1)

            def iteration(l, it, u, g, g2, kind, first, shift):
                pieces = row_pieces(kind)
                at = [0]

                def rows(n, j):
                    for k in range(at[0], min(at[0] + n, len(pieces))):
                        what, c = pieces[k]
                        if what != "M" and j < 1 or what == "D" and j < 2:
                            return
                        if what == "D":
                            pe.wait_ge(row_taken, three + first + (TR_AT if kind == "loop" else 0) + 1)
                        if what in ("TR", "R"):
                            pe.wait_ge(u_ready, one + l * (NIT + 1) + it + 1)
                        if what == "TR":
                            pe.wait_ge(m16_ready, l * NIT + it + 2)
                        if what == "M" and c == 0:
                            pe.wait_ge(q_loaded, 96 * (l * NIT + it + 3))
                        row_piece(first + k, row_bank(shift + k), what, c, g2)
                        at[0] = k + 1

                pe.wait_ge(nm_loaded, 48 * (l * NIT + it + 1))
                for j in range(KT):
                    step = KT * it + j
                    for half in range(2):
                        pe.wait_ge(exp_done, l * EXP_LAYER + 2 * step + half + 1)
                        for h in (2 * half, 2 * half + 1):
                            head = g * HG + h
                            last = nc.tensor.matmul(
                                ps[0:KROWS[j], h, :],
                                KSTK[:, bass.ds(head, 1), 128 * j:128 * j + KROWS[j]].rearrange("p a b -> p (a b)"),
                                QST[:, bass.ds(head, 1), :].rearrange("p a b -> p (a b)"),
                                start=True, stop=True)
                        last.then_inc(s_ready, 1)
                        rows(1, j)
                    if j > 0:
                        if j == 1:
                            pe.wait_ge(vg_ready, l * NIT + it + 1)
                            pe.wait_ge(u_ready, one + l * (NIT + 1) + it + 1)
                        weigh(l, step - 1, j - 1, u)
                    rows(3, j)
                rows(NCH, KT)
                weigh(l, KT * it + KT - 1, KT - 1, u)

            def attention(l):
                pe.wait_ge(k_loaded, 16 + 96 * (l + 1))
                e = 0
                pe.wait_ge(q_loaded, 96 * (l * NIT + 3))
                for n in range(2):
                    for c in range(NCH):
                        row_piece(l * ROWS_LAYER + e, row_bank(e), "M", c, n)
                        e += 1
                    if n == 0:
                        pe.wait_ge(m16_ready, l * NIT + 1)
                        row_piece(l * ROWS_LAYER + e, row_bank(e), "T", 0, 0)
                        e += 1
                first = l * ROWS_LAYER + ROWS_HEAD
                with pe.Fori(0, NIT // 2 - 1) as i:
                    for u in range(2):
                        it = 2 * i + u
                        iteration(l, it, u, it % 4, (it + 2) % 4, "loop", first + ROWS_LOOP * it, 0)
                first = first + ROWS_LOOP * (NIT - 2)
                iteration(l, NIT - 2, 0, 2, 0, "last but one", first, 0)
                iteration(l, NIT - 1, 1, 3, 0, "last", first + 2, 2)
                pe.wait_ge(u_ready, one + (l + 1) * (NIT + 1))
                row_piece(first + 4, row_bank(4), "R", 0, 0)
                pe.wait_ge(row_taken, three + first + 5)
                row_piece(first + 5, row_bank(5), "D", 0, 0)

            def output_projection(l):
                pe.wait_ge(rest_loaded, 16 * 9)
                pe.wait_ge(on_ready, one + (l + 1) * (NIT + 1))
                for t in range(NT):
                    if t >= 4:
                        pe.wait_ge(o_taken, NT * l + t - 3)
                    b, qt = divmod(t, 4)
                    for g in range(NG):
                        last = nc.tensor.matmul(ps[:, t % 4, 0:D], ON[:, NG * b + g, 128 * qt:128 * qt + 128],
                                                WO[:, l, g, :], start=(g == 0), stop=(g == NG - 1))
                    last.then_inc(o_ready, 1)

            def router_logits(l):
                pe.wait_ge(rest_loaded, 16 * 9)
                for t in range(NT):
                    if t % 2 == 0:
                        pe.wait_ge(xn_ready, two + 8 * (2 * l + 1) + t // 2 + 1)
                    for c in range(KC):
                        last = nc.tensor.matmul(ps[:, 2, NR * t:NR * t + NR], XN[:, c, 128 * t:128 * t + 128],
                                                router[:, l, c, :], start=(c == 0), stop=(c == KC - 1))
                last.then_inc(lg_ready, 1)

            def expert_output_bias():
                pe.wait_ge(pw_ready, 1)
                pe.wait_ge(y_free, y_slots + E0 * NT)
                for b in range(NB):
                    for i in range(4):
                        last = nc.tensor.transpose(ps[0:NR, 4 + b, 128 * i:128 * i + 128],
                                                   PW[:, 4 * b + i, 0:NR], ident[:, :])
                    last.then_inc(pt_ready, 1)
                for t in range(NT):
                    if t % 4 == 0:
                        pe.wait_ge(pt_copied, NB)
                    if t >= 4:
                        pe.wait_ge(yb_taken, t - 3)
                    nc.tensor.matmul(ps[:, 4 + t % 4, 0:D], PT[:, 128 * t:128 * t + 128], bout0[:, :],
                                     start=True, stop=True).then_inc(yb_ready, 1)

            def experts(m):
                hc, ne, l = m.hc, m.ne, m.l
                base_e = l * E0
                base_k = l * E0 * NB
                base_q = l * E0 * NB * HC0
                pe.wait_ge(xl_ready, 8 * (l + 1))
                pe.wait_ge(lg_read, l + 1)

                def three_passes(dst, lh, ll, rh, rl, first, final):
                    nc.tensor.matmul(dst, lh, rh, start=first, stop=False)
                    nc.tensor.matmul(dst, lh, rl, start=False, stop=False)
                    return nc.tensor.matmul(dst, ll, rh, start=False, stop=final)

                with pe.Fori(0, ne // 2) as pair:
                    for u in range(2):
                        e = 2 * pair + u
                        with pe.Fori(0, 2) as tp:
                            pe.wait_ge(wl_ready, two + base_e + e + 1)
                            for v in range(2):
                                tb = 2 * tp + v
                                for c in range(hc):
                                    q = base_q + (NB * e + tb) * hc + c
                                    pe.wait_ge(h_free, q + 1)
                                    for w in range(2 if m.gated else 1):
                                        for kc in range(KC):
                                            at = (w * KC + kc) * m.hid + 128 * c
                                            last = three_passes(
                                                ps[:, 2 * (c % 2) + w, :],
                                                m.WH[u][:, at:at + 128], m.WL[u][:, at:at + 128],
                                                XH[:, kc, bass.ds(QB * tb, QB)], XL[:, kc, bass.ds(QB * tb, QB)],
                                                kc == 0, kc == KC - 1)
                                    last.then_inc(h_ready, 1)
                            for v in range(2):
                                tb = 2 * tp + v
                                k = base_k + NB * e + tb
                                w2 = m.wcols - hc * D
                                pe.wait_ge(hl_ready, two + base_q + (NB * e + tb) * hc + hc)
                                for qt in range(4):
                                    pe.wait_ge(y_free, 4 * k + qt + 1)
                                    for c in range(hc):
                                        last = three_passes(
                                            ps[:, 4 + qt, 0:D],
                                            m.HH[v][:, c, 128 * qt:128 * qt + 128],
                                            m.HL[v][:, c, 128 * qt:128 * qt + 128],
                                            m.WH[u][:, w2 + D * c:w2 + D * c + D],
                                            m.WL[u][:, w2 + D * c:w2 + D * c + D],
                                            c == 0, c == hc - 1)
                                    last.then_inc(y_ready, 1)

            pe.wait_ge(const_loaded, 48)
            v_of_context()
            pe.wait_ge(wctx_loaded, 16 * 5)
            units("k1")
            pe.wait_ge(table_ready, 2)
            units("k0")
            norm_transposes(0)
            pe.wait_ge(xn_ready, two + 8)
            units("q0")
            attention(0)
            output_projection(0)
            norm_transposes(1)
            router_logits(0)
            experts(moe[0])
            expert_output_bias()
            norm_transposes(2)
            pe.wait_ge(xn_ready, two + 24)
            units("q1")
            attention(1)
            output_projection(1)
            norm_transposes(3)
            router_logits(1)
            experts(moe[1])

        @block.scalar
        def _(act):
            def evacuate_v(j, rows):
                act.wait_ge(v_ready, j + 1)
                for l in range(2):
                    nc.scalar.activation(V[l][0:rows, :, j, :],
                                         ps[0:rows, 4 + j % 2, D * l:D * l + D].rearrange("p (g n) -> p g n", g=NG),
                                         ACT.Copy).then_inc(v_taken, 1)

            def unit_parts(kind):
                first, _, n, _ = UNITS[kind]
                with act.Fori(0, 4) as b:
                    u0 = first + 2 * b
                    for c in range(2):
                        act.wait_ge(f_ready, u0 + c + 1)
                        act.wait_ge(parts_stored[c], 16 * (first // 2 + b + 1))
                        nc.scalar.activation(PARTS[c][:, 0, 0:n], F[c][:, 0:n], ACT.Copy).then_inc(part1_ready, 1)
                    for c in range(2):
                        act.wait_ge(rest1_ready, u0 + c + 1)
                        nc.scalar.activation(PARTS[c][:, 1, 0:n], G[c][:, 0:n], ACT.Copy).then_inc(part2_ready, 1)

            def norm_sd(k):
                act.wait_ge(var_ready, k + 1)
                nc.scalar.activation(norm[:, 3, :], norm[:, 2, :], ACT.Sqrt,
                                     bias=const[:, C_EPS:C_EPS + 1]).then_inc(sd_ready, 1)

            def norm_copies(k):
                before_experts = k % 2 == 1
                if before_experts:
                    act.wait_ge(o_ready, NT * (k + 1) // 2)
                with act.Fori(0, 4) as q:
                    for half in range(2):
                        pair = 2 * q + half
                        act.wait_ge(xt_ready, 8 * k + pair + 1)
                        act.wait_ge(sd_ready, k + 1)
                        source = ps[:, half, :].rearrange("p (c n) -> p c n", c=KC)
                        if before_experts:
                            nc.scalar.activation(XH[:, :, bass.ds(256 * pair, 256)], source, ACT.Copy)
                        nc.scalar.activation(XN[:, :, bass.ds(256 * pair, 256)], source,
                                             ACT.Copy).then_inc(xn_ready, 1)

            def exp_pair(l, it, j, half, u):
                step = KT * it + j
                rows = KROWS[j]
                act.wait_ge(s_ready, l * EXP_LAYER + 2 * step + half + 1)
                act.wait_ge(pv_done, l * PV_LAYER + step + 1)
                nc.scalar.activation(PR[p_slot(u, j, half)][0:rows, :, :],
                                     ps[0:rows, 2 * half:2 * half + 2, :], ACT.Exp,
                                     scale=DH ** -0.5).then_inc(exp_done, 1)

            def copy_sums(l, it):
                act.wait_ge(pv_done, two + l * PV_LAYER + KT * it)
                act.wait_ge(on_ready, one + l * (NIT + 1) + it)
                nc.scalar.activation(U[:, :], ps[:, ACC, :], ACT.Copy).then_inc(u_ready, 1)

            def attention(l):
                act.wait_ge(acc_set, l + 1)

                def iteration(it, u):
                    for j in range(KT):
                        for half in range(2):
                            exp_pair(l, it, j, half, u)
                        if j == 0:
                            copy_sums(l, it)

                with act.Fori(0, NIT // 2) as i:
                    for u in range(2):
                        iteration(2 * i + u, u)
                copy_sums(l, NIT)

            def router_exp(l):
                act.wait_ge(lg_moved, l + 1)
                nc.scalar.activation(PB[:, :, :], PB[:, :, :], ACT.Exp).then_inc(ex_ready, 1)

            def experts(m):
                hc, ne, l = m.hc, m.ne, m.l
                base_e, base_q, base_k = l * E0, l * E0 * NB * HC0, l * E0 * NB
                nload = 3
                base_w = l * nload * E0 // 2
                with act.Fori(0, ne // 2) as pair:
                    for u in range(2):
                        e = 2 * pair + u
                        act.wait_ge(w_loaded[u], 16 * (base_w + nload * (pair + 1)))
                        act.wait_ge(y_ready, y_start + NT * (base_e + e - 1))
                        if not m.gated:
                            nc.scalar.activation(BIN[u][:, :], BRAW[u][:, :], ACT.Copy)
                        nc.scalar.activation(m.WH[u][:, :], m.RAW[u][:, :], ACT.Copy).then_inc(wh_ready, 1)
                        act.wait_ge(wh_ready, base_e + e + 1)
                        with act.Fori(0, 2) as tp:
                            for v in range(2):
                                for c in range(hc):
                                    q = base_q + (NB * e + 2 * tp + v) * hc + c
                                    act.wait_ge(h_ready, q + 1)
                                    if m.gated:
                                        act.wait_ge(h_free, q + 1)
                                        nc.scalar.activation(m.SG[c % 2][:, :], ps[:, 2 * (c % 2), :],
                                                             ACT.Silu).then_inc(sg_ready, 1)
                                    else:
                                        act.wait_ge(hl_ready, q + 1)
                                        nc.scalar.activation(m.HF[c % 2][:, :], ps[:, 2 * (c % 2), :],
                                                             ACT.Gelu_apprx_tanh,
                                                             bias=BIN[u][:, c:c + 1]
                                                             ).then_inc(h_free, 1)

            for j, rows in enumerate(KROWS):
                evacuate_v(j, rows)
            unit_parts("k1")
            act.wait_ge(const_loaded, 48)
            act.wait_ge(angle_ready, 1)
            nc.scalar.activation(SIN[:, :], ANG[:, :], ACT.Sin, scale=const[:, C_SIGN:C_SIGN + 1]).then_inc(table_ready, 1)
            nc.scalar.activation(TURN[:, :], ANG[:, :], ACT.Abs).then_inc(act_done, 1)
            act.wait_ge(act_done, 1)
            nc.scalar.activation(COS[:, :], TURN[:, :], ACT.Sin, scale=-1.0,
                                 bias=const[:, C_HALFPI:C_HALFPI + 1]).then_inc(table_ready, 1)
            unit_parts("k0")
            norm_sd(0)
            norm_copies(0)
            unit_parts("q0")
            attention(0)
            norm_sd(1)
            norm_copies(1)
            router_exp(0)
            experts(moe[0])
            for b in range(NB):
                act.wait_ge(pt_ready, b + 1)
                nc.scalar.activation(PT[:, QB * b:QB * b + QB], ps[0:NR, 4 + b, :], ACT.Copy).then_inc(pt_copied, 1)
            norm_sd(2)
            norm_copies(2)
            unit_parts("q1")
            attention(1)
            norm_sd(3)
            norm_copies(3)
            router_exp(1)
            experts(moe[1])

        @block.gpsimd
        def _(pool):
            def unit_parts(kind):
                first, _, n, _ = UNITS[kind]
                with pool.Fori(0, 4) as b:
                    u0 = first + 2 * b
                    for c in range(2):
                        pool.wait_ge(part1_ready, u0 + c + 1)
                        nc.gpsimd.tensor_tensor(G[c][:, 0:n], F[c][:, 0:n], PARTS[c][:, 0, 0:n],
                                                ALU.subtract).then_inc(rest1_ready, 1)
                    for c in range(2):
                        pool.wait_ge(part2_ready, u0 + c + 1)
                        nc.gpsimd.tensor_tensor(PARTS[c][:, 2, 0:n], G[c][:, 0:n], PARTS[c][:, 1, 0:n],
                                                ALU.subtract).then_inc(part3_ready, 1)

            def stage_v(l, n, u, g):
                pool.wait_ge(ones_set, 3 * (l + 1))
                for rows, j0, j1 in ((128, 0, KT - 1), (KROWS[-1], KT - 1, KT)):
                    last = nc.gpsimd.tensor_copy(
                        VG[u][0:rows, j0:j1, :, 0:DH].rearrange("p j h d -> p (j h) d"),
                        V[l][0:rows, bass.ds(g, 1), j0:j1, :].rearrange("p g j (h d) -> p (g j h) d", d=DH))
                last.then_inc(vg_ready, 1)

            def cut_maxima(l, n, t_piece):
                pool.wait_ge(row_taken, three + t_piece + 1)
                pool.wait_ge(nm_loaded, 48 * (l * NIT + n))
                base = l * NIT * 3 + 3 * n
                nc.gpsimd.tensor_tensor(NM[:, 0, :], NMF[:, 0, :], ZERO[:, :], ALU.add).then_inc(cut_done, 1)
                pool.wait_ge(cut_done, base + 1)
                nc.gpsimd.tensor_tensor(NMF[:, 1, :], NMF[:, 0, :], NM[:, 0, :], ALU.subtract).then_inc(cut_done, 1)
                pool.wait_ge(cut_done, base + 2)
                nc.gpsimd.tensor_tensor(NM[:, 1, :], NMF[:, 1, :], ZERO[:, :], ALU.add).then_inc(cut_done, 1)
                pool.wait_ge(cut_done, base + 3)
                nc.gpsimd.tensor_tensor(NM[:, 2, :], NMF[:, 1, :], NM[:, 1, :], ALU.subtract).then_inc(nm_ready, 1)

            def attention(l):
                nc.gpsimd.memset(ZERO[:, :], 0.0).then_inc(ones_set, 1)
                for u in range(2):
                    nc.gpsimd.memset(VG[u][:, :, :, DH:32], 1.0).then_inc(ones_set, 1)
                stage_v(l, 0, 0, 0)
                first = l * ROWS_LAYER
                cut_maxima(l, 0, first + NCH)
                first = first + ROWS_HEAD
                with pool.Fori(0, NIT // 2 - 1) as i:
                    for u in range(2):
                        it = 2 * i + u
                        pool.wait_ge(pv_done, two + l * PV_LAYER + KT * it)
                        stage_v(l, it + 1, 1 - u, (it + 1) % 4)
                        cut_maxima(l, it + 1, first + ROWS_LOOP * it + TR_AT)
                first = first + ROWS_LOOP * (NIT - 2)
                pool.wait_ge(pv_done, two + l * PV_LAYER + KT * (NIT - 2))
                stage_v(l, NIT - 1, 1, 3)
                cut_maxima(l, NIT - 1, first)

            def split_tokens(l):
                for pair in range(8):
                    pool.wait_ge(xn_ready, two + 8 * (2 * l + 1) + pair + 1)
                    cols = slice(256 * pair, 256 * pair + 256)
                    nc.gpsimd.tensor_tensor(XL[:, :, cols], XN[:, :, cols], XH[:, :, cols].bitcast(f32),
                                            ALU.subtract).then_inc(xl_ready, 1)

            def experts(m):
                hc, ne, l = m.hc, m.ne, m.l
                base_e, base_q, base_k = l * E0, l * E0 * NB * HC0, l * E0 * NB
                with pool.Fori(0, ne // 2) as pair:
                    for u in range(2):
                        e = 2 * pair + u
                        pool.wait_ge(wh_ready, base_e + e + 1)
                        nc.gpsimd.tensor_tensor(m.WL[u][:, :], m.RAW[u][:, :], m.WH[u][:, :].bitcast(f32),
                                                ALU.subtract).then_inc(wl_ready, 1)
                        with pool.Fori(0, 2) as tp:
                            for v in range(2):
                                for c in range(hc):
                                    q = base_q + (NB * e + 2 * tp + v) * hc + c
                                    pool.wait_ge(hh_ready, q + 1)
                                    nc.gpsimd.tensor_tensor(m.HL[v][:, c, :], m.HF[c % 2][:, :],
                                                            m.HH[v][:, c, :].bitcast(f32),
                                                            ALU.subtract).then_inc(hl_ready, 1)

            unit_parts("k1")
            unit_parts("k0")
            unit_parts("q0")
            attention(0)
            split_tokens(0)
            experts(moe[0])
            unit_parts("q1")
            attention(1)
            split_tokens(1)
            experts(moe[1])

        @block.vector
        def _(dve):
            order = Order(dve, dve_done)

            def ordered(ins):
                order.then(ins)
                order.wait()

            def angles():
                dve.wait_ge(pos_loaded, 16)
                dve.wait_ge(const_loaded, 48)
                ordered(nc.vector.tensor_copy(ANG[:, :], POS[:, :]))
                ordered(nc.vector.tensor_scalar(ANG[:, :], ANG[:, :], const[:, C_FREQ:C_FREQ + 1], None, ALU.mult))
                ordered(nc.vector.tensor_scalar(TURN[:, :], ANG[:, :], float(0.5 / np.pi), ROUND, ALU.mult, ALU.add))
                ordered(nc.vector.tensor_scalar(TURN[:, :], TURN[:, :], ROUND, None, ALU.subtract))
                for part in TWO_PI_PARTS:
                    ordered(nc.vector.scalar_tensor_tensor(ANG[:, :], TURN[:, :], -part, ANG[:, :], ALU.mult, ALU.add))
                nc.vector.tensor_scalar(ANG[:, :], ANG[:, :], PI_BELOW, -PI_BELOW, ALU.min,
                                        ALU.max).then_inc(angle_ready, 1)

            def units(kind):
                first, rope, n, _ = UNITS[kind]
                col = T if kind[0] == "k" else 0
                with dve.Fori(0, 4) as b:
                    for c in range(2):
                        u = first + 2 * b + c
                        dve.wait_ge(unit_ready, u + 1)
                        dve.wait_ge(part3_ready, u + 1)
                        if rope:
                            nc.vector.tensor_tensor(F[c][:, 0:n], ps[:, 2 * c, 0:n],
                                                    COS[:, bass.ds(b * n + col, n)], ALU.mult)
                            nc.vector.tensor_tensor(G[c][:, 0:n], ps[:, 2 * c + 1, 0:n],
                                                    SIN[:, bass.ds(b * n + col, n)], ALU.mult).then_inc(unit_free, 1)
                            dve.wait_ge(unit_free, two + u + 1)
                            nc.vector.tensor_tensor(F[c][:, 0:n], F[c][:, 0:n], G[c][:, 0:n],
                                                    ALU.add).then_inc(f_ready, 1)
                        else:
                            nc.vector.tensor_copy(F[c][:, 0:n], ps[:, 2 * c, 0:n]).then_inc(f_ready, 1)
                            dve.wait_ge(f_ready, u + 1)
                            nc.vector.memset(scrap[:, 30 + c:31 + c], 0.0).then_inc(unit_free, 1)

            def norm_variance():
                half = D // 2
                ordered(nc.vector.tensor_tensor(norm[:, 0, :], stats[:, :, 1], stats[:, :, 4], ALU.add))
                ordered(nc.vector.tensor_scalar(norm[:, 0, :], norm[:, 0, :], 0.5, None, ALU.mult))
                ordered(nc.vector.tensor_tensor(norm[:, 1, :], stats[:, :, 1], stats[:, :, 4], ALU.subtract))
                ordered(nc.vector.tensor_tensor(norm[:, 1, :], norm[:, 1, :], norm[:, 1, :], ALU.mult))
                ordered(nc.vector.tensor_scalar(norm[:, 1, :], norm[:, 1, :], 0.25, None, ALU.mult))
                ordered(nc.vector.tensor_tensor(norm[:, 2, :], stats[:, :, 2], stats[:, :, 5], ALU.add))
                nc.vector.scalar_tensor_tensor(norm[:, 2, :], norm[:, 2, :], 1.0 / D, norm[:, 1, :], ALU.mult,
                                               ALU.add).then_inc(var_ready, 1)

            def norm_apply(k):
                dve.wait_ge(sd_ready, k + 1)
                ordered(nc.vector.reciprocal(norm[:, 4, :], norm[:, 3, :]))
                with dve.Fori(0, 4) as q:
                    for i in range(4):
                        t = 4 * q + i
                        if i % 2 == 0:
                            dve.wait_ge(xn_ready, 8 * k + 2 * q + i // 2 + 1)
                        nc.vector.tensor_scalar(XC[i][:, :], X[:, bass.ds(t, 1), :].rearrange("p a d -> p (a d)"),
                                                norm[:, 0, bass.ds(t, 1)],
                                                norm[:, 4, bass.ds(t, 1)], ALU.subtract, ALU.mult
                                                ).then_inc(xc_ready, 1)

            def tile_stats(t):
                nc.vector.bn_stats(stats[:, t, :], X[:, t, :]).then_inc(stats_done, 1)

            def row_piece(l, it, e, bank, what, c):
                dve.wait_ge(row_ready, e + 1)
                if what == "M":
                    pair, ch = divmod(c, len(MAXCOLS))
                    nc.vector.reduce_max(MXC[:, pair, ch:ch + 1], ps[:, bank, 0:MAXCOLS[ch][1]],
                                         AX.X).then_inc(row_taken, 1)
                elif what == "D":
                    nc.vector.tensor_tensor(ON[:, bass.ds((it + NIT - 1) % NIT, 1), :].rearrange("p a b -> p (a b)"),
                                            U[:, :], ps[:, bank, :], ALU.mult).then_inc(row_taken, 1)
                else:
                    if "T" in what:
                        dve.wait_ge(nm_ready, l * NIT + it + 1)
                        last = nc.vector.tensor_scalar(NMF[:, 0, :], ps[0:NPAIR, bank, 0:128], -1.0, None, ALU.mult)
                    if "R" in what:
                        last = nc.vector.reciprocal(R16[:, :, :].rearrange("p q h -> p (q h)"),
                                                    ps[:, bank, 128:128 + NPAIR])
                    last.then_inc(row_taken, 1)

            def output_written(l, it, d_piece):
                dve.wait_ge(row_taken, three + d_piece + 1)
                nc.vector.memset(scrap[:, 29:30], 0.0).then_inc(on_ready, 1)

            def row_maxima(e_last):
                dve.wait_ge(row_taken, three + e_last + 1)
                nc.vector.tensor_reduce(M16[:, :], MXC[:, :, :], AX.X, ALU.max).then_inc(m16_ready, 1)

            def attention(l):
                nc.vector.memset(ps[:, ACC, :], 1.0).then_inc(acc_set, 1)
                first = l * ROWS_LAYER
                for c in range(NCH):
                    row_piece(l, 0, first + c, row_bank(c), "M", c)
                row_maxima(first + NCH - 1)
                e = NCH
                row_piece(l, -1, first + e, row_bank(e), "T", 0)
                for c in range(NCH):
                    row_piece(l, 0, first + e + 1 + c, row_bank(e + 1 + c), "M", c)
                row_maxima(first + ROWS_HEAD - 1)

                def iteration(it, first, kind, shift):
                    pieces = row_pieces(kind)
                    d_at = pieces.index(("D", 0))
                    for k, (what, c) in enumerate(pieces):
                        if k == 0 and kind == "loop":
                            dve.wait_ge(m16_ready, l * NIT + it + 2)
                        row_piece(l, it, first + k, row_bank(shift + k), what, c)
                        if k == min(d_at + 1, len(pieces) - 1):
                            output_written(l, it, first + d_at)
                    if kind == "loop":
                        row_maxima(first + len(pieces) - 1)

                first = first + ROWS_HEAD
                with dve.Fori(0, NIT // 2 - 1) as i:
                    for u in range(2):
                        it = 2 * i + u
                        iteration(it, first + ROWS_LOOP * it, "loop", 0)
                first = first + ROWS_LOOP * (NIT - 2)
                iteration(NIT - 2, first, "last but one", 0)
                iteration(NIT - 1, first + 2, "last", 2)
                iteration(NIT, first + 4, "last", 4)

            def add_to_residual(ready, before, bank0, taken):
                for t in range(NT):
                    dve.wait_ge(ready, before + t + 1)
                    nc.vector.tensor_tensor(X[:, t, :], ps[:, bank0 + t % 4, 0:D], X[:, t, :], ALU.add).then_inc(taken, 1)
                    if t > 0:
                        dve.wait_ge(taken, before + t)
                        tile_stats(t - 1)
                dve.wait_ge(taken, before + NT)
                tile_stats(NT - 1)

            def wide(a):
                return a[:, :].unsqueeze(2).to_broadcast([128, NT, NR])

            def first_greatest(values, greatest, chosen):
                ordered(nc.vector.tensor_reduce(greatest[:, :], values[:, :, :], AX.X, ALU.max))
                ordered(nc.vector.tensor_tensor(TK[0][:, :, :], values[:, :, :], wide(greatest), ALU.is_equal))
                ordered(nc.vector.tensor_tensor(TK[0][:, :, :], TK[0][:, :, :], prio[:, :, :], ALU.mult))
                ordered(nc.vector.tensor_reduce(MK[:, :], TK[0][:, :, :], AX.X, ALU.max))
                ordered(nc.vector.tensor_tensor(chosen[:, :, :], TK[0][:, :, :], wide(MK), ALU.is_equal))

            def route_start(l):
                dve.wait_ge(rest_loaded, 16 * 9)
                dve.wait_ge(lg_ready, l + 1)
                logits = ps[:, 2, 0:NT * NR].rearrange("p (t e) -> p t e", e=NR)
                if l == 0:
                    nc.vector.tensor_copy(LG[:, :, :], logits).then_inc(lg_read, 1)
                else:
                    nc.vector.tensor_tensor(LG[:, :, :], logits, rbias[:, :].unsqueeze(1).to_broadcast([128, NT, NR]),
                                            ALU.add).then_inc(lg_read, 1)
                dve.wait_ge(lg_read, l + 1)
                ordered(nc.vector.tensor_reduce(M1[:, :], LG[:, :, :], AX.X, ALU.max))
                nc.vector.tensor_tensor(PB[:, :, :], LG[:, :, :], wide(M1), ALU.subtract).then_inc(lg_moved, 1)

            def share(values):
                ordered(nc.vector.tensor_reduce(M2[:, :], values[:, :, :], AX.X, ALU.add))
                ordered(nc.vector.reciprocal(M2[:, :], M2[:, :]))
                ordered(nc.vector.tensor_tensor(values[:, :, :], values[:, :, :], wide(M2), ALU.mult))

            def route_first(l):
                dve.wait_ge(ex_ready, l + 1)
                if l == 0:
                    share(PB)
                first_greatest((PB, LG)[l], M1, ONE1)

            def route_second(l):
                ordered(nc.vector.scalar_tensor_tensor(TK[1][:, :, :], ONE1[:, :, :], -3e38, (PB, LG)[l][:, :, :],
                                                       ALU.mult, ALU.add))
                first_greatest(TK[1], M2, ONE2)

            def route_weights(l):
                ordered(nc.vector.tensor_tensor(ONE1[:, :, :], ONE1[:, :, :], ONE2[:, :, :], ALU.add))
                ordered(nc.vector.tensor_tensor(PB[:, :, :], ONE1[:, :, :], PB[:, :, :], ALU.mult))
                if l == 1:
                    share(PB)
                    ordered(nc.vector.memset(PW[:, :, NR:E1], 1.0))
                nc.vector.tensor_copy(PW[:, :, 0:NR], PB[:, :, :]).then_inc(pw_ready, 1)
                dve.wait_ge(pw_ready, l + 1)

            def experts(m):
                hc, ne, l = m.hc, m.ne, m.l
                base_q, base_k = l * E0 * NB * HC0, l * E0 * NB

                def blocks(e, tp, after_hidden={}):
                    for v in range(2):
                        k = base_k + NB * e + 2 * tp + v
                        dve.wait_ge(y_ready, 4 * k + y_start - 4)
                        for c in range(hc):
                            q = base_q + (NB * e + 2 * tp + v) * hc + c
                            if m.gated:
                                dve.wait_ge(sg_ready, q - base_q + 1)
                                dve.wait_ge(hl_ready, q + 1)
                                nc.vector.tensor_tensor(m.HF[c % 2][:, :], m.SG[c % 2][:, :],
                                                        ps[:, 2 * (c % 2) + 1, :], ALU.mult).then_inc(h_free, 1)
                            dve.wait_ge(h_free, two + q + 1)
                            nc.vector.tensor_copy(m.HH[v][:, c, :], m.HF[c % 2][:, :]).then_inc(hh_ready, 1)
                            if hc * v + c in after_hidden:
                                after_hidden[hc * v + c](l)
                    for v in range(2):
                        k = base_k + NB * e + 2 * tp + v
                        for qt in range(4):
                            t = 4 * (2 * tp + v) + qt
                            dve.wait_ge(y_ready, y_start + 4 * k + qt + 1)
                            dve.wait_ge(y_free, y_slots + 4 * k + qt)
                            nc.vector.scalar_tensor_tensor(
                                X[:, bass.ds(t, 1), :].rearrange("p a d -> p (a d)"), ps[:, 4 + qt, 0:D],
                                PW[:, bass.ds(t, 1), bass.ds(e, 1)].rearrange("p a b -> p (a b)"),
                                X[:, bass.ds(t, 1), :].rearrange("p a d -> p (a d)"),
                                ALU.mult, ALU.add).then_inc(y_free, 1)

                blocks(0, 0, {0: route_first, 1: route_second, 2: route_weights})
                blocks(0, 1)
                with dve.Fori(0, 2) as tp:
                    blocks(1, tp)
                with dve.Fori(1, ne // 2) as pair:
                    for u in range(2):
                        with dve.Fori(0, 2) as tp:
                            blocks(2 * pair + u, tp)

            for col, (s, n) in enumerate(((unit_free, two), (part3_ready, two), (parts_stored[0], store_start), (parts_stored[1], store_start), (xn_ready, two),
                         (row_taken, three), (exp_done, two), (pv_done, two), (wl_ready, two), (h_free, two),
                         (hl_ready, two), (y_ready, y_start), (y_free, y_slots), (u_ready, one),
                                           (on_ready, one))):
                nc.vector.memset(scrap[:, col:col + 1], 0.0).then_inc(s, n)
            angles()
            units("k1")
            dve.wait_ge(x_loaded, 16)
            for t in range(NT):
                tile_stats(t)
            dve.wait_ge(stats_done, NT)
            norm_variance()
            dve.wait_ge(table_ready, 2)
            units("k0")
            norm_apply(0)
            dve.wait_ge(xc_ready, NT)
            dve.wait_ge(rest_loaded, 16 * 9)
            ordered(nc.vector.tensor_tensor(X[:, :, :], X[:, :, :],
                                            bo0[:, :].unsqueeze(1).to_broadcast([128, NT, D]), ALU.add))
            units("q0")
            attention(0)
            add_to_residual(o_ready, 0, 0, o_taken)
            dve.wait_ge(stats_done, 2 * NT)
            norm_variance()
            norm_apply(1)
            route_start(0)
            experts(moe[0])
            dve.wait_ge(y_free, y_slots + E0 * NT)
            add_to_residual(yb_ready, 0, 4, yb_taken)
            dve.wait_ge(stats_done, 3 * NT)
            norm_variance()
            norm_apply(2)
            units("q1")
            attention(1)
            add_to_residual(o_ready, NT, 0, o_taken)
            dve.wait_ge(stats_done, 4 * NT)
            norm_variance()
            norm_apply(3)
            route_start(1)
            experts(moe[1])


def _rows_swapped(w):
    return w.reshape(D // 2, 2, D)[:, ::-1].reshape(D, D)


def _heads_apart(wo):
    w = np.zeros((NG, HG, 32, D), wo.dtype)
    w[:, :, :DH] = wo.T.reshape(NG, HG, DH, D)
    return np.ascontiguousarray(w.reshape(NG, HG * 32, D).transpose(1, 0, 2))


def _laid_out(i):
    t = np.ascontiguousarray
    freq = np.float32(100.0) ** (-np.arange(0, DH, 2, dtype=np.float32) / np.float32(DH))
    const = np.zeros((128, 8), np.float32)
    const[:, C_FREQ] = np.tile(np.repeat(freq, 2), 128 // DH)
    const[:, C_SIGN] = np.tile([-1.0, 1.0], 64)
    const[:, C_HALFPI] = np.pi / 2
    const[:, C_EPS] = EPS
    pick = np.zeros((128, HG), np.float32)
    for h in range(HG):
        pick[32 * h + DH, h] = 1.0
    pos = np.zeros((1, NPOS), np.int32)
    pos[0, :T] = i["itok_BxS_3_4095"][0]
    pos[0, T:T + S] = i["itok_BxS2_0_4095"][0]
    ctx = np.zeros((D, SP), np.float32)
    ctx[:, :S] = i["ctx_1024"][0].T
    joined = lambda a, b: np.concatenate([i[a], i[b]], 0)
    a = {
        "x": i["x"][0], "pos": pos, "ctxT": ctx, "const": const, "ident": np.eye(128, dtype=np.float32),
        "pick": pick, "ones": np.ones((3, H, S), np.dtype("bfloat16")),
        "q0": i["L0_xattn_Wq"].T, "q0s": _rows_swapped(i["L0_xattn_Wq"]).T,
        "k0": i["L0_xattn_Wk"].T, "k0s": _rows_swapped(i["L0_xattn_Wk"]).T,
        "k1": i["L1_xattn_w_k"].T, "q1": i["L1_xattn_w_q"].T,
        "wv": np.concatenate([i["L0_xattn_Wv"].T, i["L1_xattn_w_v"].T], 1),
        "wo0": _heads_apart(i["L0_xattn_Wo"]), "wo1": _heads_apart(i["L1_xattn_w_o"]),
        "bo0": i["L0_xattn_bo"].reshape(1, D),
        "router0": i["L0_ffn_router_w"], "router1": i["L1_ffn_router_w"].T,
        "rbias": i["L1_ffn_expert_bias"].reshape(1, NR),
        "prio": np.tile(np.arange(NR, 0, -1, dtype=np.float32), (128, NT, 1)),
        "w_in": i["L0_ffn_w_in"], "w_out": i["L0_ffn_w_out"], "bout0": i["L0_ffn_b_out"],
        "bin0": i["L0_ffn_b_in"].reshape(E0, HC0, 128).transpose(0, 2, 1),
        "w1": joined("L1_ffn_w1", "L1_ffn_sw1").transpose(0, 2, 1),
        "w3": joined("L1_ffn_w3", "L1_ffn_sw3").transpose(0, 2, 1),
        "w2": joined("L1_ffn_w2", "L1_ffn_sw2").transpose(0, 2, 1),
    }
    return {n: t(v) for n, v in a.items()}


def kernel(**inputs):
    import concourse.bacc as _bacc
    from concourse.bass_utils import run_bass_kernel_spmd as _run

    nc = _bacc.Bacc("TRN2", target_bir_lowering=False, num_devices=1)
    arrays = _laid_out({n: np.asarray(v) for n, v in inputs.items()})
    dram = {n: nc.dram_tensor(f"in_{n}", a.shape, mybir.dt.from_np(a.dtype), kind="ExternalInput").ap()
            for n, a in arrays.items()}
    out = nc.dram_tensor("out", (T, D), mybir.dt.float32, kind="ExternalOutput").ap()
    build(nc, dram, out)
    r = _run(nc, [{f"in_{n}": a for n, a in arrays.items()}], core_ids=[0])
    return r.results[0]["out"].reshape(1, T, D)
```

```python
from contextlib import ExitStack

import concourse.bass as bass
import numpy as np
from concourse import mybir

T, D, S, H, DH = 2048, 256, 1601, 16, 16
NT = T // 128
KC = D // 128
NB, QB = 4, 512
NG, HG = 4, 4
NIT = NB * NG
KT = -(-S // 128)
KROWS = [min(128, S - 128 * j) for j in range(KT)]
SC = 401
SP = 4 * SC
MAXCOLS = [(0, 401), (401, 400), (801, 400), (1201, 400)]
WIDE_STEP, WIDE = 400, 401
PRODUCTS = [(0, 0), (0, 1), (0, 2), (1, 0), (1, 1), (2, 0)]
NSTACK = 16 * len(PRODUCTS)
NPAIR = HG * (QB // 128)
NCH = NPAIR * len(MAXCOLS)
NPOS = T + SP
CTX_FIRST = 4 * 128
V_BANKS = 4
E0, HC0 = 8, 2
E1, HC1 = 8, 4
NSH = 2
VT = 256
SHB = T // VT
NV = (2 * T + E1 * (VT - 1)) // VT
SLOTS = NV * VT
WCOLS = 2 * KC * 128 * HC1 + HC1 * D
NR = 8
EPS = 1e-5
ROUND = 12582912.0
PI_BELOW = 3.1415925
TWO_PI_PARTS = (6.28125, 0.0019350051879882812, 3.0199159819e-07)

C_FREQ, C_HALFPI, C_EPS, C_EVEN, C_ODD = range(5)


def build(nc, dram, out):
    f32, bf16, f32r, i32, u32 = (mybir.dt.float32, mybir.dt.bfloat16, mybir.dt.float32r, mybir.dt.int32,
                                 mybir.dt.uint32)
    ALU, ACT, AX = mybir.AluOpType, mybir.ActivationFunctionType, mybir.AxisListType

    start, limit = -(-nc.sbuf_base // 32) * 32, nc.sbuf_usable_end

    def place(offset, name, shape, dt):
        return nc.alloc_sbuf_tensor_at(name, shape, dt, offset=offset)

    class Region:
        def __init__(self, start):
            self.at = start

        def take(self, name, shape, dt):
            size = int(np.prod(shape[1:])) * (2 if dt == bf16 else 4)
            t = place(self.at, name, shape, dt)
            self.at += -(-size // 32) * 32
            assert self.at <= limit, (name, self.at)
            return t

    keep = Region(start)
    X = keep.take("X", [128, NT, D], f32)
    xn_at = keep.at
    XN = keep.take("XN", [128, KC, T], f32)
    ident = keep.take("ident", [128, 128], f32)
    pick = keep.take("pick", [128, 2, HG], f32)
    const = keep.take("const", [128, 8], f32)
    stats_at = keep.at
    stats = keep.take("stats", [128, NT, 6], f32)
    norm = keep.take("norm", [128, 6, NT], f32)
    wo_at = keep.at
    WO = keep.take("WO", [128, 2, NG // 2, D], f32)
    W5 = {n: keep.take(f"W_{n}", [128, KC, D], f32) for n in ("k1", "q0")}
    WQ1 = keep.take("WQ1", [128, KC, D], f32)
    router_at = keep.at
    router = keep.take("router", [128, 2, KC, NR], f32)
    rbias = keep.take("rbias", [128, NR], f32)
    PW = keep.take("PW", [128, NT, NR], f32)
    prio = keep.take("prio", [128, NT, NR], f32)
    BRAW = [keep.take(f"BRAW{u}", [128, HC0], f32) for u in range(2)]
    BIN = [keep.take(f"BIN{u}", [128, HC0], f32) for u in range(2)]
    bout0 = keep.take("bout0", [NR, D], f32)
    bo0_at = keep.at
    bo0 = keep.take("bo0", [128, D], f32)
    scrap = keep.take("scrap", [1, 32], f32)
    kregion = keep.at
    KSTK = keep.take("KSTK", [NSTACK + 3, H, S], bf16)
    vregion = keep.at
    V = [keep.take(f"V{l}", [128, NG, KT, HG * DH], f32) for l in range(2)]
    gregion = keep.at
    VG = [keep.take(f"VG{u}", [128, KT, HG, 32], f32) for u in range(2)]
    rregion = keep.at

    r = Region(kregion)
    ANG = r.take("ANG", [128, NPOS], f32)
    TURN = r.take("TURN", [128, NPOS], f32)
    POS = place(kregion + -(-4 * NPOS // 32) * 32, "POS", [128, NPOS], i32)
    CTX = place(gregion, "CTX", [128, KC, SP], f32)
    r = Region(rregion)
    W5["k0"] = r.take("W_k0", [128, KC, D], f32)
    WV = r.take("WV", [128, KC, 2 * D], f32)
    XC0 = [r.take(f"XC0{i}", [128, D], f32) for i in range(8)]
    r = Region(rregion + 2 * HG * NG * QB)
    COS = r.take("COS", [128, NPOS], f32)
    SIN = r.take("SIN", [128, NPOS], f32)
    F = [[r.take(f"F0{c}", [128, QB], f32) for c in range(2)],
         [place(rregion + (2 * NG - 2 + c) * 4 * QB, f"F1{c}", [128, QB], f32) for c in range(2)]]
    G = [r.take(f"G{c}", [128, QB], f32) for c in range(2)]
    PARTS = [[r.take(f"PARTS{v}{c}", [128, 3, QB], bf16) for c in range(2)] for v in range(2)]
    TMP = [r.take(f"TMP{c}", [128, QB], f32) for c in range(2)]
    XC = [place((gregion if i < 4 else rregion + 2 * 4 * KC * T) + 1024 * i, f"XC{i}", [128, D], f32)
          for i in range(8)]
    XCK = [XC0, XC, XC]

    r = Region(rregion)
    QST = r.take("QST", [NSTACK + 3, H, QB], bf16)
    PR = [r.take(f"PR{n}", [128, 2, QB], f32) for n in range(4)]
    ON = r.take("ON", [128, NIT // 2, QB], f32)
    ODD = r.take("ODD", [128, QB], f32)
    r.at += 4 * QB * (NIT // 2)
    U = r.take("U", [128, QB], f32)
    R16 = r.take("R16", [128, QB // 128, HG], f32)
    NM = r.take("NM", [NPAIR, 3, 128], bf16)
    NMF = r.take("NMF", [NPAIR, 2, 128], f32)
    ZERO = r.take("ZERO", [NPAIR, 128], f32)
    MXC = r.take("MXC", [128, NPAIR, len(MAXCOLS)], f32)
    M16 = r.take("M16", [128, NPAIR], f32)

    r = Region(rregion)
    XH = r.take("XH", [128, KC, T], f32r)
    XL = r.take("XL", [128, KC, T], f32r)
    moe_at = r.at

    def topk_buffers(name, topk):
        wide = [topk.take(name + n, [128, NT, NR], f32) for n in ("LG", "PB", "TK0", "TK1", "ONE1", "ONE2")]
        return wide + [topk.take(name + n, [128, NT], f32) for n in ("M1", "M2", "MK")]

    PT = place(moe_at, "PT", [NR, T], f32)

    HID0, WCOLS0 = 128 * HC0, KC * 128 * HC0 + HC0 * D
    topk0 = topk_buffers("l0_", Region(gregion))
    r = Region(moe_at)
    HH = [r.take(f"HH{u}", [128, HC0, QB], f32r) for u in range(2)]
    HL = [r.take(f"HL{u}", [128, HC0, QB], f32r) for u in range(2)]
    WH = [r.take(f"WH{u}", [128, WCOLS0], f32r) for u in range(2)]
    WL = [r.take(f"WL{u}", [128, WCOLS0], f32r) for u in range(2)]
    HF = [r.take(f"HF{u}", [128, QB], f32) for u in range(2)]
    raw = Region(gregion + 5120)
    RAW = [raw.take(f"RAW{u}", [128, WCOLS0], f32) for u in range(2)]

    r = Region(kregion)
    RES = r.take("RES", [128, E1, WCOLS], f32)
    VWH = [r.take(f"VWH{u}", [128, WCOLS], f32r) for u in range(2)]
    VWL = [r.take(f"VWL{u}", [128, WCOLS], f32r) for u in range(2)]
    VHH = [r.take(f"VHH{u}", [128, HC1, VT], f32r) for u in range(2)]
    VHL = [r.take(f"VHL{u}", [128, HC1, VT], f32r) for u in range(2)]
    VHF = [r.take("VHF0", [128, VT], f32), place(bo0_at, "VHF1", [128, VT], f32)]
    late = kregion + 4 * 4 * WCOLS
    r = Region(late)
    XR = r.take("XR", [128, NT, D], f32)
    topk1 = topk_buffers("l1_", r)
    LG, PB, TK0, TK1, ONE1, ONE2, M1, M2, MK = zip(topk0, topk1)
    TRI = r.take("TRI", [128, 128], f32)
    ONES = r.take("ONES", [128, 128], f32)
    POSN = r.take("POSN", [128, NT, NR], f32)
    SCAN = [r.take(f"SCAN{i}", [128, NT, NR], f32) for i in range(2)]
    VISITS = [r.take(f"VISITS{i}", [128, NR], f32) for i in range(4)]
    assert r.at <= late + 2 * 4 * WCOLS
    SRAW = [place(late + (2 + i) * 4 * WCOLS, f"SRAW{i}", [128, WCOLS], f32) for i in range(NSH)]
    r = Region(wo_at)
    VXH = [r.take(f"VXH{u}", [128, KC, VT], f32r) for u in range(2)]
    VXL = [r.take(f"VXL{u}", [128, KC, VT], f32r) for u in range(2)]
    SG = [r.take(f"SG{u}", [128, VT], f32) for u in range(2)]
    assert r.at <= router_at
    r = Region(xn_at)
    XROWS = [r.take(f"XROWS{u}", [128, 2, D], f32) for u in range(2)]
    YROWS = [r.take(f"YROWS{u}", [128, 2, D], f32) for u in range(2)]
    YG = place(kregion, "YG", [128, NT, 2, D], f32)
    r = Region(stats_at)
    VNUM = r.take("VNUM", [1, NV], f32)
    SLOT = [r.take(f"SLOT{i}", [128, NT], u32) for i in range(2)]
    SHARE = [r.take(f"SHARE{i}", [128, NT], f32) for i in range(2)]
    EXPERT = r.take("EXPERT", [1, NV], i32)
    VEXP = r.take("VEXP", [1, NV], f32)
    assert r.at <= stats_at + 2 * 4 * 6 * NT

    ctx = ExitStack()
    with ctx:
        ps = ctx.enter_context(nc.psum_tensor("ps", [128, 8, 512], f32))

        def sem(name):
            return ctx.enter_context(nc.semaphore(name))

        kd = [nc.dram_tensor(f"k_parts{l}", [3, D, SP], bf16).ap() for l in range(2)]
        xs = nc.dram_tensor("x_by_slot", [SLOTS, D], f32).ap()
        ys = nc.dram_tensor("y_by_slot", [SLOTS, D], f32).ap()
        qd = [nc.dram_tensor(f"q_parts{l}", [3, D, T], bf16).ap() for l in range(2)]

        pos_loaded = [sem("pos_loaded_k"), sem("pos_loaded_q")]
        ctx_loaded = [sem("ctx_loaded_first"), sem("ctx_loaded_rest")]
        const_loaded, wctx_loaded, x_loaded, rest_loaded = (
            sem("const_loaded"), sem("wctx_loaded"), sem("x_loaded"), sem("rest_loaded"))
        dve_done, act_done = sem("dve_done"), sem("act_done")
        angle_ready, table_ready = sem("angle_ready"), sem("table_ready")
        v_ready, v_taken = sem("v_ready"), sem("v_taken")
        unit_ready, unit_free, f_ready = sem("unit_ready"), sem("unit_free"), sem("f_ready")
        part1_ready, rest1_ready, part2_ready, part3_ready = (
            sem("part1_ready"), sem("rest1_ready"), sem("part2_ready"), sem("part3_ready"))
        parts_stored = [[sem(f"parts_stored{v}{c}") for c in range(2)] for v in range(2)]
        stats_done = sem("stats_done")
        var_ready, sd_ready, xc_ready, xt_ready, xn_ready = (
            sem("var_ready"), sem("sd_ready"), sem("xc_ready"), sem("xt_ready"), sem("xn_ready"))
        k_first, q_first = sem("k_first"), sem("q_first")
        k_loaded, q_loaded, nm_loaded = sem("k_loaded"), sem("q_loaded"), sem("nm_loaded")
        row_ready, row_taken, m16_ready, cut_done, nm_ready, ones_set = (
            sem("row_ready"), sem("row_taken"), sem("m16_ready"), sem("cut_done"), sem("nm_ready"),
            sem("ones_set"))
        odd_added = sem("odd_added")
        s_ready, exp_done, vg_ready, pv_done, acc_set, u_ready, on_ready = (
            sem("s_ready"), sem("exp_done"), sem("vg_ready"), sem("pv_done"), sem("acc_set"),
            sem("u_ready"), sem("on_ready"))
        o_ready, o_taken, bias_added = sem("o_ready"), sem("o_taken"), sem("bias_added")
        lg_ready, lg_read, lg_moved, ex_ready, pw_ready, pt_ready, pt_copied, yb_ready, yb_taken, xl_ready = (
            sem("lg_ready"), sem("lg_read"), sem("lg_moved"), sem("ex_ready"), sem("pw_ready"), sem("pt_ready"),
            sem("pt_copied"), sem("yb_ready"), sem("yb_taken"), sem("xl_ready"))
        w_loaded = [sem(f"w_loaded{u}") for u in range(2)]
        wh_ready, wl_ready = sem("wh_ready"), sem("wl_ready")
        h_ready, h_free, sg_ready, hh_ready, hl_ready, y_ready, y_free = (
            sem("h_ready"), sem("h_free"), sem("sg_ready"), sem("hh_ready"), sem("hl_ready"),
             sem("y_ready"), sem("y_free"))
        shared_loaded = [sem(f"shared_loaded{u}") for u in range(NSH)]
        tables_loaded, routed_loaded, xs_cleared = sem("tables_loaded"), sem("routed_loaded"), sem("xs_cleared")
        chosen_ready, prefix_ready, slots_ready, scattered = (
            sem("chosen_ready"), sem("prefix_ready"), sem("slots_ready"), sem("scattered"))
        rows_loaded = [sem(f"rows_loaded{u}") for u in range(2)]
        rows_ready, vxh_ready, vxl_ready, vwh_ready, vwl_ready = (
            sem("rows_ready"), sem("vxh_ready"), sem("vxl_ready"), sem("vwh_ready"), sem("vwl_ready"))
        shared0_done = sem("shared0_done")
        vwl_last = sem("vwl_last")
        hid_ready, gate_ready, vhf_ready, vhh_ready, vhl_ready, vy_ready, vy_taken = (
            sem("hid_ready"), sem("gate_ready"), sem("vhf_ready"), sem("vhh_ready"), sem("vhl_ready"),
            sem("vy_ready"), sem("vy_taken"))
        y_stored = [sem(f"y_stored{u}") for u in range(2)]
        gathered = [sem(f"gathered{b}") for b in range(NB)]
        summed = sem("summed")
        out_stored = sem("out_stored")

        class Order:

            def __init__(self, eng, done):
                self.eng, self.done, self.count = eng, done, 0

            def then(self, ins):
                ins.then_inc(self.done, 1)
                self.count = self.count + 1

            def wait(self):
                self.eng.wait_ge(self.done, self.count)

        one, two, three, four, y_start, y_slots, store_start, vhf_start, vy_start = 1, 2, 3, 4, 32, 4, 16, 4, 1

        UNITS = {"k0": (0, True, SC, kd[0]), "q0": (8, True, QB, qd[0]),
                 "k1": (16, False, SC, kd[1]), "q1": (24, False, QB, qd[1])}

        def row_pieces(kind):
            if kind == "loop":
                return [("M", c) for c in range(8)] + [("TR", 0)] + [("M", c) for c in range(8, 14)] + \
                       [("D", 0)] + [("M", c) for c in range(14, NCH)]
            return [("TR", 0), ("D", 0)] if kind == "last but one" else [("R", 0), ("D", 0)]

        ROWS_HEAD = NPAIR + 1 + NPAIR
        ROWS_LOOP = len(row_pieces("loop"))
        TR_AT = row_pieces("loop").index(("TR", 0))
        ROWS_LAYER = ROWS_HEAD + (NIT - 2) * ROWS_LOOP + 6
        PAIRS = 2 * KT
        EXP_LAYER, PV_LAYER = PAIRS * NIT, KT * NIT

        ACC = 4

        assert ROWS_HEAD % 3 == 0 and ROWS_LOOP % 3 == 0 and ROWS_LAYER % 3 == 0

        def row_bank(k):
            return 5 + k % 3

        TAIL_ROWS = 7

        def score_bank(tail, j, half):
            return 2 * half if tail is None else (0, 2, 5)[(2 * (KT * tail + j) + half) % 3]

        def wide_banks(e):
            return 4 * (e % 2)

        def p_slot(u, j, half):
            return (2 * (u * KT + j) + half) % 4

        block = ctx.enter_context(nc.Block())

        @block.sync
        def _(sp):
            context = dram["ctxT"].rearrange("(c p) n -> p c n", p=128)
            sp.dma_start(WV[:, :, :], dram["wv"].rearrange("(c p) n -> p c n", p=128)).then_inc(ctx_loaded[0], 16)
            sp.dma_start(CTX[:, :, 0:CTX_FIRST], context[:, :, 0:CTX_FIRST]).then_inc(ctx_loaded[0], 16)
            sp.dma_start(const[:, :], dram["const"]).then_inc(const_loaded, 16)
            sp.dma_start(ident[:, :], dram["ident"]).then_inc(const_loaded, 16)
            sp.dma_start(pick[:, :, :], dram["pick"]).then_inc(const_loaded, 16)
            sp.dma_start(POS[:, T:], dram["pos"][:, T:].to_broadcast([128, SP])).then_inc(pos_loaded[0], 16)
            sp.dma_start(CTX[:, :, CTX_FIRST:], context[:, :, CTX_FIRST:]).then_inc(ctx_loaded[1], 16)
            sp.dma_start(POS[:, 0:T], dram["pos"][:, 0:T].to_broadcast([128, T])).then_inc(pos_loaded[1], 16)
            for n in ("k0", "k1", "q0"):
                sp.dma_start(W5[n][:, :, :], dram[n].rearrange("(c p) n -> p c n", p=128)).then_inc(wctx_loaded, 16)
            sp.dma_start(X[:, :, :], dram["x"].rearrange("(t p) d -> p t d", p=128)).then_inc(x_loaded, 16)
            sp.dma_start(WQ1[:, :, :], dram["q1"].rearrange("(c p) n -> p c n", p=128)).then_inc(rest_loaded, 16)
            for l in range(2):
                sp.dma_start(WO[:, l, :, :], dram[f"wo{l}"]).then_inc(rest_loaded, 16)
                sp.dma_start(router[:, l, :, :],
                             dram[f"router{l}"].rearrange("(c p) n -> p c n", p=128)).then_inc(rest_loaded, 16)
            sp.dma_start(rbias[:, :], dram["rbias"].to_broadcast([128, NR])).then_inc(rest_loaded, 16)
            sp.dma_start(prio[:, :, :], dram["prio"]).then_inc(rest_loaded, 16)
            sp.dma_start(bo0[:, :], dram["bo0"].to_broadcast([128, D])).then_inc(rest_loaded, 16)
            sp.dma_start(bout0[:, :], dram["bout0"]).then_inc(rest_loaded, 16)

            def store_parts(kind, b0=0, b1=4):
                first, _, n, dst = UNITS[kind]
                view = dst.rearrange("s f n -> f s n")
                for b in range(b0, b1):
                    for c in range(2):
                        sp.wait_ge(part3_ready, two + first + 2 * b + c + 1)
                        sp.dma_start(view[128 * c:128 * c + 128, :, b * n:b * n + n],
                                     PARTS[b % 2][c][:, :, 0:n]).then_inc(parts_stored[b % 2][c], 16)

            def wait_stored(kind, blocks):
                for v in range(min(blocks, 2)):
                    for c in range(2):
                        sp.wait_ge(parts_stored[v][c], store_start + 16 * (UNITS[kind][0] // 4 + -(-blocks // 2)))

            def load_k(l, h0=0, loaded=k_loaded):
                h1 = HG if loaded is k_first else H
                for p, (_, part) in enumerate(PRODUCTS):
                    sp.dma_start(KSTK[16 * p:16 * p + 16, h0:h1, :],
                                 kd[l][part].rearrange("(d h) n -> d h n", h=H)[:, h0:h1, 0:S]).then_inc(loaded, 16)

            def load_q(l, slot, b, g, loaded=q_loaded):
                for p, (part, _) in enumerate(PRODUCTS):
                    src = qd[l][part].rearrange("(d g h) n -> d g h n", g=NG, h=HG)
                    sp.dma_start(QST[16 * p:16 * p + 16, bass.ds(slot * HG, HG), :],
                                 src[:, bass.ds(g, 1), :, bass.ds(b * QB, QB)].rearrange("d g h n -> d (g h) n")
                                 ).then_inc(loaded, 16)

            def load_nm(l, n, slot):
                sp.wait_ge(nm_ready, l * NIT + n + 1)
                for s in range(3):
                    sp.dma_start(QST[NSTACK + s:NSTACK + s + 1, bass.ds(slot * HG, HG), :],
                                 NM[:, s, :]).then_inc(nm_loaded, 16)

            def attention(l):
                kind = f"q{l}"
                if l == 0:
                    load_k(0, loaded=k_first)
                store_parts(kind, 0, 1)
                wait_stored(kind, 1)
                load_q(l, 0, 0, 0, q_first)
                store_parts(kind, 1, 4)
                if l == 0:
                    store_parts("k1")
                    load_k(0, h0=HG)
                for n in (1, 2):
                    load_q(l, n, 0, n)
                wait_stored(kind, 4)
                load_nm(l, 0, 0)
                if l == 0:
                    sp.dma_start(xs, dram["zeros"].to_broadcast([SLOTS, D])).then_inc(xs_cleared, 16)
                with sp.Fori(3, NIT) as n:
                    sp.wait_ge(row_ready, l * ROWS_LAYER + ROWS_HEAD + ROWS_LOOP * (n - 3) + 1)
                    load_q(l, n % 4, n // 4, n % 4)
                    load_nm(l, n - 2, (n - 2) % 4)
                load_nm(l, NIT - 2, (NIT - 2) % 4)
                load_nm(l, NIT - 1, (NIT - 1) % 4)

            def expert_weights():
                with sp.Fori(0, E0 // 2) as pair:
                    for u in range(2):
                        e = 2 * pair + u
                        sp.wait_ge(wl_ready, e + 1)
                        sp.dma_start(BRAW[u][:, :], dram["bin0"][bass.ds(e, 1), :, :].rearrange("e p c -> p (e c)")
                                     ).then_inc(w_loaded[u], 16)
                        at = 0
                        for name in ("w_in", "w_out"):
                            src = dram[name]
                            rows, cols = src.shape[1] // 128, src.shape[2]
                            sp.dma_start(RAW[u][:, at:at + rows * cols].rearrange("p (c n) -> p c n", c=rows),
                                         src[bass.ds(e, 1), :, :].rearrange("e (c p) n -> p (e c) n", p=128)
                                         ).then_inc(w_loaded[u], 16)
                            at += rows * cols

            def load_expert(dst, prefix, e, loaded):
                at = 0
                for name in ("w1", "w3", "w2"):
                    src = dram[prefix + name]
                    rows, cols = src.shape[1] // 128, src.shape[2]
                    sp.dma_start(dst[:, at:at + rows * cols].rearrange("p (c n) -> p c n", c=rows),
                                 src[e, :, :].rearrange("(c p) n -> p c n", p=128)).then_inc(loaded, 16)
                    at += rows * cols

            def visits():
                def load_rows(n, u):
                    sp.dma_start(XROWS[u][:, :, :],
                                 xs[bass.ds(n * VT, VT), :].rearrange("(i p) d -> p i d", p=128)
                                 ).then_inc(rows_loaded[u], 16)

                def store_rows(n, u):
                    sp.wait_ge(vy_taken, vy_start + SHB + n + 1)
                    sp.dma_start(ys[bass.ds(n * VT, VT), :].rearrange("(i p) d -> p i d", p=128),
                                 YROWS[u][:, :, :]).then_inc(y_stored[u], 16)

                for s in range(NSH):
                    load_expert(SRAW[s][:, :], "s", s, shared_loaded[s])
                sp.dma_start(TRI[:, :], dram["tri"]).then_inc(tables_loaded, 16)
                sp.dma_start(ONES[:, :], dram["all_ones"]).then_inc(tables_loaded, 16)
                for e in range(4):
                    load_expert(RES[:, e, :], "", e, routed_loaded)
                sp.wait_ge(var_ready, 4)
                sp.dma_start(VNUM[:, :], dram["visit"]).then_inc(tables_loaded, 16)
                sp.wait_ge(scattered, 16 * 2 * NT)
                sp.wait_ge(vwl_ready, NSH)
                for e in range(4, E1):
                    load_expert(RES[:, e, :], "", e, routed_loaded)
                sp.wait_ge(vxl_ready, SHB)
                for n in range(3):
                    if n >= 2:
                        sp.wait_ge(rows_ready, n - 1)
                    load_rows(n, n % 2)
                with sp.Fori(0, (NV - 3) // 2) as i:
                    for u in range(2):
                        n = 2 * i + u
                        sp.wait_ge(rows_ready, n + 2)
                        load_rows(n + 3, 1 - u)
                        store_rows(n, u)
                for n in range(NV - 3, NV):
                    store_rows(n, n % 2)

            store_parts("k0")
            wait_stored("k0", 4)
            sp.wait_ge(table_ready, 4)
            sp.dma_start(KSTK[NSTACK:NSTACK + 3, :, :], dram["ones"]).then_inc(k_loaded, 16)
            attention(0)
            sp.wait_ge(s_ready, EXP_LAYER)
            wait_stored("k1", 4)
            load_k(1)
            sp.wait_ge(pv_done, two + PV_LAYER)
            expert_weights()
            attention(1)
            sp.wait_ge(s_ready, 2 * EXP_LAYER)
            sp.wait_ge(pv_done, two + 2 * PV_LAYER)
            visits()
            for b in range(NB):
                sp.wait_ge(summed, 2 * 4 * (b + 1))
                sp.dma_start(out.rearrange("(t p) d -> p t d", p=128)[:, 4 * b:4 * b + 4, :],
                             X[:, 4 * b:4 * b + 4, :]).then_inc(out_stored, 16)
            sp.wait_ge(out_stored, 16 * NB)

        @block.tensor
        def _(pe):
            def v_of_context():
                pe.wait_ge(ctx_loaded[0], 32)
                for j, rows in enumerate(KROWS):
                    if 128 * j == CTX_FIRST:
                        pe.wait_ge(ctx_loaded[1], 16)
                    if j >= V_BANKS:
                        pe.wait_ge(v_taken, 2 * (j - V_BANKS + 1))
                    for c in range(KC):
                        last = nc.tensor.matmul(ps[0:rows, 4 + j % V_BANKS, :], CTX[:, c, 128 * j:128 * j + rows],
                                                WV[:, c, :], start=(c == 0), stop=(c == KC - 1))
                    last.then_inc(v_ready, 1)

            def units(kind, b0=0, b1=4):
                first, _, n, _ = UNITS[kind]
                w = WQ1 if kind == "q1" else W5[kind]
                src = CTX if kind[0] == "k" else XN
                for b in range(b0, b1):
                    for c in range(2):
                        pe.wait_ge(unit_free, first + 2 * b + c + 1)
                        for kc in range(KC):
                            last = nc.tensor.matmul(ps[:, 2 * c + b % 2, 0:n], w[:, kc, 128 * c:128 * c + 128],
                                                    src[:, kc, b * n:b * n + n], start=(kc == 0), stop=(kc == KC - 1))
                        last.then_inc(unit_ready, 1)

            def norm_transposes(k):
                def half_of_tiles(q):
                    for slot in range(4):
                        pair = 4 * q + slot
                        pe.wait_ge(xc_ready, NT * k + 2 * pair + 2)
                        pe.wait_ge(xn_ready, 8 * k + pair + 1)
                        for i in range(2):
                            for c in range(KC):
                                last = nc.tensor.transpose(
                                    ps[:, 4 + slot, 256 * c + 128 * i:256 * c + 128 * i + 128],
                                    (XR[:, 2 * pair + i, 128 * c:128 * c + 128] if k == 3 else
                                     XCK[k][2 * slot + i][:, 128 * c:128 * c + 128]), ident[:, :])
                        last.then_inc(xt_ready, 1)

                if k == 3:
                    for q in range(2):
                        half_of_tiles(q)
                else:
                    with pe.Fori(0, 2) as q:
                        half_of_tiles(q)

            def row_piece(e, bank, what, c, kq, odd=0):
                pe.wait_ge(row_taken, e + 1)
                if what in ("T", "TR"):
                    last = nc.tensor.transpose(ps[0:NPAIR, bank, 0:128], M16[:, :], ident[:, :])
                if what in ("R", "TR"):
                    for qt in range(QB // 128):
                        last = nc.tensor.matmul(ps[:, bank, 128 + HG * qt:128 + HG * qt + HG],
                                                U[:, 128 * qt:128 * qt + 128], pick[:, odd, :], start=True,
                                                stop=True)
                elif what == "D":
                    for qt in range(QB // 128):
                        for h in range(HG):
                            last = nc.tensor.matmul(ps[32 * h:32 * h + 32, bank, 128 * qt:128 * qt + 128],
                                                    R16[:, qt, h:h + 1].to_broadcast([128, 32]), ident[:, :],
                                                    start=True, stop=True, tile_position=(0, 32 * h))
                elif what == "M":
                    pair, ch = divmod(c, len(MAXCOLS))
                    h, qt = divmod(pair, QB // 128)
                    off, w = MAXCOLS[ch]
                    head = kq * HG + h
                    last = nc.tensor.matmul(
                        ps[:, bank, 0:w],
                        QST[0:NSTACK, bass.ds(head, 1), 128 * qt:128 * qt + 128].rearrange("p a b -> p (a b)"),
                        KSTK[0:NSTACK, bass.ds(head, 1), off:off + w].rearrange("p a b -> p (a b)"),
                        start=True, stop=True)
                last.then_inc(row_ready, 1)

            def wide_piece(first, e, pair, kq):
                h, qt = divmod(pair, QB // 128)
                head = kq * HG + h
                pe.wait_ge(row_taken, three + first + e - 1)
                for ch in range(4):
                    last = nc.tensor.matmul(ps[:, wide_banks(e) + ch, 0:WIDE], QST[0:NSTACK, head, 128 * qt:128 * qt + 128],
                                            KSTK[0:NSTACK, head, WIDE_STEP * ch:WIDE_STEP * ch + WIDE],
                                            start=True, stop=True)
                last.then_inc(row_ready, 1)

            def weigh(l, step, j, u):
                pe.wait_ge(exp_done, two + l * EXP_LAYER + 2 * step + 2)
                rows = KROWS[j]
                for h in range(HG):
                    last = nc.tensor.matmul(ps[32 * h:32 * h + 32, ACC, :], VG[u][0:rows, j, h, :],
                                            PR[p_slot(u, j, h // 2)][0:rows, h % 2, :],
                                            start=(j == 0), stop=(j == KT - 1), tile_position=(0, 32 * h))
                last.then_inc(pv_done, 1)

            def iteration(l, it, u, g, g2, kind, first, tail=None, follows=True):
                pieces = row_pieces(kind)
                at = [0]

                def rows(n, j):
                    for k in range(at[0], min(at[0] + n, len(pieces))):
                        what, c = pieces[k]
                        if what != "M" and j < 1 or what == "D" and j < 2:
                            return
                        if what == "D":
                            pe.wait_ge(row_taken, three + first + (TR_AT if kind == "loop" else 0) + 1)
                        if what in ("TR", "R"):
                            pe.wait_ge(u_ready, one + l * (NIT + 1) + it + 1)
                        if what == "TR":
                            pe.wait_ge(m16_ready, l * NIT + it + 2)
                        if what == "M" and c == 0:
                            pe.wait_ge(q_loaded, 96 * (l * (NIT - 1) + it + 2))
                        if tail is not None:
                            pe.wait_ge(row_taken, three + first + k)
                        row_piece(first + k, row_bank(k) if tail is None else TAIL_ROWS, what, c, g2, 1 - u)
                        at[0] = k + 1

                pe.wait_ge(nm_loaded, 48 * (l * NIT + it + 1))
                for j in range(KT):
                    step = KT * it + j
                    for half in range(2):
                        piece = l * EXP_LAYER + 2 * step + half
                        if tail == 0 and (j, half) == (1, 0):
                            pe.wait_ge(row_taken, three + first)
                        elif tail is None or tail == 0 and j == 0:
                            pe.wait_ge(exp_done, two + piece - 1)
                        else:
                            pe.wait_ge(exp_done, two + piece - 2)
                        for h in (2 * half, 2 * half + 1):
                            head = g * HG + h
                            last = nc.tensor.matmul(
                                ps[0:KROWS[j], score_bank(tail, j, half) + h % 2, :],
                                KSTK[:, bass.ds(head, 1), 128 * j:128 * j + KROWS[j]].rearrange("p a b -> p (a b)"),
                                QST[:, bass.ds(head, 1), :].rearrange("p a b -> p (a b)"),
                                start=True, stop=True)
                        last.then_inc(s_ready, 1)
                        rows(2 if (half, j) == (0, 6) else 1, j)
                    if j == 0 and follows:
                        weigh(l, step - 1, KT - 1, 1 - u)
                    if j > 0:
                        if j == 1:
                            pe.wait_ge(vg_ready, l * NIT + it + 1)
                            pe.wait_ge(u_ready, one + l * (NIT + 1) + it + 1)
                        weigh(l, step - 1, j - 1, u)
                    rows(3, j)
                rows(NCH, KT)

            def attention(l):
                if l == 0:
                    pe.wait_ge(k_first, 96)
                pe.wait_ge(q_first, 96 * (l + 1))
                pe.wait_ge(unit_free, four + 24 + 8 * l)
                first = l * ROWS_LAYER
                for n in range(2):
                    if n + l == 1:
                        pe.wait_ge(k_loaded, 16 + 96 * (l + 1))
                    if n == 1:
                        pe.wait_ge(q_loaded, 96 * (l * (NIT - 1) + 2))
                    for pair in range(NPAIR):
                        wide_piece(first, (NPAIR + 1) * n + pair, pair, n)
                    if n == 0:
                        pe.wait_ge(m16_ready, l * NIT + 1)
                        nc.tensor.transpose(ps[0:NPAIR, wide_banks(NPAIR), 0:128], M16[:, :],
                                            ident[:, :]).then_inc(row_ready, 1)
                pe.wait_ge(row_taken, three + first + ROWS_HEAD)
                first = l * ROWS_LAYER + ROWS_HEAD
                iteration(l, 0, 0, 0, 2, "loop", first, follows=False)
                with pe.Fori(0, NIT // NG - 1) as i:
                    for k in range(1, NG + 1):
                        it = NG * i + k
                        iteration(l, it, k % 2, k % NG, (k + 2) % NG, "loop", first + ROWS_LOOP * it)
                iteration(l, NIT - 3, 1, 1, 3, "loop", first + ROWS_LOOP * (NIT - 3))
                first = first + ROWS_LOOP * (NIT - 2)
                iteration(l, NIT - 2, 0, 2, 0, "last but one", first, 0)
                iteration(l, NIT - 1, 1, 3, 0, "last", first + 2, 1)
                weigh(l, KT * NIT - 1, KT - 1, 1)
                pe.wait_ge(u_ready, one + (l + 1) * (NIT + 1))
                pe.wait_ge(row_taken, three + first + 4)
                row_piece(first + 4, TAIL_ROWS, "R", 0, 0, 1)
                pe.wait_ge(row_taken, three + first + 5)
                row_piece(first + 5, TAIL_ROWS, "D", 0, 0)

            def output_projection(l):
                pe.wait_ge(rest_loaded, 16 * 9)
                pe.wait_ge(odd_added, one + (l + 1) * (NIT // 2 + 1))
                for t in range(NT):
                    if t >= 4:
                        pe.wait_ge(o_taken, NT * l + t - 3)
                    b, qt = divmod(t, 4)
                    for g in range(NG // 2):
                        last = nc.tensor.matmul(ps[:, t % 4, 0:D], ON[:, NG // 2 * b + g, 128 * qt:128 * qt + 128],
                                                WO[:, l, g, :], start=(g == 0), stop=(g == NG // 2 - 1))
                    last.then_inc(o_ready, 1)

            def router_logits(l):
                pe.wait_ge(rest_loaded, 16 * 9)
                for t in range(NT):
                    if t % 2 == 0:
                        pe.wait_ge(xn_ready, four + 8 * (2 * l + 1) + t // 2 + 1)
                    for c in range(KC):
                        last = nc.tensor.matmul(ps[:, 2, NR * t:NR * t + NR], XN[:, c, 128 * t:128 * t + 128],
                                                router[:, l, c, :], start=(c == 0), stop=(c == KC - 1))
                last.then_inc(lg_ready, 1)

            def expert_output_bias():
                pe.wait_ge(pw_ready, 1)
                pe.wait_ge(y_free, y_slots + E0 * NT)
                for b in range(NB):
                    for i in range(4):
                        last = nc.tensor.transpose(ps[0:NR, 4 + b, 128 * i:128 * i + 128],
                                                   PW[:, 4 * b + i, 0:NR], ident[:, :])
                    last.then_inc(pt_ready, 1)
                for t in range(NT):
                    if t % 4 == 0:
                        pe.wait_ge(pt_copied, NB)
                    if t >= 4:
                        pe.wait_ge(yb_taken, t - 3)
                    nc.tensor.matmul(ps[:, 4 + t % 4, 0:D], PT[:, 128 * t:128 * t + 128], bout0[:, :],
                                     start=True, stop=True).then_inc(yb_ready, 1)

            def three_passes(dst, lh, ll, rh, rl, first, final):
                nc.tensor.matmul(dst, lh, rh, start=first, stop=False)
                nc.tensor.matmul(dst, lh, rl, start=False, stop=False)
                return nc.tensor.matmul(dst, ll, rh, start=False, stop=final)

            def experts():
                pe.wait_ge(xl_ready, 8)
                pe.wait_ge(lg_read, 1)
                with pe.Fori(0, E0 // 2) as pair:
                    for u in range(2):
                        e = 2 * pair + u
                        with pe.Fori(0, 2) as tp:
                            pe.wait_ge(wl_ready, two + e + 1)
                            for v in range(2):
                                tb = 2 * tp + v
                                for c in range(HC0):
                                    q = (NB * e + tb) * HC0 + c
                                    pe.wait_ge(h_free, q + 1)
                                    for kc in range(KC):
                                        at = kc * HID0 + 128 * c
                                        last = three_passes(
                                            ps[:, 2 * (c % 2), :], WH[u][:, at:at + 128], WL[u][:, at:at + 128],
                                            XH[:, kc, bass.ds(QB * tb, QB)], XL[:, kc, bass.ds(QB * tb, QB)],
                                            kc == 0, kc == KC - 1)
                                    last.then_inc(h_ready, 1)
                            for v in range(2):
                                k = NB * e + 2 * tp + v
                                w2 = KC * HID0
                                pe.wait_ge(hl_ready, two + k * HC0 + HC0)
                                for qt in range(4):
                                    pe.wait_ge(y_free, 4 * k + qt + 1)
                                    for c in range(HC0):
                                        last = three_passes(
                                            ps[:, 4 + qt, 0:D],
                                            HH[v][:, c, 128 * qt:128 * qt + 128],
                                            HL[v][:, c, 128 * qt:128 * qt + 128],
                                            WH[u][:, w2 + D * c:w2 + D * c + D],
                                            WL[u][:, w2 + D * c:w2 + D * c + D],
                                            c == 0, c == HC0 - 1)
                                    last.then_inc(y_ready, 1)

            def visit_hidden(u, slot, q):
                for c in range(HC1):
                    pe.wait_ge(vhf_ready, vhf_start + q + c - HC1 + 1)
                    for w in range(2):
                        for kc in range(KC):
                            at = (w * KC + kc) * 128 * HC1 + 128 * c
                            last = three_passes(ps[:, c, VT * w:VT * w + VT],
                                                VWH[u][:, at:at + 128], VWL[u][:, at:at + 128],
                                                VXH[slot][:, kc, :], VXL[slot][:, kc, :], kc == 0, kc == KC - 1)
                    last.then_inc(hid_ready, 1)

            def visit_output(u, q, chunks, first, final):
                w2 = 2 * KC * 128 * HC1
                pe.wait_ge(vhl_ready, q + chunks[-1] + 1)
                for i in range(2):
                    for c in chunks:
                        last = three_passes(ps[:, 4 + i, 0:D],
                                            VHH[u][:, c, 128 * i:128 * i + 128],
                                            VHL[u][:, c, 128 * i:128 * i + 128],
                                            VWH[u][:, w2 + D * c:w2 + D * c + D],
                                            VWL[u][:, w2 + D * c:w2 + D * c + D],
                                            first and c == 0, final and c == HC1 - 1)
                return last

            def shared_block(b, v, last=False):
                pe.wait_ge(vxl_ready, b + 1)

                def output(s):
                    q = HC1 * (NSH * b + s)
                    visit_output(s, q, range(HC1 - 1), s == 0, False)
                    return visit_output(s, q, [HC1 - 1], False, s == NSH - 1)

                visit_hidden(0, v, HC1 * NSH * b)
                if last:
                    pe.wait_ge(vy_taken, vy_start + b)
                    output(0).then_inc(shared0_done, 1)
                visit_hidden(1, v, HC1 * (NSH * b + 1))
                if not last:
                    pe.wait_ge(vy_taken, vy_start + b)
                    output(0)
                output(1).then_inc(vy_ready, 1)

            def transpose_rows(n, u):
                pe.wait_ge(vxl_ready, SHB + n - 1)
                pe.wait_ge(rows_loaded[u], 16 * (n // 2 + 1))
                for i in range(2):
                    for c in range(KC):
                        last = nc.tensor.transpose(ps[:, 6 + u, VT * c + 128 * i:VT * c + 128 * i + 128],
                                                   XROWS[u][:, i, 128 * c:128 * c + 128], ident[:, :])
                last.then_inc(rows_ready, 1)

            def visit(n, u, more):
                q = HC1 * (NSH * SHB + n)
                pe.wait_ge(vwl_ready, NSH + 3 * (n + 1))
                pe.wait_ge(vxl_ready, SHB + n + 1)
                visit_hidden(u, u, q)
                if more:
                    transpose_rows(n + 1, 1 - u)
                pe.wait_ge(vwl_last, n + 1)
                pe.wait_ge(vy_taken, vy_start + SHB + n)
                visit_output(u, q, range(HC1 - 2), True, False)
                visit_output(u, q, [HC1 - 2], False, False)
                visit_output(u, q, [HC1 - 1], False, True).then_inc(vy_ready, 1)

            def visits():
                pe.wait_ge(vwl_ready, NSH)
                shared_block(0, 0)
                shared_block(1, 1)
                shared_block(2, 0)
                pe.wait_ge(tables_loaded, 48)
                pe.wait_ge(chosen_ready, 1)
                chosen = POSN[:, :, :].rearrange("p t e -> p (t e)")
                nc.tensor.matmul(ps[:, 7, 0:NT * NR], TRI[:, :], chosen, start=True, stop=True)
                nc.tensor.matmul(ps[:, 7, NT * NR:2 * NT * NR], ONES[:, :], chosen, start=True,
                                 stop=True).then_inc(prefix_ready, 1)
                shared_block(3, 1)
                with pe.Fori(2, SHB // 2 - 1) as i:
                    for v in range(2):
                        shared_block(2 * i + v, v)
                shared_block(SHB - 2, 0)
                shared_block(SHB - 1, 1, last=True)
                transpose_rows(0, 0)
                with pe.Fori(0, NV // 2) as i:
                    for u in range(2):
                        visit(2 * i + u, u, True)
                visit(NV - 1, 0, False)

            pe.wait_ge(const_loaded, 48)
            v_of_context()
            pe.wait_ge(wctx_loaded, 16 * 3)
            units("k0", 0, 1)
            norm_transposes(0)
            pe.wait_ge(xn_ready, four + 8)
            units("k0", 1, 4)
            units("q0")
            units("k1")
            attention(0)
            output_projection(0)
            norm_transposes(1)
            router_logits(0)
            experts()
            expert_output_bias()
            norm_transposes(2)
            pe.wait_ge(xn_ready, four + 24)
            units("q1")
            attention(1)
            output_projection(1)
            norm_transposes(3)
            router_logits(1)
            visits()

        @block.scalar
        def _(act):
            def evacuate_v(j, rows):
                act.wait_ge(v_ready, j + 1)
                for l in range(2):
                    nc.scalar.activation(V[l][0:rows, :, j, :],
                                         ps[0:rows, 4 + j % V_BANKS, D * l:D * l + D].rearrange("p (g n) -> p g n", g=NG),
                                         ACT.Copy).then_inc(v_taken, 1)

            def unit_parts(kind):
                first, _, n, _ = UNITS[kind]
                with act.Fori(0, 2) as i:
                    for v in range(2):
                        u0 = first + 4 * i + 2 * v
                        for c in range(2):
                            act.wait_ge(f_ready, u0 + c + 1)
                            act.wait_ge(parts_stored[v][c], 16 * (first // 4 + i + 1))
                            nc.scalar.activation(PARTS[v][c][:, 0, 0:n], F[v][c][:, 0:n], ACT.Copy).then_inc(part1_ready, 1)
                        for c in range(2):
                            act.wait_ge(rest1_ready, four + u0 + c + 1)
                            nc.scalar.activation(PARTS[v][c][:, 1, 0:n], G[c][:, 0:n], ACT.Copy).then_inc(part2_ready, 1)

            def norm_sd(k):
                act.wait_ge(var_ready, k + 1)
                nc.scalar.activation(norm[:, 3, :], norm[:, 2, :], ACT.Sqrt,
                                     bias=const[:, C_EPS:C_EPS + 1]).then_inc(sd_ready, 1)

            def norm_copies(k):
                before_experts = k == 1
                if before_experts:
                    act.wait_ge(o_ready, NT)
                with act.Fori(0, 2) as q:
                    for slot in range(4):
                        pair = 4 * q + slot
                        act.wait_ge(xt_ready, 8 * k + pair + 1)
                        act.wait_ge(sd_ready, k + 1)
                        source = ps[:, 4 + slot, :].rearrange("p (c n) -> p c n", c=KC)
                        if before_experts:
                            nc.scalar.activation(XH[:, :, bass.ds(256 * pair, 256)], source, ACT.Copy)
                        nc.scalar.activation(XN[:, :, bass.ds(256 * pair, 256)], source,
                                             ACT.Copy).then_inc(xn_ready, 1)

            def exp_pair(l, it, j, half, u, tail):
                bank = score_bank(tail, j, half)
                step = KT * it + j
                rows = KROWS[j]
                act.wait_ge(s_ready, l * EXP_LAYER + 2 * step + half + 1)
                act.wait_ge(pv_done, l * PV_LAYER + step + 1)
                nc.scalar.activation(PR[p_slot(u, j, half)][0:rows, :, :],
                                     ps[0:rows, bank:bank + 2, :], ACT.Exp,
                                     scale=DH ** -0.5).then_inc(exp_done, 1)

            def copy_sums(l, it):
                act.wait_ge(pv_done, two + l * PV_LAYER + KT * it)
                act.wait_ge(on_ready, one + l * (NIT + 1) + it)
                nc.scalar.activation(U[:, :], ps[:, ACC, :], ACT.Copy).then_inc(u_ready, 1)

            def attention(l):
                act.wait_ge(acc_set, l + 1)

                def iteration(it, u, tail=None):
                    for j in range(KT):
                        for half in range(2):
                            exp_pair(l, it, j, half, u, tail)
                        if j == 0:
                            copy_sums(l, it)

                with act.Fori(0, NIT // 2 - 1) as i:
                    for u in range(2):
                        iteration(2 * i + u, u)
                iteration(NIT - 2, 0, 0)
                iteration(NIT - 1, 1, 1)
                copy_sums(l, NIT)

            def router_exp(l):
                act.wait_ge(lg_moved, l + 1)
                nc.scalar.activation(PB[l][:, :, :], PB[l][:, :, :], ACT.Exp).then_inc(ex_ready, 1)

            def expert_weights(e, u, turn):
                nload = 3
                act.wait_ge(w_loaded[u], 16 * nload * (turn + 1))
                act.wait_ge(y_ready, y_start + NT * (e - 1))
                nc.scalar.activation(BIN[u][:, :], BRAW[u][:, :], ACT.Copy)
                nc.scalar.activation(WH[u][:, :], RAW[u][:, :], ACT.Copy).then_inc(wh_ready, 1)

            def experts():
                def blocks(e, u, tp):
                    act.wait_ge(wh_ready, e + 1)
                    for v in range(2):
                        for c in range(HC0):
                            q = (NB * e + 2 * tp + v) * HC0 + c
                            act.wait_ge(h_ready, q + 1)
                            act.wait_ge(hl_ready, q + 1)
                            nc.scalar.activation(HF[c % 2][:, :], ps[:, 2 * (c % 2), :], ACT.Gelu_apprx_tanh,
                                                 bias=BIN[u][:, c:c + 1]).then_inc(h_free, 1)

                def expert(pair, u, more):
                    e = 2 * pair + u
                    blocks(e, u, 0)
                    if more:
                        expert_weights(e + 1, 1 - u, pair + u)
                    blocks(e, u, 1)

                with act.Fori(0, E0 // 2 - 1) as pair:
                    for u in range(2):
                        expert(pair, u, True)
                expert(E0 // 2 - 1, 0, True)
                expert(E0 // 2 - 1, 1, False)

            def gate(q, c):
                act.wait_ge(hid_ready, q + c + 1)
                act.wait_ge(vhf_ready, vhf_start + q + c - 1)
                nc.scalar.activation(SG[c % 2][:, :], ps[:, c, 0:VT], ACT.Silu).then_inc(gate_ready, 1)

            def round_block(b, v):
                nc.scalar.activation(VXH[v][:, :, :], XN[:, :, bass.ds(VT * b, VT)], ACT.Copy).then_inc(vxh_ready, 1)

            def shared_block(b, v, more):
                q = HC1 * NSH * b
                for c in range(HC1):
                    gate(q, c)
                if more:
                    round_block(b + 1, 1 - v)
                else:
                    act.wait_ge(routed_loaded, 48 * E1)
                    act.wait_ge(slots_ready, 1)
                    first = expert_of(0)
                for c in range(HC1):
                    gate(q + HC1, c)
                    if not more:
                        act.wait_ge(shared0_done, 1)
                        round_weights(first, 0, c)

            def round_rows(n, u):
                act.wait_ge(rows_ready, n + 1)
                nc.scalar.activation(VXH[u][:, :, :], ps[:, 6 + u, :].rearrange("p (c n) -> p c n", c=KC),
                                     ACT.Copy).then_inc(vxh_ready, 1)

            def expert_of(n):
                return act.value_load(EXPERT[0:1, bass.ds(n, 1)], min_val=0, max_val=E1 - 1)

            def round_weights(e, u, piece):
                cols = slice(WCOLS // 4 * piece, WCOLS // 4 * (piece + 1))
                nc.scalar.activation(VWH[u][:, cols], RES[:, bass.ds(e, 1), cols].rearrange("p a b -> p (a b)"),
                                     ACT.Copy).then_inc(vwh_ready, 1)

            def take_output(n, u):
                act.wait_ge(y_stored[u], 16 * (n // 2) + store_start)
                act.wait_ge(vy_ready, SHB + n + 1)
                nc.scalar.activation(YROWS[u][:, :, :], ps[:, 4:6, 0:D],
                                     ACT.Copy).then_inc(vy_taken, 1)

            def round_shared_weights():
                for s in range(NSH):
                    act.wait_ge(shared_loaded[s], 48)
                    nc.scalar.activation(VWH[s][:, :], SRAW[s][:, :], ACT.Copy).then_inc(vwh_ready, 1)

            def visits():
                round_block(0, 0)
                shared_block(0, 0, True)
                with act.Fori(0, SHB // 2 - 1) as i:
                    for v in range(2):
                        shared_block(2 * i + 1 + v, 1 - v, True)
                shared_block(SHB - 1, 1, False)
                round_rows(0, 0)

                def visit(n, u, more, before):
                    if before:
                        take_output(n - 1, 1 - u)
                    if more:
                        following = expert_of(n + 1)
                    for c in range(HC1):
                        gate(HC1 * (NSH * SHB + n), c)
                        if more:
                            round_weights(following, 1 - u, c)
                    if more:
                        round_rows(n + 1, 1 - u)

                visit(0, 0, True, False)
                with act.Fori(0, (NV - 2) // 2) as i:
                    for u in range(2):
                        visit(2 * i + 1 + u, 1 - u, True, True)
                visit(NV - 2, 1, True, True)
                visit(NV - 1, 0, False, True)
                take_output(NV - 1, 0)

            def tables(which):
                cols = (slice(T, NPOS), slice(0, T))[which]
                act.wait_ge(angle_ready, which + 1)
                nc.scalar.activation(SIN[:, cols], ANG[:, cols], ACT.Sin).then_inc(table_ready, 1)
                nc.scalar.activation(TURN[:, cols], ANG[:, cols], ACT.Abs).then_inc(act_done, 1)
                act.wait_ge(act_done, which + 1)
                nc.scalar.activation(COS[:, cols], TURN[:, cols], ACT.Sin, scale=-1.0,
                                     bias=const[:, C_HALFPI:C_HALFPI + 1]).then_inc(table_ready, 1)

            act.wait_ge(const_loaded, 48)
            for j, rows in enumerate(KROWS):
                evacuate_v(j, rows)
                if j == 6:
                    tables(0)
            tables(1)
            norm_sd(0)
            norm_copies(0)
            unit_parts("k0")
            unit_parts("q0")
            unit_parts("k1")
            attention(0)
            norm_sd(1)
            norm_copies(1)
            expert_weights(0, 0, 0)
            router_exp(0)
            experts()
            for b in range(NB):
                act.wait_ge(pt_ready, b + 1)
                nc.scalar.activation(PT[:, QB * b:QB * b + QB], ps[0:NR, 4 + b, :], ACT.Copy).then_inc(pt_copied, 1)
            norm_sd(2)
            norm_copies(2)
            unit_parts("q1")
            attention(1)
            round_shared_weights()
            norm_sd(3)
            norm_copies(3)
            router_exp(1)
            visits()

        @block.gpsimd
        def _(pool):
            def unit_parts(kind):
                first, _, n, _ = UNITS[kind]
                with pool.Fori(0, 2) as i:
                    for v in range(2):
                        u0 = first + 4 * i + 2 * v
                        for c in range(2):
                            pool.wait_ge(part1_ready, u0 + c + 1)
                            pool.wait_ge(part3_ready, u0 + c + 1)
                            nc.gpsimd.tensor_tensor(G[c][:, 0:n], F[v][c][:, 0:n], PARTS[v][c][:, 0, 0:n],
                                                    ALU.subtract).then_inc(rest1_ready, 1)
                        for c in range(2):
                            pool.wait_ge(part2_ready, u0 + c + 1)
                            nc.gpsimd.tensor_tensor(PARTS[v][c][:, 2, 0:n], G[c][:, 0:n], PARTS[v][c][:, 1, 0:n],
                                                    ALU.subtract).then_inc(part3_ready, 1)

            def stage_v(l, n, u, g):
                pool.wait_ge(ones_set, 3 * (l + 1))
                for rows, j0, j1 in ((128, 0, KT - 1), (KROWS[-1], KT - 1, KT)):
                    last = nc.gpsimd.tensor_copy(
                        VG[u][0:rows, j0:j1, :, DH * u:DH * u + DH].rearrange("p j h d -> p (j h) d"),
                        V[l][0:rows, bass.ds(g, 1), j0:j1, :].rearrange("p g j (h d) -> p (g j h) d", d=DH))
                last.then_inc(vg_ready, 1)

            def cut_maxima(l, n, t_piece):
                pool.wait_ge(row_taken, three + t_piece + 1)
                pool.wait_ge(nm_loaded, 48 * (l * NIT + n))
                base = l * NIT * 3 + 3 * n
                nc.gpsimd.tensor_tensor(NM[:, 0, :], NMF[:, 0, :], ZERO[:, :], ALU.add).then_inc(cut_done, 1)
                pool.wait_ge(cut_done, base + 1)
                nc.gpsimd.tensor_tensor(NMF[:, 1, :], NMF[:, 0, :], NM[:, 0, :], ALU.subtract).then_inc(cut_done, 1)
                pool.wait_ge(cut_done, base + 2)
                nc.gpsimd.tensor_tensor(NM[:, 1, :], NMF[:, 1, :], ZERO[:, :], ALU.add).then_inc(cut_done, 1)
                pool.wait_ge(cut_done, base + 3)
                nc.gpsimd.tensor_tensor(NM[:, 2, :], NMF[:, 1, :], NM[:, 1, :], ALU.subtract).then_inc(nm_ready, 1)

            def add_odd(l, it, slot):
                pool.wait_ge(on_ready, one + l * (NIT + 1) + it + 1)
                on = ON[:, bass.ds(slot, 1), :].rearrange("p a b -> p (a b)")
                nc.gpsimd.tensor_tensor(on, on, ODD[:, :], ALU.add).then_inc(odd_added, 1)

            def attention(l):
                nc.gpsimd.memset(ZERO[:, :], 0.0).then_inc(ones_set, 1)
                for u in range(2):
                    nc.gpsimd.memset(VG[u][:, :, :, DH * (1 - u):DH * (1 - u) + DH], 1.0).then_inc(ones_set, 1)
                nc.gpsimd.memset(ON[:, NIT // 2 - 1, :], 0.0)
                stage_v(l, 0, 0, 0)
                if l == 0:
                    pool.wait_ge(xc_ready, NT)
                    pool.wait_ge(rest_loaded, 16 * 9)
                    nc.gpsimd.tensor_tensor(X[:, :, :], X[:, :, :], bo0[:, :].unsqueeze(1).to_broadcast([128, NT, D]),
                                            ALU.add).then_inc(bias_added, 1)
                first = l * ROWS_LAYER
                cut_maxima(l, 0, first + NPAIR)
                first = first + ROWS_HEAD
                with pool.Fori(0, NIT // 2 - 1) as i:
                    for u in range(2):
                        it = 2 * i + u
                        pool.wait_ge(pv_done, two + l * PV_LAYER + KT * it)
                        stage_v(l, it + 1, 1 - u, (it + 1) % 4)
                        cut_maxima(l, it + 1, first + ROWS_LOOP * it + TR_AT)
                        if u == 0:
                            add_odd(l, it, (i + NIT // 2 - 1) % (NIT // 2))
                first = first + ROWS_LOOP * (NIT - 2)
                pool.wait_ge(pv_done, two + l * PV_LAYER + KT * (NIT - 2))
                stage_v(l, NIT - 1, 1, 3)
                cut_maxima(l, NIT - 1, first)
                add_odd(l, NIT - 2, NIT // 2 - 2)
                add_odd(l, NIT, NIT // 2 - 1)

            def experts():
                def rest_of_weights(e, u):
                    pool.wait_ge(wh_ready, e + 1)
                    nc.gpsimd.tensor_tensor(WL[u][:, :], RAW[u][:, :], WH[u][:, :].bitcast(f32),
                                            ALU.subtract).then_inc(wl_ready, 1)

                def blocks(e, tp):
                    for v in range(2):
                        for c in range(HC0):
                            q = (NB * e + 2 * tp + v) * HC0 + c
                            pool.wait_ge(hh_ready, q + 1)
                            nc.gpsimd.tensor_tensor(HL[v][:, c, :], HF[c % 2][:, :], HH[v][:, c, :].bitcast(f32),
                                                    ALU.subtract).then_inc(hl_ready, 1)

                def expert(e, u, more):
                    blocks(e, 0)
                    if more:
                        rest_of_weights(e + 1, 1 - u)
                    blocks(e, 1)

                rest_of_weights(0, 0)
                with pool.Fori(0, E0 // 2 - 1) as pair:
                    for u in range(2):
                        expert(2 * pair + u, u, True)
                expert(E0 - 2, 0, True)
                expert(E0 - 1, 1, False)

            def visits():
                pool.wait_ge(o_ready, 2 * NT)
                for s in range(NSH):
                    pool.wait_ge(vwh_ready, s + 1)
                    nc.gpsimd.tensor_tensor(VWL[s][:, :], SRAW[s][:, :], VWH[s][:, :].bitcast(f32),
                                            ALU.subtract).then_inc(vwl_ready, 1)
                pool.wait_ge(xs_cleared, 16)
                pool.wait_ge(slots_ready, 1)
                for t in range(NT):
                    for i in range(2):
                        nc.gpsimd.indirect_dma_start(xs, bass.IndirectOffsetOnAxis(SLOT[i][:, t:t + 1], 0),
                                                     XR[:, t, :], None).then_inc(scattered, 16)

                def cut_weights(n, u):
                    e = pool.value_load(EXPERT[0:1, bass.ds(n, 1)], min_val=0, max_val=E1 - 1)
                    for piece in range(3):
                        cols = slice(WCOLS // 4 * piece, WCOLS // 4 * (piece + 1))
                        pool.wait_ge(vwh_ready, NSH + HC1 * n + piece + 1)
                        nc.gpsimd.tensor_tensor(VWL[u][:, cols],
                                                RES[:, bass.ds(e, 1), cols].rearrange("p a b -> p (a b)"),
                                                VWH[u][:, cols].bitcast(f32), ALU.subtract).then_inc(vwl_ready, 1)

                cut_weights(0, 0)
                with pool.Fori(0, NV // 2) as i:
                    for u in range(2):
                        cut_weights(2 * i + u + 1, 1 - u)
                for u in range(2):
                    pool.wait_ge(y_stored[u], store_start + 16 * ((NV + 1 - u) // 2))
                for t in range(NT):
                    for i in range(2):
                        nc.gpsimd.indirect_dma_start(YG[:, t, i, :], None, ys,
                                                     bass.IndirectOffsetOnAxis(SLOT[i][:, t:t + 1], 0)
                                                     ).then_inc(gathered[t // 4], 16)

            unit_parts("k0")
            unit_parts("q0")
            unit_parts("k1")
            attention(0)
            experts()
            unit_parts("q1")
            attention(1)
            visits()

        @block.vector
        def _(dve):
            order = Order(dve, dve_done)

            def ordered(ins):
                order.then(ins)
                order.wait()

            def angles(which):
                cols = (slice(T, NPOS), slice(0, T))[which]
                ang, turn = ANG[:, cols], TURN[:, cols]
                dve.wait_ge(pos_loaded[which], 16)
                dve.wait_ge(const_loaded, 48)
                ordered(nc.vector.tensor_copy(ang, POS[:, cols]))
                ordered(nc.vector.tensor_scalar(ang, ang, const[:, C_FREQ:C_FREQ + 1], None, ALU.mult))
                ordered(nc.vector.tensor_scalar(turn, ang, float(0.5 / np.pi), ROUND, ALU.mult, ALU.add))
                ordered(nc.vector.tensor_scalar(turn, turn, ROUND, None, ALU.subtract))
                for part in TWO_PI_PARTS:
                    ordered(nc.vector.scalar_tensor_tensor(ang, turn, -part, ang, ALU.mult, ALU.add))
                nc.vector.tensor_scalar(ang, ang, PI_BELOW, -PI_BELOW, ALU.min, ALU.max).then_inc(angle_ready, 1)

            def units(kind):
                first, rope, n, _ = UNITS[kind]
                col = T if kind[0] == "k" else 0
                with dve.Fori(0, 2) as i:
                    for v in range(2):
                        u0 = first + 4 * i + 2 * v
                        cos = COS[:, bass.ds(i * 2 * n + (v * n + col), n)]
                        sin = SIN[:, bass.ds(i * 2 * n + (v * n + col), n)]
                        x1, x2 = ps[:, v, 0:n], ps[:, 2 + v, 0:n]
                        for c in range(2):
                            dve.wait_ge(unit_ready, u0 + c + 1)
                            dve.wait_ge(rest1_ready, u0 + c + 1)
                            if not rope:
                                nc.vector.tensor_copy(F[v][c][:, 0:n], (x1, x2)[c]).then_inc(f_ready, 1)
                                dve.wait_ge(f_ready, u0 + c + 1)
                                nc.vector.memset(scrap[:, 30 + c:31 + c], 0.0).then_inc(unit_free, 1)
                        if rope:
                            nc.vector.tensor_tensor(F[v][0][:, 0:n], x1, cos, ALU.mult)
                            nc.vector.tensor_tensor(F[v][1][:, 0:n], x1, sin, ALU.mult).then_inc(unit_free, 1)
                            nc.vector.tensor_tensor(TMP[0][:, 0:n], x2, sin, ALU.mult)
                            nc.vector.tensor_tensor(TMP[1][:, 0:n], x2, cos, ALU.mult).then_inc(unit_free, 1)
                            dve.wait_ge(unit_free, four + u0 + 2)
                            nc.vector.tensor_tensor(F[v][0][:, 0:n], F[v][0][:, 0:n], TMP[0][:, 0:n],
                                                    ALU.subtract).then_inc(f_ready, 1)
                            nc.vector.tensor_tensor(F[v][1][:, 0:n], F[v][1][:, 0:n], TMP[1][:, 0:n],
                                                    ALU.add).then_inc(f_ready, 1)
                            dve.wait_ge(f_ready, u0 + 2)

            def norm_variance():
                half = D // 2
                ordered(nc.vector.tensor_tensor(norm[:, 0, :], stats[:, :, 1], stats[:, :, 4], ALU.add))
                ordered(nc.vector.tensor_scalar(norm[:, 0, :], norm[:, 0, :], 0.5, None, ALU.mult))
                ordered(nc.vector.tensor_tensor(norm[:, 1, :], stats[:, :, 1], stats[:, :, 4], ALU.subtract))
                ordered(nc.vector.tensor_tensor(norm[:, 1, :], norm[:, 1, :], norm[:, 1, :], ALU.mult))
                ordered(nc.vector.tensor_scalar(norm[:, 1, :], norm[:, 1, :], 0.25, None, ALU.mult))
                ordered(nc.vector.tensor_tensor(norm[:, 2, :], stats[:, :, 2], stats[:, :, 5], ALU.add))
                nc.vector.scalar_tensor_tensor(norm[:, 2, :], norm[:, 2, :], 1.0 / D, norm[:, 1, :], ALU.mult,
                                               ALU.add).then_inc(var_ready, 1)

            def norm_apply(k):
                dve.wait_ge(sd_ready, k + 1)
                ordered(nc.vector.reciprocal(norm[:, 4, :], norm[:, 3, :]))
                def half_of_tiles(q):
                    for i in range(8):
                        t = 8 * q + i
                        if i % 2 == 0:
                            dve.wait_ge(xn_ready, 8 * k + 4 * q + i // 2 + 1)
                        nc.vector.tensor_scalar(XR[:, t, :] if k == 3 else XCK[k][i][:, :],
                                                X[:, bass.ds(t, 1), :].rearrange("p a d -> p (a d)"),
                                                norm[:, 0, bass.ds(t, 1)],
                                                norm[:, 4, bass.ds(t, 1)], ALU.subtract, ALU.mult
                                                ).then_inc(xc_ready, 1)

                if k == 3:
                    for q in range(2):
                        half_of_tiles(q)
                else:
                    with dve.Fori(0, 2) as q:
                        half_of_tiles(q)

            def tile_stats(t):
                nc.vector.bn_stats(stats[:, t, :], X[:, t, :]).then_inc(stats_done, 1)

            def row_piece(l, it, e, bank, what, c, u=0):
                dve.wait_ge(row_ready, e + 1)
                if what == "M":
                    pair, ch = divmod(c, len(MAXCOLS))
                    nc.vector.reduce_max(MXC[:, pair, ch:ch + 1], ps[:, bank, 0:MAXCOLS[ch][1]],
                                         AX.X).then_inc(row_taken, 1)
                elif what == "D":
                    if u == 0:
                        dve.wait_ge(odd_added, one + l * (NIT // 2 + 1) + it // 2)
                        dst, rows = ODD[:, :], const[:, C_ODD:C_ODD + 1]
                    else:
                        dst = ON[:, bass.ds((it - 1) // 2, 1), :].rearrange("p a b -> p (a b)")
                        rows = const[:, C_EVEN:C_EVEN + 1]
                    nc.vector.scalar_tensor_tensor(dst, U[:, :], rows, ps[:, bank, :], ALU.mult,
                                                   ALU.mult).then_inc(row_taken, 1)
                else:
                    if "T" in what:
                        dve.wait_ge(nm_ready, l * NIT + it + 1)
                        last = nc.vector.tensor_scalar(NMF[:, 0, :], ps[0:NPAIR, bank, 0:128], -1.0, None, ALU.mult)
                    if "R" in what:
                        last = nc.vector.reciprocal(R16[:, :, :].rearrange("p q h -> p (q h)"),
                                                    ps[:, bank, 128:128 + NPAIR])
                    last.then_inc(row_taken, 1)

            def output_written(l, it, d_piece):
                dve.wait_ge(row_taken, three + d_piece + 1)
                nc.vector.memset(scrap[:, 29:30], 0.0).then_inc(on_ready, 1)

            def row_maxima(e_last):
                dve.wait_ge(row_taken, three + e_last + 1)
                nc.vector.tensor_reduce(M16[:, :], MXC[:, :, :], AX.X, ALU.max).then_inc(m16_ready, 1)

            def attention(l):
                first = l * ROWS_LAYER

                def wide_maxima(n):
                    for pair in range(NPAIR):
                        e = (NPAIR + 1) * n + pair
                        dve.wait_ge(row_ready, first + e + 1)
                        nc.vector.tensor_reduce(M16[:, pair:pair + 1], ps[:, wide_banks(e):wide_banks(e) + 4, 0:WIDE],
                                                AX.XY, ALU.max).then_inc(row_taken, 1)
                    dve.wait_ge(row_taken, three + first + (NPAIR + 1) * n + NPAIR)
                    nc.vector.memset(scrap[:, 28:29], 0.0).then_inc(m16_ready, 1)

                wide_maxima(0)
                row_piece(l, -1, first + NPAIR, wide_banks(NPAIR), "T", 0)
                wide_maxima(1)
                nc.vector.memset(ps[:, ACC, :], 1.0).then_inc(acc_set, 1)

                def iteration(it, first, kind, u):
                    pieces = row_pieces(kind)
                    d_at = pieces.index(("D", 0))
                    for k, (what, c) in enumerate(pieces):
                        if k == 0 and kind == "loop":
                            dve.wait_ge(m16_ready, l * NIT + it + 2)
                        row_piece(l, it, first + k, row_bank(k) if kind == "loop" else TAIL_ROWS, what, c, u)
                        if k == min(d_at + 1, len(pieces) - 1):
                            output_written(l, it, first + d_at)
                    if kind == "loop":
                        row_maxima(first + len(pieces) - 1)

                first = first + ROWS_HEAD
                with dve.Fori(0, NIT // 2 - 1) as i:
                    for u in range(2):
                        it = 2 * i + u
                        iteration(it, first + ROWS_LOOP * it, "loop", u)
                first = first + ROWS_LOOP * (NIT - 2)
                iteration(NIT - 2, first, "last but one", 0)
                iteration(NIT - 1, first + 2, "last", 1)
                iteration(NIT, first + 4, "last", 0)

            def split_tokens():
                for pair in range(8):
                    dve.wait_ge(xn_ready, four + 8 + pair + 1)
                    cols = slice(256 * pair, 256 * pair + 256)
                    nc.vector.tensor_tensor(XL[:, :, cols], XN[:, :, cols], XH[:, :, cols].bitcast(f32),
                                            ALU.subtract).then_inc(xl_ready, 1)

            def add_to_residual(ready, before, bank0, taken):
                for t in range(NT):
                    dve.wait_ge(ready, before + t + 1)
                    nc.vector.tensor_tensor(X[:, t, :], ps[:, bank0 + t % 4, 0:D], X[:, t, :], ALU.add).then_inc(taken, 1)
                    if t > 0:
                        dve.wait_ge(taken, before + t)
                        tile_stats(t - 1)
                dve.wait_ge(taken, before + NT)
                tile_stats(NT - 1)

            def wide(a):
                return a[:, :].unsqueeze(2).to_broadcast([128, NT, NR])

            def first_greatest(l, values, greatest, chosen):
                ordered(nc.vector.tensor_reduce(greatest[:, :], values[:, :, :], AX.X, ALU.max))
                ordered(nc.vector.tensor_tensor(TK0[l][:, :, :], values[:, :, :], wide(greatest), ALU.is_equal))
                ordered(nc.vector.tensor_tensor(TK0[l][:, :, :], TK0[l][:, :, :], prio[:, :, :], ALU.mult))
                ordered(nc.vector.tensor_reduce(MK[l][:, :], TK0[l][:, :, :], AX.X, ALU.max))
                ordered(nc.vector.tensor_tensor(chosen[:, :, :], TK0[l][:, :, :], wide(MK[l]), ALU.is_equal))

            def route_start(l):
                dve.wait_ge(rest_loaded, 16 * 9)
                dve.wait_ge(lg_ready, l + 1)
                logits = ps[:, 2, 0:NT * NR].rearrange("p (t e) -> p t e", e=NR)
                if l == 0:
                    nc.vector.tensor_copy(LG[l][:, :, :], logits).then_inc(lg_read, 1)
                else:
                    nc.vector.tensor_tensor(LG[l][:, :, :], logits,
                                            rbias[:, :].unsqueeze(1).to_broadcast([128, NT, NR]),
                                            ALU.add).then_inc(lg_read, 1)
                dve.wait_ge(lg_read, l + 1)
                ordered(nc.vector.tensor_reduce(M1[l][:, :], LG[l][:, :, :], AX.X, ALU.max))
                nc.vector.tensor_tensor(PB[l][:, :, :], LG[l][:, :, :], wide(M1[l]), ALU.subtract).then_inc(lg_moved, 1)

            def to_shares(l):
                ordered(nc.vector.tensor_reduce(M2[l][:, :], PB[l][:, :, :], AX.X, ALU.add))
                ordered(nc.vector.reciprocal(M2[l][:, :], M2[l][:, :]))
                ordered(nc.vector.tensor_tensor(PB[l][:, :, :], PB[l][:, :, :], wide(M2[l]), ALU.mult))

            def route_first(l):
                dve.wait_ge(ex_ready, l + 1)
                if l == 0:
                    to_shares(l)
                first_greatest(l, (PB[0], LG[1])[l], M1[l], ONE1[l])

            def route_second(l):
                ordered(nc.vector.scalar_tensor_tensor(TK1[l][:, :, :], ONE1[l][:, :, :], -3e38,
                                                       (PB[0], LG[1])[l][:, :, :], ALU.mult, ALU.add))
                first_greatest(l, TK1[l], M2[l], ONE2[l])

            def route_weights(l):
                if l == 0:
                    ordered(nc.vector.tensor_tensor(ONE1[l][:, :, :], ONE1[l][:, :, :], ONE2[l][:, :, :], ALU.add))
                    nc.vector.tensor_tensor(PW[:, :, :], ONE1[l][:, :, :], PB[l][:, :, :], ALU.mult).then_inc(pw_ready, 1)
                    dve.wait_ge(pw_ready, 1)
                else:
                    nc.vector.tensor_tensor(POSN[:, :, :], ONE1[l][:, :, :], ONE2[l][:, :, :],
                                            ALU.add).then_inc(chosen_ready, 1)
                    dve.wait_ge(chosen_ready, 1)
                    ordered(nc.vector.tensor_tensor(PB[l][:, :, :], PB[l][:, :, :], POSN[:, :, :], ALU.mult))
                    to_shares(l)
                    for one, share in ((ONE1[l], SHARE[0]), (ONE2[l], SHARE[1])):
                        ordered(nc.vector.tensor_tensor(TK0[l][:, :, :], one[:, :, :], PB[l][:, :, :], ALU.mult))
                        ordered(nc.vector.tensor_reduce(share[:, :], TK0[l][:, :, :], AX.X, ALU.add))

            def route_slots(l):
                dve.wait_ge(prefix_ready, 1)
                tile = lambda at: ps[:, 7, at:at + NT * NR].rearrange("p (t e) -> p t e", e=NR)
                ordered(nc.vector.tensor_copy(SCAN[0][:, :, :], tile(NT * NR)))
                a, b, d = SCAN[0], SCAN[1], 1
                while d < NT:
                    nc.vector.tensor_copy(b[:, 0:d, :], a[:, 0:d, :])
                    ordered(nc.vector.tensor_tensor(b[:, d:NT, :], a[:, d:NT, :], a[:, 0:NT - d, :], ALU.add))
                    a, b, d = b, a, 2 * d
                n, ends, other, scratch = VISITS
                ordered(nc.vector.tensor_scalar(scratch[:, :], a[:, NT - 1, :], (VT - 1) / 2, 1.0 / VT, ALU.add, ALU.mult))
                ordered(nc.vector.tensor_scalar(n[:, :], scratch[:, :], ROUND, None, ALU.add))
                ordered(nc.vector.tensor_scalar(n[:, :], n[:, :], ROUND, None, ALU.subtract))
                ordered(nc.vector.tensor_copy(ends[:, :], n[:, :]))
                d = 1
                while d < NR:
                    nc.vector.tensor_copy(other[:, 0:d], ends[:, 0:d])
                    ordered(nc.vector.tensor_tensor(other[:, d:NR], ends[:, d:NR], ends[:, 0:NR - d], ALU.add))
                    ends, other, d = other, ends, 2 * d
                ordered(nc.vector.tensor_tensor(n[:, :], ends[:, :], n[:, :], ALU.subtract))
                ordered(nc.vector.tensor_scalar(n[:, :], n[:, :], float(VT), None, ALU.mult))
                ordered(nc.vector.tensor_tensor(a[:, :, :], a[:, :, :], tile(NT * NR), ALU.subtract))
                ordered(nc.vector.tensor_tensor(a[:, :, :], a[:, :, :], tile(0), ALU.add))
                ordered(nc.vector.tensor_tensor(a[:, :, :], a[:, :, :], n[:, :].unsqueeze(1).to_broadcast([128, NT, NR]),
                                                ALU.add))
                for one, slot in ((ONE1[l], SLOT[0]), (ONE2[l], SLOT[1])):
                    ordered(nc.vector.tensor_tensor(TK0[l][:, :, :], one[:, :, :], a[:, :, :], ALU.mult))
                    ordered(nc.vector.tensor_reduce(MK[l][:, :], TK0[l][:, :, :], AX.X, ALU.add))
                    ordered(nc.vector.tensor_copy(slot[:, :], MK[l][:, :]))
                dve.wait_ge(tables_loaded, 48)
                ordered(nc.vector.memset(VEXP[:, :], 0.0))
                for e in range(NR - 1):
                    ordered(nc.vector.scalar_tensor_tensor(VEXP[:, :], VNUM[:, :], ends[0:1, e:e + 1], VEXP[:, :],
                                                           ALU.is_ge, ALU.add))
                nc.vector.tensor_copy(EXPERT[:, :], VEXP[:, :]).then_inc(slots_ready, 1)

            def experts():
                def blocks(e, tp, after_hidden={}):
                    for v in range(2):
                        k = NB * e + 2 * tp + v
                        dve.wait_ge(y_ready, 4 * k + y_start - 4)
                        for c in range(HC0):
                            q = k * HC0 + c
                            dve.wait_ge(h_free, two + q + 1)
                            nc.vector.tensor_copy(HH[v][:, c, :], HF[c % 2][:, :]).then_inc(hh_ready, 1)
                            if HC0 * v + c in after_hidden:
                                after_hidden[HC0 * v + c](0)
                    for v in range(2):
                        k = NB * e + 2 * tp + v
                        for qt in range(4):
                            t = 4 * (2 * tp + v) + qt
                            dve.wait_ge(y_ready, y_start + 4 * k + qt + 1)
                            dve.wait_ge(y_free, y_slots + 4 * k + qt)
                            nc.vector.scalar_tensor_tensor(
                                X[:, bass.ds(t, 1), :].rearrange("p a d -> p (a d)"), ps[:, 4 + qt, 0:D],
                                PW[:, bass.ds(t, 1), bass.ds(e, 1)].rearrange("p a b -> p (a b)"),
                                X[:, bass.ds(t, 1), :].rearrange("p a d -> p (a d)"),
                                ALU.mult, ALU.add).then_inc(y_free, 1)

                blocks(0, 0, {0: route_first, 1: route_second, 2: route_weights})
                blocks(0, 1)
                with dve.Fori(0, 2) as tp:
                    blocks(1, tp)
                with dve.Fori(1, E0 // 2) as pair:
                    for u in range(2):
                        with dve.Fori(0, 2) as tp:
                            blocks(2 * pair + u, tp)

            def hidden(u, q, y_done, after_chunk={}):
                for c in range(HC1):
                    dve.wait_ge(gate_ready, q + c + 1)
                    nc.vector.tensor_tensor(VHF[c % 2][:, :], SG[c % 2][:, :], ps[:, c, VT:2 * VT],
                                            ALU.mult).then_inc(vhf_ready, 1)
                    if c == 0:
                        dve.wait_ge(vy_ready, y_done)
                    dve.wait_ge(vhf_ready, vhf_start + q + c + 1)
                    nc.vector.tensor_copy(VHH[u][:, c, :], VHF[c % 2][:, :]).then_inc(vhh_ready, 1)
                    dve.wait_ge(vhh_ready, q + c + 1)
                    nc.vector.tensor_tensor(VHL[u][:, c, :], VHF[c % 2][:, :], VHH[u][:, c, :].bitcast(f32),
                                            ALU.subtract).then_inc(vhl_ready, 1)
                    if c in after_chunk:
                        after_chunk[c](1)

            def shared_block(b, v, y_done, more, after_chunk={}):
                q = HC1 * NSH * b
                hidden(0, q, y_done, after_chunk)
                if more:
                    rest_of_block(b + 1, 1 - v)
                hidden(1, q + HC1, y_done)
                dve.wait_ge(vy_ready, b + 1)
                x = X[:, bass.ds(2 * b, 2), :]
                nc.vector.tensor_tensor(x, ps[:, 4:6, 0:D], x, ALU.add).then_inc(vy_taken, 1)

            def rest_of_block(b, v):
                dve.wait_ge(vxh_ready, b + 1)
                nc.vector.tensor_tensor(VXL[v][:, :, :], XN[:, :, bass.ds(VT * b, VT)], VXH[v][:, :, :].bitcast(f32),
                                        ALU.subtract).then_inc(vxl_ready, 1)

            def rest_of_rows(n, u):
                dve.wait_ge(vxh_ready, SHB + n + 1)
                nc.vector.tensor_tensor(VXL[u][:, :, :], ps[:, 6 + u, :].rearrange("p (c n) -> p c n", c=KC),
                                        VXH[u][:, :, :].bitcast(f32), ALU.subtract).then_inc(vxl_ready, 1)

            def expert_of(n):
                return dve.value_load(EXPERT[0:1, bass.ds(n, 1)], min_val=0, max_val=E1 - 1)

            def cut_last_weights(n, u, e):
                cols = slice(WCOLS // 4 * 3, WCOLS)
                dve.wait_ge(vwh_ready, NSH + HC1 * (n + 1))
                nc.vector.tensor_tensor(VWL[u][:, cols], RES[:, bass.ds(e, 1), cols].rearrange("p a b -> p (a b)"),
                                        VWH[u][:, cols].bitcast(f32), ALU.subtract).then_inc(vwl_last, 1)

            def visits():
                rest_of_block(0, 0)
                shared_block(0, 0, 0, True, {0: route_first, 2: route_second})
                shared_block(1, 1, 1, True, {0: route_weights})
                shared_block(2, 0, 2, True)
                shared_block(3, 1, 3, True, {0: route_slots})
                with dve.Fori(2, SHB // 2 - 1) as i:
                    for v in range(2):
                        b = 2 * i + v
                        shared_block(b, v, b, True)
                shared_block(SHB - 2, 0, SHB - 2, True)
                shared_block(SHB - 1, 1, SHB - 1, False)
                rest_of_rows(0, 0)
                cut_last_weights(0, 0, expert_of(0))
                with dve.Fori(0, NV // 2) as i:
                    for u in range(2):
                        n = 2 * i + u
                        following = expert_of(n + 1)
                        hidden(u, HC1 * (NSH * SHB + n), SHB + n)
                        rest_of_rows(n + 1, 1 - u)
                        cut_last_weights(n + 1, 1 - u, following)
                hidden(0, HC1 * (NSH * SHB + NV - 1), SHB + NV - 1)
                for b in range(NB):
                    dve.wait_ge(gathered[b], 16 * 2 * 4)
                    for i in range(2):
                        for t in range(4 * b, 4 * b + 4):
                            if i == 1:
                                dve.wait_ge(summed, 8 * b + t - 4 * b + 1)
                            nc.vector.scalar_tensor_tensor(X[:, t, :], YG[:, t, i, :], SHARE[i][:, t:t + 1], X[:, t, :],
                                                           ALU.mult, ALU.add).then_inc(summed, 1)

            for col, (s, n) in enumerate((
                    (unit_free, four), (rest1_ready, four), (part3_ready, two),
                    (parts_stored[0][0], store_start), (parts_stored[0][1], store_start),
                    (parts_stored[1][0], store_start), (parts_stored[1][1], store_start),
                    (xn_ready, four), (row_taken, three), (exp_done, two), (pv_done, two),
                    (u_ready, one), (on_ready, one), (odd_added, one),
                    (wl_ready, two), (h_free, two), (hl_ready, two), (y_ready, y_start), (y_free, y_slots),
                    (vhf_ready, vhf_start), (vy_taken, vy_start),
                    (y_stored[0], store_start), (y_stored[1], store_start))):
                nc.vector.memset(scrap[:, col:col + 1], 0.0).then_inc(s, n)
            angles(0)
            angles(1)
            dve.wait_ge(x_loaded, 16)
            for t in range(NT):
                tile_stats(t)
            dve.wait_ge(stats_done, NT)
            norm_variance()
            norm_apply(0)
            dve.wait_ge(table_ready, 2)
            units("k0")
            dve.wait_ge(table_ready, 4)
            units("q0")
            units("k1")
            attention(0)
            dve.wait_ge(bias_added, 1)
            add_to_residual(o_ready, 0, 0, o_taken)
            dve.wait_ge(stats_done, 2 * NT)
            norm_variance()
            norm_apply(1)
            split_tokens()
            route_start(0)
            experts()
            dve.wait_ge(y_free, y_slots + E0 * NT)
            add_to_residual(yb_ready, 0, 4, yb_taken)
            dve.wait_ge(stats_done, 3 * NT)
            norm_variance()
            norm_apply(2)
            units("q1")
            attention(1)
            add_to_residual(o_ready, NT, 0, o_taken)
            dve.wait_ge(stats_done, 4 * NT)
            norm_variance()
            norm_apply(3)
            route_start(1)
            visits()


def _pairs_apart(w):
    return w.reshape(H, DH // 2, 2, D).transpose(3, 2, 1, 0).reshape(D, D)


def _by_group_pairs(wo):
    w = wo.T.reshape(NG // 2, 2, HG, DH, D)
    return np.ascontiguousarray(w.transpose(2, 1, 3, 0, 4).reshape(128, NG // 2, D))


def _laid_out(i):
    t = np.ascontiguousarray
    freq = np.float32(100.0) ** (-np.arange(0, DH, 2, dtype=np.float32) / np.float32(DH))
    const = np.zeros((128, 8), np.float32)
    const[:, C_FREQ] = np.repeat(freq, H)
    const[:, C_HALFPI] = np.pi / 2
    const[:, C_EPS] = EPS
    const[:, C_EVEN] = np.arange(128) % 32 < DH
    const[:, C_ODD] = np.arange(128) % 32 >= DH
    pick = np.zeros((128, 2, HG), np.float32)
    for h in range(HG):
        pick[32 * h + DH, 0, h] = pick[32 * h, 1, h] = 1.0
    pos = np.zeros((1, NPOS), np.int32)
    pos[0, :T] = i["itok_BxS_3_4095"][0]
    pos[0, T:T + S] = i["itok_BxS2_0_4095"][0]
    ctx = np.zeros((D, SP), np.float32)
    ctx[:, :S] = i["ctx_1024"][0].T
    a = {
        "x": i["x"][0], "pos": pos, "ctxT": ctx, "const": const, "ident": np.eye(128, dtype=np.float32),
        "pick": pick, "ones": np.ones((3, H, S), np.dtype("bfloat16")),
        "q0": _pairs_apart(i["L0_xattn_Wq"]), "k0": _pairs_apart(i["L0_xattn_Wk"]),
        "q1": _pairs_apart(i["L1_xattn_w_q"]), "k1": _pairs_apart(i["L1_xattn_w_k"]),
        "wv": np.concatenate([i["L0_xattn_Wv"].T, i["L1_xattn_w_v"].T], 1),
        "wo0": _by_group_pairs(i["L0_xattn_Wo"]), "wo1": _by_group_pairs(i["L1_xattn_w_o"]),
        "bo0": i["L0_xattn_bo"].reshape(1, D),
        "router0": i["L0_ffn_router_w"], "router1": i["L1_ffn_router_w"].T,
        "rbias": i["L1_ffn_expert_bias"].reshape(1, NR),
        "prio": np.tile(np.arange(NR, 0, -1, dtype=np.float32), (128, NT, 1)),
        "w_in": i["L0_ffn_w_in"], "w_out": i["L0_ffn_w_out"], "bout0": i["L0_ffn_b_out"],
        "bin0": i["L0_ffn_b_in"].reshape(E0, HC0, 128).transpose(0, 2, 1),
        "w1": i["L1_ffn_w1"].transpose(0, 2, 1), "sw1": i["L1_ffn_sw1"].transpose(0, 2, 1),
        "w3": i["L1_ffn_w3"].transpose(0, 2, 1), "sw3": i["L1_ffn_sw3"].transpose(0, 2, 1),
        "w2": i["L1_ffn_w2"].transpose(0, 2, 1), "sw2": i["L1_ffn_sw2"].transpose(0, 2, 1),
        "tri": np.triu(np.ones((128, 128), np.float32), 1), "all_ones": np.ones((128, 128), np.float32),
        "visit": np.arange(NV, dtype=np.float32).reshape(1, NV), "zeros": np.zeros((1, D), np.float32),
    }
    return {n: t(v) for n, v in a.items()}


def kernel(**inputs):
    import concourse.bacc as _bacc
    from concourse.bass_utils import run_bass_kernel_spmd as _run

    nc = _bacc.Bacc("TRN2", target_bir_lowering=False, num_devices=1)
    arrays = _laid_out({n: np.asarray(v) for n, v in inputs.items()})
    dram = {n: nc.dram_tensor(f"in_{n}", a.shape, mybir.dt.from_np(a.dtype), kind="ExternalInput").ap()
            for n, a in arrays.items()}
    out = nc.dram_tensor("out", (T, D), mybir.dt.float32, kind="ExternalOutput").ap()
    build(nc, dram, out)
    r = _run(nc, [{f"in_{n}": a for n, a in arrays.items()}], core_ids=[0])
    return r.results[0]["out"].reshape(1, T, D)
```
